# Optimizing a Trainium2 kernel written in Bass

```python
import numpy as np
import jax
import jax.numpy as jnp

def _softmax(x, axis=-1):
    return jax.nn.softmax(x, axis=axis)

def _gelu(x):
    return jax.nn.gelu(x, approximate=True)

def _silu(x):
    return jax.nn.silu(x)

def _sigmoid(x):
    return jax.nn.sigmoid(x)

def _layernorm(x, axis=-1, eps=1e-05):
    m = jnp.mean(x, axis=axis, keepdims=True)
    v = jnp.var(x, axis=axis, keepdims=True)
    return (x - m) / jnp.sqrt(v + eps)

def _scatter_add(tgt, idx, src, axis=0):
    return tgt.at[idx].add(src)

def _segment_sum(src, seg, n):
    return jax.ops.segment_sum(src, seg, n)
kernel_name = 'mk_gnn_resnorm_d2_gnn_r8_6e7853'

def setup_inputs(seed: int=0):
    np.random.seed(seed)
    _w = jnp.asarray

    def _rec_inputs():
        import jax
        import jax.numpy as jnp
        _gk = jax.random.key(seed)
        x = -0.000202 + 1 * jax.random.normal(jax.random.fold_in(_gk, 1), (6250, 128), jnp.float32)
        src = jax.random.randint(jax.random.fold_in(_gk, 2), (200000,), 0, 6250, jnp.int32)
        dst = jnp.minimum((6250 * jax.random.uniform(jax.random.fold_in(_gk, 3), (200000,)) ** 2.0).astype(jnp.int32), 49999)
        _o = jnp.argsort(dst, stable=True)
        src = src[_o]
        dst = dst[_o]
        edge_attr_32 = 0.00012405 + 0.99998 * jax.random.normal(jax.random.fold_in(_gk, 11), (200000, 32), jnp.float32)
        edge_weight = jax.random.uniform(jax.random.fold_in(_gk, 13), (200000,), jnp.float32, 0.0, 0.999999)
        node_vec = jax.random.uniform(jax.random.fold_in(_gk, 14), (6250,), jnp.float32, 0.0, 0.999994)
        return (x, src, dst, edge_attr_32, edge_weight, node_vec)
    x, src, dst, edge_attr_32, edge_weight, node_vec = _rec_inputs()

    def _L0_gnn_setup():
        import jax, jax.numpy as jnp
        import numpy as np
        N, E = (6250, 100000)
        MEM, EDGE, TIME = (128, 32, 32)
        NUM_ITERS, EPSILON, GAMMA = (1, 1.0, 0.1)
        MEAN_DT, STD_DT = (0.0, 1.0)

        def _transformer_conv(h, src, dst, edge_attr, Wq, bq, Wk, bk, Wv, bv, We):
            q = h @ Wq.T + bq
            k = h @ Wk.T + bk
            v = h @ Wv.T + bv
            e = edge_attr @ We.T
            kj = k[src] + e
            alpha = jnp.sum(q[dst] * kj, axis=-1) / jnp.sqrt(jnp.asarray(MEM, h.dtype))
            amax = jax.ops.segment_max(alpha, dst, num_segments=N)
            alpha = jnp.exp(alpha - amax[dst])
            asum = jax.ops.segment_sum(alpha, dst, num_segments=N)
            alpha = alpha / (asum[dst] + 1e-16)
            out_e = (v[src] + e) * alpha[:, None]
            return jax.ops.segment_sum(out_e, dst, num_segments=N)
        key = jax.random.key(seed)
        ks = jax.random.split(key, 20)
        inv = lambda f: 1.0 / np.sqrt(f)
        return {'x': jax.random.normal(ks[0], (N, MEM), jnp.float32), 'last_update': jax.random.uniform(ks[1], (N,), jnp.float32), 'edge_index': jax.random.randint(ks[2], (2, E), 0, N, jnp.int64), 't': jax.random.uniform(ks[3], (E,), jnp.float32), 'msg': jax.random.normal(ks[4], (E, EDGE), jnp.float32), 'time_w': jax.random.normal(ks[5], (TIME,), jnp.float32), 'time_b': jax.random.normal(ks[6], (TIME,), jnp.float32) * 0.1, 'Wx': jax.random.normal(ks[7], (MEM, MEM), jnp.float32) * inv(MEM), 'bx': jnp.zeros((MEM,), jnp.float32), 'Wq': jax.random.normal(ks[8], (MEM, MEM), jnp.float32) * inv(MEM), 'bq': jnp.zeros((MEM,), jnp.float32), 'Wk': jax.random.normal(ks[9], (MEM, MEM), jnp.float32) * inv(MEM), 'bk': jnp.zeros((MEM,), jnp.float32), 'Wv': jax.random.normal(ks[10], (MEM, MEM), jnp.float32) * inv(MEM), 'bv': jnp.zeros((MEM,), jnp.float32), 'We': jax.random.normal(ks[11], (MEM, EDGE + TIME), jnp.float32) * inv(EDGE + TIME), 'W_ac': jax.random.normal(ks[12], (MEM, MEM), jnp.float32) * inv(MEM), 'b_ac': jnp.zeros((MEM,), jnp.float32)}
    _L0_gnn_all = _L0_gnn_setup()
    _L0_gnn_in = {k: v for k, v in _L0_gnn_all.items() if k in ('time_w', 'time_b', 'Wx', 'bx', 'Wq', 'bq', 'Wk', 'bk', 'Wv', 'bv', 'We', 'W_ac', 'b_ac')}
    del _L0_gnn_all

    def _L1_gnn_setup():
        import jax, jax.numpy as jnp
        import numpy as np
        N_NODES = 6250
        N_EDGES = 100000
        D = 128

        def _mlp(h, W1, b1, W2, b2):
            return jax.nn.relu(h @ W1 + b1) @ W2 + b2
        key = jax.random.key(seed)
        ks = jax.random.split(key, 6)
        s = 0.05
        x = jax.random.normal(ks[0], (N_NODES, D), dtype=jnp.float32)
        edge_index = jax.random.randint(ks[1], (2, N_EDGES), 0, N_NODES, dtype=jnp.int64)
        We1 = jax.random.normal(ks[2], (2 * D, D), dtype=jnp.float32) * s
        be1 = jnp.zeros((D,), dtype=jnp.float32)
        We2 = jax.random.normal(ks[3], (D, D), dtype=jnp.float32) * s
        be2 = jnp.zeros((D,), dtype=jnp.float32)
        Wn1 = jax.random.normal(ks[4], (2 * D, D), dtype=jnp.float32) * s
        bn1 = jnp.zeros((D,), dtype=jnp.float32)
        Wn2 = jax.random.normal(ks[5], (D, D), dtype=jnp.float32) * s
        bn2 = jnp.zeros((D,), dtype=jnp.float32)
        return {'x': x, 'edge_index': edge_index, 'We1': We1, 'be1': be1, 'We2': We2, 'be2': be2, 'Wn1': Wn1, 'bn1': bn1, 'Wn2': Wn2, 'bn2': bn2}
    _L1_gnn_all = _L1_gnn_setup()
    _L1_gnn_in = {k: v for k, v in _L1_gnn_all.items() if k in ('We1', 'be1', 'We2', 'be2', 'Wn1', 'bn1', 'Wn2', 'bn2')}
    del _L1_gnn_all
    return {'x': x, 'src': src, 'dst': dst, 'edge_attr_32': edge_attr_32, 'edge_weight': edge_weight, 'node_vec': node_vec, 'L0_gnn_time_w': _L0_gnn_in['time_w'], 'L0_gnn_time_b': _L0_gnn_in['time_b'], 'L0_gnn_Wx': _L0_gnn_in['Wx'], 'L0_gnn_bx': _L0_gnn_in['bx'], 'L0_gnn_Wq': _L0_gnn_in['Wq'], 'L0_gnn_bq': _L0_gnn_in['bq'], 'L0_gnn_Wk': _L0_gnn_in['Wk'], 'L0_gnn_bk': _L0_gnn_in['bk'], 'L0_gnn_Wv': _L0_gnn_in['Wv'], 'L0_gnn_bv': _L0_gnn_in['bv'], 'L0_gnn_We': _L0_gnn_in['We'], 'L0_gnn_W_ac': _L0_gnn_in['W_ac'], 'L0_gnn_b_ac': _L0_gnn_in['b_ac'], 'L1_gnn_We1': _L1_gnn_in['We1'], 'L1_gnn_be1': _L1_gnn_in['be1'], 'L1_gnn_We2': _L1_gnn_in['We2'], 'L1_gnn_be2': _L1_gnn_in['be2'], 'L1_gnn_Wn1': _L1_gnn_in['Wn1'], 'L1_gnn_bn1': _L1_gnn_in['bn1'], 'L1_gnn_Wn2': _L1_gnn_in['Wn2'], 'L1_gnn_bn2': _L1_gnn_in['bn2']}

def reference(x, src, dst, edge_attr_32, edge_weight, node_vec, L0_gnn_time_w, L0_gnn_time_b, L0_gnn_Wx, L0_gnn_bx, L0_gnn_Wq, L0_gnn_bq, L0_gnn_Wk, L0_gnn_bk, L0_gnn_Wv, L0_gnn_bv, L0_gnn_We, L0_gnn_W_ac, L0_gnn_b_ac, L1_gnn_We1, L1_gnn_be1, L1_gnn_We2, L1_gnn_be2, L1_gnn_Wn1, L1_gnn_bn1, L1_gnn_Wn2, L1_gnn_bn2):
    import jax
    import jax.numpy as jnp

    def _L0_gnn_ref(x, last_update, edge_index, t, msg, time_w, time_b, Wx, bx, Wq, bq, Wk, bk, Wv, bv, We, W_ac, b_ac):
        import jax, jax.numpy as jnp
        import numpy as np
        N, E = (6250, 100000)
        MEM, EDGE, TIME = (128, 32, 32)
        NUM_ITERS, EPSILON, GAMMA = (1, 1.0, 0.1)
        MEAN_DT, STD_DT = (0.0, 1.0)

        def _transformer_conv(h, src, dst, edge_attr, Wq, bq, Wk, bk, Wv, bv, We):
            q = h @ Wq.T + bq
            k = h @ Wk.T + bk
            v = h @ Wv.T + bv
            e = edge_attr @ We.T
            kj = k[src] + e
            alpha = jnp.sum(q[dst] * kj, axis=-1) / jnp.sqrt(jnp.asarray(MEM, h.dtype))
            amax = jax.ops.segment_max(alpha, dst, num_segments=N)
            alpha = jnp.exp(alpha - amax[dst])
            asum = jax.ops.segment_sum(alpha, dst, num_segments=N)
            alpha = alpha / (asum[dst] + 1e-16)
            out_e = (v[src] + e) * alpha[:, None]
            return jax.ops.segment_sum(out_e, dst, num_segments=N)
        src, dst = (edge_index[0], edge_index[1])
        rel_t = jnp.abs(last_update[src] - t)
        rel_t = ((rel_t - MEAN_DT) / STD_DT).astype(x.dtype)
        time_feat = jnp.cos(rel_t[:, None] * time_w[None, :] + time_b[None, :])
        edge_attr = jnp.concatenate([msg, time_feat], axis=-1)
        h = x @ Wx.T + bx
        A = W_ac - W_ac.T - GAMMA * jnp.eye(MEM, dtype=x.dtype)
        for _ in range(NUM_ITERS):
            m = _transformer_conv(h, src, dst, edge_attr, Wq, bq, Wk, bk, Wv, bv, We)
            u = jnp.tanh(h @ A.T + m + b_ac)
            h = h + EPSILON * u
        return jnp.tanh(h)

    def _L1_gnn_ref(x, edge_index, We1, be1, We2, be2, Wn1, bn1, Wn2, bn2):
        import jax, jax.numpy as jnp
        import numpy as np
        N_NODES = 6250
        N_EDGES = 100000
        D = 128

        def _mlp(h, W1, b1, W2, b2):
            return jax.nn.relu(h @ W1 + b1) @ W2 + b2
        src = edge_index[0]
        dst = edge_index[1]
        e_in = jnp.concatenate([x[src], x[dst]], axis=-1)
        edge_new = _mlp(e_in, We1, be1, We2, be2)
        agg = jax.ops.segment_sum(edge_new, dst, num_segments=x.shape[0])
        mesh_new = _mlp(jnp.concatenate([x, agg], axis=-1), Wn1, bn1, Wn2, bn2)
        return x + mesh_new
    edge_index = jnp.stack([src, dst])
    x = _layernorm(x + _L0_gnn_ref(x, node_vec, edge_index, edge_weight, edge_attr_32, L0_gnn_time_w, L0_gnn_time_b, L0_gnn_Wx, L0_gnn_bx, L0_gnn_Wq, L0_gnn_bq, L0_gnn_Wk, L0_gnn_bk, L0_gnn_Wv, L0_gnn_bv, L0_gnn_We, L0_gnn_W_ac, L0_gnn_b_ac), axis=-1)
    x = _layernorm(x + _L1_gnn_ref(x, edge_index, L1_gnn_We1, L1_gnn_be1, L1_gnn_We2, L1_gnn_be2, L1_gnn_Wn1, L1_gnn_bn1, L1_gnn_Wn2, L1_gnn_bn2), axis=-1)
    return x

_drawn_inputs = setup_inputs


def setup_inputs(seed=0):
    import zlib

    import numpy as np

    out = dict(_drawn_inputs(seed))
    spreads = {'L0_gnn_bx': (0.0, 0.1),
     'L0_gnn_bq': (0.0, 0.8),
     'L0_gnn_bk': (0.0, 0.8),
     'L0_gnn_bv': (0.0, 0.298),
     'L0_gnn_b_ac': (0.0, 0.283),
     'L1_gnn_be1': (0.0, 0.1),
     'L1_gnn_be2': (0.0, 0.1),
     'L1_gnn_bn1': (0.0, 0.545),
     'L1_gnn_bn2': (0.0, 0.1)}
    factors = {'edge_weight': 4.778, 'node_vec': 4.807, 'L0_gnn_time_w': 2.946, 'L0_gnn_time_b': 8.0}
    for name, (base, spread) in spreads.items():
        noise = np.random.default_rng([zlib.crc32(name.encode()), seed]).standard_normal(out[name].shape)
        drawn = base * np.exp(spread * noise) if base else spread * noise
        out[name] = jnp.asarray(drawn.astype(out[name].dtype))
    for name, factor in factors.items():
        out[name] = (out[name] * factor).astype(out[name].dtype)
    return out
```

```python
from contextlib import ExitStack
from math import pi

import concourse.bass as bass
from concourse import mybir

F32 = mybir.dt.float32
BF16 = mybir.dt.bfloat16
I32 = mybir.dt.int32
ALU = mybir.AluOpType
ACT = mybir.ActivationFunctionType
AX_X = mybir.AxisListType.X

P = 128
D = 128
FE = 32
J = 8
CH = P * J
HALF = CH // 2
W = 128
SLOTS = 4
G = 512
GB = G // P
ROW = 1 + D
A2 = 2 * FE + 1
HEW = ROW + A2
NEVER = -1.0e30
LOW = -1.0e20
ROUND = 1.5 * 2.0**23
EPS = 1.0e-5
GAMMA = 0.1


def gnn_kernel(nc, x, src, dst, edge_attr, edge_weight, node_vec, time_w, time_b, Wx, bx, Wq, bq, Wk, bk,
               Wv, bv, We, W_ac, b_ac, We1, be1, We2, be2, Wn1, bn1, Wn2, bn2, out):
    N = x.shape[0]
    E = src.shape[0]
    NCH = -(-E // CH)
    LAST = E - CH
    DUP = NCH * CH - E
    TURNS = NCH // SLOTS
    NG = -(-(N + W) // G)
    NP = NG * G
    BLOCKS = NP // P
    FULL, REST = N // P, N % P
    ROUNDS = -(-N // W)
    SCALE = float(D) ** -0.5
    assert NCH % SLOTS == 0 and DUP % J == 0 and TURNS > 1 and REST and FULL // GB == NG - 1

    h_table = nc.dram_tensor("h_table", [NP, ROW], F32)
    qk_table = nc.dram_tensor("qk_table", [P, 2, NP], F32)
    hT_dram = nc.dram_tensor("hT_dram", [P, NP], F32)
    p_table = nc.dram_tensor("p_table", [NP, D], F32)
    r_table = nc.dram_tensor("r_table", [NP, 3 * D], BF16)
    start_dram = nc.dram_tensor("start_dram", [2, NCH], F32)

    with ExitStack() as whole:
        def sb(name, shape, dt=F32, ctx=whole):
            return ctx.enter_context(nc.sbuf_tensor(name, shape, dt))

        def sem(name):
            return whole.enter_context(nc.semaphore(name))

        def val(eng, v):
            return v if isinstance(v, int) else eng.snap(v)

        def again(eng, s, v):
            if not isinstance(v, int) or v > 0:
                eng.wait_ge(s, v)

        ident = sb("ident", [P, P])
        ones = sb("ones", [P, P])
        iota_row = sb("iota_row", [P, W])
        iota_col = sb("iota_col", [P, 1])
        start_i = sb("start_i", [1, NCH], I32)
        start_b = sb("start_b", [P, NCH])
        node_of = sb("node_of", [P, NCH])
        span_i = sb("span_i", [1, 1], I32)
        wvT = sb("wvT", [P, D])
        we_bvT = sb("we_bvT", [A2, D])
        one_row = sb("one_row", [A2, P])
        aT = sb("aT", [P, D])
        bac_c = sb("bac_c", [P, 1])
        tw_b = sb("tw_b", [P, FE])
        tb_b = sb("tb_b", [P, FE])
        acc = sb("acc", [P, 2, NP])

        passed = sem("passed")

        layer0 = whole.enter_context(ExitStack())
        tops_so_far = sb("tops_so_far", [1, NP], ctx=layer0)

        with ExitStack() as ctx:
            xg = [sb(f"xg{k}", [P, GB, D], ctx=ctx) for k in range(2)]
            x_tail = sb("x_tail", [P, GB, D], ctx=ctx)
            wx = sb("wx", [P, D], ctx=ctx)
            wq = sb("wq", [P, D], ctx=ctx)
            wk = sb("wk", [P, D], ctx=ctx)
            wv = sb("wv", [P, D], ctx=ctx)
            wac = sb("wac", [P, D], ctx=ctx)
            we_bk = sb("we_bk", [P, A2], ctx=ctx)
            wxT = sb("wxT", [P, D], ctx=ctx)
            wqT = sb("wqT", [P, D], ctx=ctx)
            bx_c = sb("bx_c", [P, 1], ctx=ctx)
            bq_c = sb("bq_c", [P, 1], ctx=ctx)
            bx_b = sb("bx_b", [P, D], ctx=ctx)
            tw_raw = sb("tw_raw", [P, FE], ctx=ctx)
            tb_raw = sb("tb_raw", [P, FE], ctx=ctx)
            nv_rows = sb("nv_rows", [BLOCKS, P], ctx=ctx)
            nv_cols = sb("nv_cols", [P, BLOCKS], ctx=ctx)
            dT = sb("dT", [P, D], ctx=ctx)
            xT = sb("xT", [P, G], ctx=ctx)
            hT = sb("hT", [P, G], ctx=ctx)
            qT = sb("qT", [P, G], ctx=ctx)
            qk = sb("qk", [P, 2, G], ctx=ctx)
            h_rows = sb("h_rows", [P, GB, ROW], ctx=ctx)
            CP = (NCH - 1) // 3
            dst_a = sb("dst_a", [CP, 3, CH], I32, ctx=ctx)
            dst_z = sb("dst_z", [1, CH], I32, ctx=ctx)
            ends_a = sb("ends_a", [CP, 2, 3], ctx=ctx)
            ends_z = sb("ends_z", [1, 2], ctx=ctx)
            ends_r = sb("ends_r", [1, 2, NCH], ctx=ctx)
            span_r = sb("span_r", [1, NCH], ctx=ctx)
            span_m = sb("span_m", [1, 1], ctx=ctx)

            ps = [ctx.enter_context(nc.psum_tensor(f"psA{k}", [P, 512], F32)) for k in range(7)]
            p_xT, p_hT, p_rows, p_qT, p_k1, p_k2, p_w = ps

            loads = sem("loads")
            x_zero = sem("x_zero")
            x_in = [sem(f"x_in{k}") for k in range(2)]
            tail_in = sem("tail_in")
            qk_out = sem("qk_out")
            dst_in = sem("dst_in")
            ends_done = sem("ends_done")
            ends_out = sem("ends_out")
            ends_in = sem("ends_in")
            consts = sem("consts")
            w_turned = sem("w_turned")
            w_copied = sem("w_copied")
            step = sem("step")
            one_done = sem("one_done")
            xT_full = sem("xT_full")
            xT_done = sem("xT_done")
            hT_full = sem("hT_full")
            hT_done = sem("hT_done")
            rows_full = sem("rows_full")
            rows_done = sem("rows_done")
            q_full = sem("q_full")
            q_done = sem("q_done")
            k1_full = sem("k1_full")
            k1_done = sem("k1_done")
            k2_full = sem("k2_full")
            k2_done = sem("k2_done")
            h_out = sem("h_out")
            hT_out = sem("hT_out")

            def col(v):
                return v.rearrange("(p o) -> p o", o=1)

            def row(v):
                return v.rearrange("(o d) -> o d", o=1)

            block = ctx.enter_context(nc.Block())

            LOADS = 16 * 14

            @block.sync
            def _(e):
                for tile, m in ((wx, Wx), (wq, Wq), (wk, Wk), (wv, Wv), (wac, W_ac)):
                    e.dma_start(tile[:, :], m).then_inc(loads, 16)
                e.dma_start(we_bk[:, 0:2 * FE], We).then_inc(loads, 16)
                with nc.allow_non_contiguous_dma(reason="bias columns, 128 numbers each"):
                    e.dma_start(we_bk[:, 2 * FE:A2], col(bk)).then_inc(loads, 16)
                    e.dma_start(bx_c[:, :], col(bx)).then_inc(loads, 16)
                    e.dma_start(bq_c[:, :], col(bq)).then_inc(loads, 16)
                    e.dma_start(bac_c[:, :], col(b_ac)).then_inc(loads, 16)
                e.dma_start(bx_b[:, :], bx.partition_broadcast(P)).then_inc(loads, 16)
                e.dma_start(tw_raw[:, :], time_w.partition_broadcast(P)).then_inc(loads, 16)
                e.dma_start(tb_raw[:, :], time_b.partition_broadcast(P)).then_inc(loads, 16)
                e.dma_start(we_bvT[2 * FE:A2, :], row(bv)).then_inc(loads, 16)
                e.wait_ge(x_zero, 2)
                e.dma_start(x_tail[0:REST, 0, :], x[FULL * P:N, :]).then_inc(tail_in, 16)
                e.dma_start(nv_rows[0:FULL, :], node_vec[0:FULL * P].rearrange("(b p) -> b p", p=P)).then_inc(tail_in, 16)
                e.dma_start(nv_rows[FULL:FULL + 1, 0:REST], row(node_vec[FULL * P:N])).then_inc(tail_in, 16)
                e.dma_start(dst_a[:, :, :], dst[0:3 * CP * CH].rearrange("(p k c) -> p k c", k=3, c=CH)).then_inc(dst_in, 16)
                e.dma_start(dst_z[:, :], row(dst[LAST:E])).then_inc(dst_in, 16)
                e.wait_ge(ends_done, 4)
                for k in range(2):
                    e.dma_start(start_dram[k, 0:NCH - 1].rearrange("(p k) -> p k", k=3), ends_a[:, k, :]).then_inc(ends_out, 16)
                    e.dma_start(start_dram[k:k + 1, NCH - 1:NCH], ends_z[:, k:k + 1]).then_inc(ends_out, 16)
                e.wait_ge(ends_out, 64)
                e.dma_start(ends_r[:, :, :], start_dram[:, :].rearrange("(o k) c -> o k c", o=1)).then_inc(ends_in, 16)
                e.dma_start(start_b[:, :], start_dram[0, :].partition_broadcast(P)).then_inc(ends_in, 16)

                def load(g, k):
                    at = val(e, g * G)
                    again(e, xT_full, val(e, g - 1))
                    e.sem_inc(passed, 1)
                    e.dma_start(xg[k][:, :, :], x[bass.ds(at, G), :].rearrange("(b p) d -> p b d", p=P)).then_inc(x_in[k], 16)

                def store(g):
                    at = val(e, g * G)
                    seen = val(e, g + 1)
                    e.wait_ge(hT_done, seen)
                    e.sem_inc(passed, 1)
                    e.dma_start(hT_dram[:, bass.ds(at, G)], hT[:, :]).then_inc(hT_out, 16)
                    e.wait_ge(rows_done, seen)
                    e.sem_inc(passed, 1)
                    e.dma_start(h_table[bass.ds(at, G), :].rearrange("(b p) d -> p b d", p=P), h_rows[:, :, :]).then_inc(h_out, 16)
                    e.wait_ge(k1_done, seen)
                    e.wait_ge(k2_done, seen)
                    e.sem_inc(passed, 1)
                    e.dma_start(qk_table[:, :, bass.ds(at, G)], qk[:, :, :]).then_inc(qk_out, 16)

                load(0, 0)
                load(1, 1)
                store(0)
                with e.Fori(0, NG // 2 - 1) as m:
                    load(m * 2 + 2, 0)
                    store(m * 2 + 1)
                    load(m * 2 + 3, 1)
                    store(m * 2 + 2)
                store(NG - 2)
                store(NG - 1)
                e.wait_ge(hT_out, 16 * NG)
                e.wait_ge(h_out, 16 * NG)
                e.wait_ge(qk_out, 16 * NG)

            @block.gpsimd
            def _(e):
                e.memset(x_tail[:, :, :], 0.0).then_inc(x_zero, 1)
                e.memset(nv_rows[:, :], 0.0).then_inc(x_zero, 1)
                e.memset(ident[:, :], 0.0).then_inc(step, 1)
                e.memset(ones[:, :], 1.0).then_inc(consts, 1)
                e.wait_ge(step, 1)
                e.affine_select(out=ident[:, :], in_=ident[:, :], compare_op=ALU.not_equal, fill=1.0, base=0,
                                pattern=[[-1, P]], channel_multiplier=1).then_inc(consts, 1)
                e.iota(iota_row[:, :], pattern=[[1, W]], base=0, channel_multiplier=0,
                       allow_small_or_imprecise_dtypes=True).then_inc(consts, 1)
                e.iota(iota_col[:, :], pattern=[[1, 1]], base=0, channel_multiplier=1,
                       allow_small_or_imprecise_dtypes=True).then_inc(consts, 1)
                e.memset(acc[:, :, :], 0.0).then_inc(consts, 1)
                e.memset(tops_so_far[:, :], LOW).then_inc(consts, 1)
                e.memset(qk[:, 1, :], 0.0).then_inc(consts, 1)

            @block.tensor
            def _(e):
                e.wait_ge(consts, 4)
                e.wait_ge(loads, LOADS)
                e.wait_ge(tail_in, 48)
                turned = 0
                for tile in (wx, wq, wv, wac):
                    e.transpose(p_w[:, turned * P:(turned + 1) * P], tile[:, :], ident[:, :])
                    turned += 1
                e.transpose(p_k2[0:2 * FE, 0:P], we_bk[:, 0:2 * FE], ident[:, :])
                e.transpose(p_k2[:, P:P + BLOCKS], nv_rows[:, :], ident[0:BLOCKS, 0:BLOCKS]).then_inc(w_turned, 1)
                e.wait_ge(w_copied, 6)

                def group(g, k, t):
                    before, seen = val(e, g), val(e, g + 1)
                    rows = x_tail if k is None else xg[k]
                    if k is not None:
                        e.wait_ge(x_in[k], val(e, t * 16 + 16))
                    again(e, xT_done, before)
                    for b in range(GB):
                        mm = e.transpose(p_xT[:, b * P:(b + 1) * P], rows[:, b, :], ident[:, :])
                    mm.then_inc(xT_full, 1)
                    e.wait_ge(xT_done, seen)
                    again(e, hT_done, before)
                    e.matmul(p_hT[:, :], wxT[:, :], xT[:, :], start=True, stop=True).then_inc(hT_full, 1)
                    again(e, rows_done, before)
                    for k in range(GB):
                        mm = e.matmul(p_rows[:, k * D:(k + 1) * D], xT[:, k * P:(k + 1) * P], wxT[:, :], start=True, stop=True)
                    mm.then_inc(rows_full, 1)
                    e.wait_ge(hT_done, seen)
                    again(e, q_done, before)
                    e.matmul(p_qT[:, :], wqT[:, :], hT[:, :], start=True, stop=True).then_inc(q_full, 1)
                    e.wait_ge(q_done, seen)
                    again(e, k1_done, before)
                    e.matmul(p_k1[:, :], wk[:, :], qT[:, :], start=True, stop=True).then_inc(k1_full, 1)
                    again(e, k2_done, before)
                    e.matmul(p_k2[0:A2, :], we_bk[:, :], qT[:, :], start=True, stop=True).then_inc(k2_full, 1)

                group(0, 0, 0)
                with e.Fori(0, NG // 2 - 1) as m:
                    group(m * 2 + 1, 1, m)
                    group(m * 2 + 2, 0, m + 1)
                group(NG - 2, 1, NG // 2 - 1)
                group(NG - 1, None, 0)

            @block.scalar
            def _(e):
                e.wait_ge(loads, LOADS)
                e.wait_ge(consts, 7)

                def group(g):
                    before, seen = val(e, g), val(e, g + 1)
                    again(e, rows_full, before)
                    e.wait_ge(xT_full, seen)
                    e.sem_inc(passed, 1)
                    e.activation(xT[:, :], p_xT[:, :], ACT.Copy).then_inc(xT_done, 1)
                    again(e, q_full, before)
                    again(e, hT_out, g * 16)
                    e.wait_ge(hT_full, seen)
                    e.sem_inc(passed, 1)
                    e.activation(hT[:, :], p_hT[:, :], ACT.Identity, bias=bx_c[:, 0:1]).then_inc(hT_done, 1)
                    again(e, k2_full, before)
                    e.wait_ge(q_full, seen)
                    e.sem_inc(passed, 1)
                    e.activation(qT[:, :], p_qT[:, :], ACT.Identity, bias=bq_c[:, 0:1]).then_inc(q_done, 1)
                    e.wait_ge(k2_full, seen)
                    again(e, qk_out, g * 16)
                    e.sem_inc(passed, 1)
                    e.activation(qk[0:A2, 1, :], p_k2[0:A2, :], ACT.Copy, scale=SCALE).then_inc(k2_done, 1)

                group(0)
                with e.Fori(1, NG) as g:
                    group(g)

            @block.vector
            def _(e):
                e.memset(one_row[:, :], 0.0).then_inc(one_done, 1)
                e.wait_ge(one_done, 1)
                e.memset(one_row[2 * FE:A2, :], 1.0).then_inc(one_done, 1)
                e.wait_ge(w_turned, 1)
                e.tensor_copy(wxT[:, :], p_w[:, 0:P]).then_inc(w_copied, 1)
                e.tensor_copy(wqT[:, :], p_w[:, P:2 * P]).then_inc(w_copied, 1)
                e.tensor_copy(wvT[:, :], p_w[:, 2 * P:3 * P]).then_inc(w_copied, 1)
                e.tensor_copy(we_bvT[0:2 * FE, :], p_k2[0:2 * FE, 0:P]).then_inc(w_copied, 1)
                e.tensor_copy(nv_cols[:, :], p_k2[:, P:P + BLOCKS]).then_inc(w_copied, 1)
                e.tensor_tensor(dT[:, :], p_w[:, 3 * P:4 * P], wac[:, :], ALU.subtract).then_inc(w_copied, 1)
                e.wait_ge(w_copied, 6)
                e.scalar_tensor_tensor(out=aT[:, :], in0=ident[:, :], scalar=-GAMMA, in1=dT[:, :], op0=ALU.mult,
                                       op1=ALU.add).then_inc(w_copied, 1)
                e.wait_ge(loads, LOADS)
                e.tensor_scalar(tw_b[:, :], tw_raw[:, :], 1.0 / (2.0 * pi), None, ALU.mult)
                e.tensor_scalar(tb_b[:, :], tb_raw[:, :], 1.0 / (2.0 * pi), 0.25, ALU.mult, ALU.add)
                e.wait_ge(dst_in, 32)
                for k, op in enumerate((ALU.min, ALU.max)):
                    e.tensor_reduce(ends_a[:, k, :], dst_a[:, :, :], AX_X, op).then_inc(ends_done, 1)
                    e.tensor_reduce(ends_z[:, k:k + 1], dst_z[:, :], AX_X, op).then_inc(ends_done, 1)
                e.wait_ge(ends_in, 32)
                e.wait_ge(consts, 7)
                e.tensor_copy(start_i[:, :], ends_r[:, 0, :])
                e.tensor_scalar(node_of[:, :], start_b[:, :], iota_col[:, 0:1], None, ALU.add)
                e.tensor_tensor(span_r[:, :], ends_r[:, 1, :], ends_r[:, 0, :], ALU.subtract).then_inc(ends_done, 1)
                e.wait_ge(ends_done, 5)
                e.tensor_reduce(span_m[:, :], span_r[:, :], AX_X, ALU.max).then_inc(ends_done, 1)
                e.wait_ge(ends_done, 6)
                e.tensor_copy(span_i[:, :], span_m[:, :]).then_inc(ends_done, 1)

                def group(g):
                    blk = g * GB if isinstance(g, int) else e.snap(g * GB, min_val=0, max_val=BLOCKS - GB)
                    seen = val(e, g + 1)
                    again(e, h_out, g * 16)
                    e.tensor_copy(h_rows[:, :, 0:1], nv_cols[:, bass.ds(blk, GB)].rearrange("p (b o) -> p b o", o=1))
                    e.wait_ge(rows_full, seen)
                    e.tensor_tensor(h_rows[:, :, 1:ROW], p_rows[:, :].rearrange("p (b d) -> p b d", d=D),
                                    bx_b[:, :].unsqueeze(1).broadcast_to([P, GB, D]), ALU.add).then_inc(rows_done, 1)
                    e.wait_ge(k1_full, seen)
                    again(e, qk_out, g * 16)
                    e.tensor_scalar(qk[:, 0, :], p_k1[:, :], SCALE, None, ALU.mult).then_inc(k1_done, 1)

                group(0)
                with e.Fori(1, NG) as g:
                    group(g)


        moved = sem("moved")

        def move_windows():
            with ExitStack() as ctx:
                block = ctx.enter_context(nc.Block())

                @block.vector
                def _(e):
                    e.tensor_scalar(start_b[:, :], start_b[:, :], float(W), float(N), ALU.add, ALU.min).then_inc(moved, 1)
                    e.wait_ge(moved, 1)
                    e.tensor_scalar(node_of[:, :], start_b[:, :], iota_col[:, 0:1], None, ALU.add)
                    e.tensor_copy(start_i[:, :], start_b[0:1, :]).then_inc(moved, 1)
                    e.wait_ge(moved, 2)
                    e.sem_clear(moved)

        def pick(e, row, index):
            return e.value_load(row[0:1, bass.ds(index, 1)], min_val=0, max_val=N)

        with ExitStack() as ctx:
            he = [sb(f"he{k}", [P, J, HEW], ctx=ctx) for k in range(SLOTS)]
            src_i = [sb(f"src_i{k}", [P, J], I32, ctx=ctx) for k in range(SLOTS)]
            when = [sb(f"when{k}", [P, J], ctx=ctx) for k in range(SLOTS)]
            feat = [sb(f"feat{k}", [P, J, FE], ctx=ctx) for k in range(SLOTS)]
            dst_b = [sb(f"dst_b{k}", [P, CH], I32, ctx=ctx) for k in range(2)]
            gap = sb("gap", [P, J], ctx=ctx)
            dist = sb("dist", [P, J], ctx=ctx)
            turns_w = sb("turns_w", [P, J, FE], ctx=ctx)
            turns = sb("turns", [P, J, FE], ctx=ctx)
            turns_r = sb("turns_r", [P, J, FE], ctx=ctx)
            phase = [sb(f"phase{k}", [P, J, FE], ctx=ctx) for k in range(2)]
            qk_win = [sb(f"qk_win{k}", [P, 2, W], ctx=ctx) for k in range(2)]
            top_win = sb("top_win", [1, W], ctx=ctx)
            mask = sb("mask", [P, CH], BF16, ctx=ctx)
            heT1 = sb("heT1", [P, CH], ctx=ctx)
            heT2 = sb("heT2", [A2, CH], ctx=ctx)
            prob = sb("prob", [P, CH], ctx=ctx)
            probT = sb("probT", [P, J, W], ctx=ctx)
            top2 = sb("top2", [P, 2], ctx=ctx)
            top = sb("top", [P, 1], ctx=ctx)
            neg_top = sb("neg_top", [P, 1], ctx=ctx)
            fade = sb("fade", [P, 1], ctx=ctx)
            fade_d = sb("fade_d", [P, W], ctx=ctx)

            p_turn = [ctx.enter_context(nc.psum_tensor(f"p_turn{k}", [P, 512], F32)) for k in range(3)]
            p_score = [ctx.enter_context(nc.psum_tensor(f"p_score{k}", [P, HALF], F32)) for k in range(2)]
            p_sum = ctx.enter_context(nc.psum_tensor("p_sum", [P, 2, W], F32))
            p_small = ctx.enter_context(nc.psum_tensor("p_small", [P, 512], F32))
            p_small2 = ctx.enter_context(nc.psum_tensor("p_small2", [P, 512], F32))
            p_fade, p_old, p_row = p_small[:, 0:W], p_small2[:, 0:1], p_small2[0:1, W:2 * W]

            src_in = [sem(f"src_in{k}") for k in range(SLOTS)]
            feat_in = [sem(f"feat_in{k}") for k in range(SLOTS)]
            win_in = [sem(f"win0_in{k}") for k in range(2)]
            top_win_done = sem("top_win_done")
            rows_in = [sem(f"rows_in{k}") for k in range(SLOTS)]
            gap_done = sem("gap_done")
            dist_done = sem("dist_done")
            turns_w_done = sem("turns_w_done")
            turns_done = sem("turns_done")
            turns_r_done = sem("turns_r_done")
            phase_done = sem("phase_done")
            he_done = sem("he_done")
            mask_done = sem("mask_done")
            turn_full = [sem(f"turn_full{q}") for q in range(6)]
            turn_done = [sem(f"turn_done{q}") for q in range(6)]
            score_full = [sem(f"score_full{h}") for h in range(2)]
            masked = [sem(f"masked{h}") for h in range(2)]
            old_full = sem("old_full")
            top_done = sem("top_done")
            neg_done = sem("neg_done")
            fade_done = sem("fade_done")
            prob_done = sem("prob_done")
            row_full = sem("row_full")
            row_done = sem("row_done")
            fade_d_done = sem("fade_d_done")
            fade_full = sem("fade_full")
            faded = sem("faded")
            sum_full = sem("sum_full")
            added = sem("added")
            cut_done = sem("cut_done")
            ready = sem("ready")

            with ExitStack() as c2:
                block = c2.enter_context(nc.Block())

                @block.gpsimd
                def _(e):
                    for k in range(SLOTS):
                        e.memset(he[k][:, :, HEW - 1:HEW], 1.0).then_inc(ready, 1)

                @block.vector
                def _(e):
                    e.memset(p_sum[:, :, :], 0.0).then_inc(ready, 1)

            def layer0_round(r):
                base = r * TURNS
                with ExitStack() as c2:
                    block = c2.enter_context(nc.Block())

                    def shift(c, k):
                        return c[0] + (c[1] + k) // SLOTS, (c[1] + k) % SLOTS

                    def number(c):
                        return c[0] * SLOTS + c[1]

                    def count(c):
                        return (c[0] + base) * SLOTS + c[1]

                    @block.sync
                    def _(e):
                        def load(c):
                            i, u = c
                            v = u % 2
                            last = isinstance(i, int) and number(c) == NCH - 1
                            at = LAST if last else val(e, number(c) * CH)
                            start = pick(e, start_i, number(c))
                            n = count(c)
                            free, free2 = val(e, n - SLOTS + 1), val(e, n - 1)
                            again(e, sum_full, free)
                            e.sem_inc(passed, 1)
                            e.dma_start(src_i[u][:, :], src[bass.ds(at, CH)].rearrange("(p j) -> p j", j=J)).then_inc(src_in[u], 16)
                            e.dma_start(when[u][:, :], edge_weight[bass.ds(at, CH)].rearrange("(p j) -> p j", j=J)).then_inc(feat_in[u], 16)
                            e.dma_start(feat[u][:, :, :], edge_attr[bass.ds(at, CH), :].rearrange("(p j) f -> p j f", j=J)).then_inc(feat_in[u], 16)
                            again(e, mask_done, free2)
                            again(e, score_full[1], free2)
                            e.sem_inc(passed, 1)
                            e.dma_start(dst_b[v][:, :], dst[bass.ds(at, CH)].partition_broadcast(P)).then_inc(win_in[v], 16)
                            e.dma_start(qk_win[v][:, :, :], qk_table[:, :, bass.ds(start, W)]).then_inc(win_in[v], 16)

                        for u in range(SLOTS):
                            load((0, u))
                        with e.Fori(1, TURNS - 1) as i:
                            for u in range(SLOTS):
                                load((i, u))
                        for u in range(SLOTS):
                            load((TURNS - 1, u))

                    @block.gpsimd
                    def _(e):
                        def gather(c):
                            u = c[1]
                            e.wait_ge(src_in[u], val(e, (c[0] + base) * 16 + 16))
                            e.sem_inc(passed, 1)
                            for j in range(J):
                                e.indirect_dma_start(
                                    out=he[u][:, j, 0:ROW], out_offset=None, in_=h_table[:, :],
                                    in_offset=bass.IndirectOffsetOnAxis(ap=src_i[u][:, j:j + 1], axis=0)).then_inc(rows_in[u], 16)

                        with e.Fori(0, TURNS) as i:
                            for u in range(SLOTS):
                                gather((i, u))

                    @block.tensor
                    def _(e):
                        def turn(q, c):
                            u = c[1]
                            for k in range(4):
                                j = 4 * (q % 2) + k
                                if q < 2:
                                    mm = e.transpose(p_turn[q % 3][:, k * P:(k + 1) * P], he[u][:, j, 1:ROW], ident[:, :])
                                else:
                                    mm = e.transpose(p_turn[q % 3][0:A2, k * P:(k + 1) * P], he[u][:, j, ROW:HEW], ident[:, :])
                            mm.then_inc(turn_full[q], 1)

                        def front_turns(c):
                            n = count(c)
                            n0, n1, nm = val(e, n), val(e, n + 1), val(e, n - 1)
                            e.wait_ge(he_done, n1)
                            again(e, turn_done[3], n0)
                            turn(0, c)
                            again(e, turn_done[4], nm)
                            turn(1, c)
                            again(e, turn_done[5], nm)
                            turn(2, c)
                            e.wait_ge(turn_done[0], n1)
                            turn(3, c)

                        def back_turns(c):
                            n1 = val(e, count(c) + 1)
                            e.wait_ge(prob_done, n1)
                            for q in (4, 5):
                                if not (isinstance(c[0], int) and number(c) == NCH - 1):
                                    e.wait_ge(turn_done[q - 3], val(e, count(c) + 2))
                                else:
                                    e.wait_ge(turn_done[q], val(e, count(c)))
                                for k in range(4):
                                    j = 4 * (q - 4) + k
                                    mm = e.transpose(p_turn[q % 3][:, k * P:(k + 1) * P], prob[:, j * P:(j + 1) * P], ident[:, :])
                                mm.then_inc(turn_full[q], 1)

                        def scores(c):
                            v = c[1] % 2
                            n = count(c)
                            n0, n1 = val(e, n), val(e, n + 1)
                            e.wait_ge(win_in[v], val(e, ((c[0] + base) * 2 + c[1] // 2 + 1) * 32))
                            for h in range(2):
                                e.wait_ge(turn_done[h], n1)
                                e.wait_ge(turn_done[2 + h], n1)
                                again(e, masked[h], n0)
                                e.matmul(p_score[h][:, :], qk_win[v][:, 0, :], heT1[:, h * HALF:(h + 1) * HALF], start=True, stop=False)
                                e.matmul(p_score[h][:, :], qk_win[v][0:A2, 1, :], heT2[:, h * HALF:(h + 1) * HALF], start=False,
                                         stop=True).then_inc(score_full[h], 1)

                        def old_top(c):
                            n = count(c)
                            again(e, fade_done, val(e, n))
                            e.wait_ge(top_win_done, val(e, n + 1))
                            e.matmul(p_old, top_win[:, :], ones[0:1, 0:1], start=True,
                                     stop=True).then_inc(old_full, 1)

                        def new_row(c):
                            n = count(c)
                            n0, n1 = val(e, n), val(e, n + 1)
                            e.wait_ge(top_done, n1)
                            e.wait_ge(fade_done, n1)
                            again(e, row_done, n0)
                            e.matmul(p_row, top[:, 0:1], ident[:, :], start=True, stop=True).then_inc(row_full, 1)

                        def fades(c):
                            n = count(c)
                            n0, n1 = val(e, n), val(e, n + 1)
                            e.wait_ge(fade_d_done, n1)
                            again(e, faded, n0)
                            e.matmul(p_fade, ones[:, :], fade_d[:, :], start=True, stop=True).then_inc(fade_full, 1)

                        def sums(c):
                            u = c[1]
                            n = count(c)
                            n0, n1 = val(e, n), val(e, n + 1)
                            e.wait_ge(turn_done[4], n1)
                            e.wait_ge(turn_done[5], n1)
                            again(e, added, n0)
                            for k, (a, b) in enumerate(((1, ROW), (ROW, HEW))):
                                for j in range(J):
                                    mm = e.matmul(p_sum[0:b - a, k, :], he[u][:, j, a:b], probT[:, j, :], start=(j == 0), stop=(j == J - 1))
                            mm.then_inc(sum_full, 1)

                        def front(c):
                            front_turns(c)
                            scores(c)
                            old_top(c)
                            new_row(c)

                        def step(c, nxt=True):
                            if nxt:
                                front_turns(shift(c, 1))
                            back_turns(c)
                            if nxt:
                                scores(shift(c, 1))
                            fades(c)
                            if nxt:
                                old_top(shift(c, 1))
                            sums(c)
                            if nxt:
                                new_row(shift(c, 1))

                        e.wait_ge(ready, SLOTS + 1)
                        front((0, 0))
                        for u in range(SLOTS):
                            step((0, u))
                        with e.Fori(1, TURNS - 1) as i:
                            for u in range(SLOTS):
                                step((i, u))
                        for u in range(SLOTS):
                            step((TURNS - 1, u), u < SLOTS - 1)

                    @block.scalar
                    def _(e):
                        def times(c):
                            u = c[1]
                            n1 = val(e, count(c) + 1)
                            e.wait_ge(phase_done, n1)
                            e.sem_inc(passed, 1)
                            e.activation(he[u][:, :, ROW:ROW + FE], feat[u][:, :, :], ACT.Copy)
                            e.activation(he[u][:, :, ROW + FE:ROW + 2 * FE], phase[u % 2][:, :, :], ACT.Sin, scale=-2.0 * pi).then_inc(he_done, 1)

                        def copy_turns(c):
                            n1 = val(e, count(c) + 1)
                            for q in range(2):
                                e.wait_ge(turn_full[q], n1)
                                e.sem_inc(passed, 1)
                                e.activation(heT1[:, q * HALF:(q + 1) * HALF], p_turn[q % 3][:, :], ACT.Copy).then_inc(turn_done[q], 1)

                        def copy_prob(c):
                            e.wait_ge(turn_full[4], val(e, count(c) + 1))
                            e.sem_inc(passed, 1)
                            e.activation(probT[:, 0:4, :], p_turn[1][:, :].rearrange("p (j n) -> p j n", n=W), ACT.Copy).then_inc(turn_done[4], 1)

                        def window_top(c):
                            n = count(c)
                            start = pick(e, start_i, number(c))
                            again(e, row_done, val(e, n))
                            again(e, old_full, val(e, n))
                            e.sem_inc(passed, 1)
                            e.activation(top_win[:, :], tops_so_far[:, bass.ds(start, W)], ACT.Copy).then_inc(top_win_done, 1)

                        def exps(c):
                            n1 = val(e, count(c) + 1)
                            start = pick(e, start_i, number(c))
                            e.wait_ge(neg_done, n1)
                            e.sem_inc(passed, 1)
                            e.activation(fade[:, :], p_old, ACT.Exp, bias=neg_top[:, 0:1]).then_inc(fade_done, 1)
                            e.activation(prob[:, :], prob[:, :], ACT.Exp, bias=neg_top[:, 0:1]).then_inc(prob_done, 1)
                            e.wait_ge(row_full, n1)
                            e.sem_inc(passed, 1)
                            e.activation(tops_so_far[:, bass.ds(start, W)], p_row, ACT.Copy).then_inc(row_done, 1)

                        def step(c, nxt=True, after=True):
                            if nxt:
                                window_top(shift(c, 1))
                                copy_turns(shift(c, 1))
                            copy_prob(c)
                            if nxt:
                                exps(shift(c, 1))
                            if after:
                                times(shift(c, 2))

                        e.wait_ge(ready, SLOTS + 1)
                        times((0, 0))
                        window_top((0, 0))
                        copy_turns((0, 0))
                        exps((0, 0))
                        times((0, 1))
                        for u in range(SLOTS):
                            step((0, u))
                        with e.Fori(1, TURNS - 1) as i:
                            for u in range(SLOTS):
                                step((i, u))
                        for u in range(SLOTS):
                            step((TURNS - 1, u), u < SLOTS - 1, u < SLOTS - 2)

                    @block.vector
                    def _(e):
                        def phases(c):
                            i, u = c
                            n = count(c)
                            n1 = val(e, n + 1)
                            e.wait_ge(feat_in[u], val(e, (i + base) * 32 + 32))
                            e.wait_ge(rows_in[u], val(e, (i + base) * (16 * J) + 16 * J))
                            e.tensor_tensor(gap[:, :], he[u][:, :, 0:1].rearrange("p j o -> p (j o)"), when[u][:, :], ALU.subtract).then_inc(gap_done, 1)
                            e.wait_ge(gap_done, n1)
                            e.scalar_tensor_tensor(out=dist[:, :], in0=gap[:, :], scalar=-1.0, in1=gap[:, :], op0=ALU.mult,
                                                   op1=ALU.max).then_inc(dist_done, 1)
                            e.wait_ge(dist_done, n1)
                            e.tensor_tensor(turns_w[:, :, :], dist[:, :].unsqueeze(2).broadcast_to([P, J, FE]),
                                            tw_b[:, :].unsqueeze(1).broadcast_to([P, J, FE]), ALU.mult).then_inc(turns_w_done, 1)
                            e.wait_ge(turns_w_done, n1)
                            e.tensor_tensor(turns[:, :, :], turns_w[:, :, :], tb_b[:, :].unsqueeze(1).broadcast_to([P, J, FE]),
                                            ALU.add).then_inc(turns_done, 1)
                            e.wait_ge(turns_done, n1)
                            e.tensor_scalar(turns_r[:, :, :], turns[:, :, :], ROUND, None, ALU.add).then_inc(turns_r_done, 1)
                            again(e, he_done, val(e, n - 1))
                            e.wait_ge(turns_r_done, n1)
                            e.scalar_tensor_tensor(out=phase[u % 2][:, :, :], in0=turns_r[:, :, :], scalar=-ROUND, in1=turns[:, :, :],
                                                   op0=ALU.add, op1=ALU.subtract).then_inc(phase_done, 1)

                        def masks(c):
                            i, u = c
                            v = u % 2
                            e.wait_ge(win_in[v], val(e, ((i + base) * 2 + u // 2 + 1) * 32))
                            if isinstance(i, int) and number(c) == NCH - 1:
                                e.memset(dst_b[v][:, 0:DUP], -1).then_inc(cut_done, 1)
                                e.wait_ge(cut_done, val(e, r + 1))
                            idx = number(c)
                            e.tensor_scalar(mask[:, :], dst_b[v][:, :], node_of[:, bass.ds(idx, 1)], NEVER, ALU.not_equal,
                                            ALU.mult).then_inc(mask_done, 1)

                        def copy_turns(c):
                            n1 = val(e, count(c) + 1)
                            for q in (2, 3):
                                e.wait_ge(turn_full[q], n1)
                                e.tensor_copy(heT2[:, (q - 2) * HALF:(q - 1) * HALF], p_turn[q % 3][0:A2, :]).then_inc(turn_done[q], 1)

                        def tops(c):
                            n1 = val(e, count(c) + 1)
                            by_j = mask[:, :].rearrange("p (q j) -> p j q", j=J)
                            for h in range(2):
                                e.wait_ge(score_full[h], n1)
                                e.wait_ge(mask_done, n1)
                                e.sem_inc(passed, 1)
                                e.tensor_tensor_reduce(prob[:, h * HALF:(h + 1) * HALF].rearrange("p (j q) -> p j q", q=P),
                                                       p_score[h][:, :].rearrange("p (j q) -> p j q", q=P),
                                                       by_j[:, 4 * h:4 * h + 4, :], 1.0, NEVER, ALU.add, ALU.max,
                                                       top2[:, h:h + 1]).then_inc(masked[h], 1)
                            e.wait_ge(old_full, n1)
                            e.wait_ge(masked[0], n1)
                            e.wait_ge(masked[1], n1)
                            e.tensor_scalar(top[:, :], top2[:, 0:1], top2[:, 1:2], p_old, ALU.max, ALU.max).then_inc(top_done, 1)
                            e.wait_ge(top_done, n1)
                            e.tensor_scalar(neg_top[:, :], top[:, :], -1.0, None, ALU.mult).then_inc(neg_done, 1)

                        def spread(c):
                            e.wait_ge(fade_done, val(e, count(c) + 1))
                            e.tensor_scalar(fade_d[:, :], ident[:, :], fade[:, 0:1], None, ALU.mult).then_inc(fade_d_done, 1)

                        def copy_prob(c):
                            e.wait_ge(turn_full[5], val(e, count(c) + 1))
                            e.tensor_copy(probT[:, 4:8, :], p_turn[2][:, :].rearrange("p (j n) -> p j n", n=W)).then_inc(turn_done[5], 1)

                        def add(c):
                            n = count(c)
                            n0, n1 = val(e, n), val(e, n + 1)
                            start = pick(e, start_i, number(c))
                            here = acc[:, :, bass.ds(start, W)]
                            again(e, added, n0)
                            e.wait_ge(fade_full, n1)
                            e.tensor_tensor(here, here, p_fade.unsqueeze(1).broadcast_to([P, 2, W]), ALU.mult).then_inc(faded, 1)
                            e.wait_ge(faded, n1)
                            e.wait_ge(sum_full, n1)
                            e.tensor_tensor(here, here, p_sum[:, :, :], ALU.add).then_inc(added, 1)

                        def step(c, nxt=True, after=True):
                            if nxt:
                                masks(shift(c, 1))
                                copy_turns(shift(c, 1))
                            spread(c)
                            copy_prob(c)
                            if nxt:
                                tops(shift(c, 1))
                            if after:
                                phases(shift(c, 2))
                            add(c)

                        e.wait_ge(ready, SLOTS + 1)
                        phases((0, 0))
                        masks((0, 0))
                        copy_turns((0, 0))
                        tops((0, 0))
                        phases((0, 1))
                        for u in range(SLOTS):
                            step((0, u))
                        with e.Fori(1, TURNS - 1) as i:
                            for u in range(SLOTS):
                                step((i, u))
                        for u in range(SLOTS):
                            step((TURNS - 1, u), u < SLOTS - 1, u < SLOTS - 2)

            layer0_round(0)
            spread_out = nc.values_load(span_i[0:1, 0:1], min_val=0, max_val=N)
            with nc.If(spread_out >= W):
                with nc.Fori(1, ROUNDS) as w:
                    move_windows()
                    layer0_round(w)

        layer0.close()
        x1_rows = sb("x1_rows", [P, BLOCKS, D])
        x1T = sb("x1T", [P, NP])
        bn2_b = sb("bn2_b", [P, D])
        be2_r = sb("be2_r", [1, D])
        bn1_c = sb("bn1_c", [P, 1])
        we2 = sb("we2", [P, D])
        wn1 = sb("wn1", [P, 2, D])
        wn2 = sb("wn2", [P, D])
        eps_c = sb("eps_c", [P, 1])

        with ExitStack() as ctx:
            X = sb("X2", [P, BLOCKS, D], ctx=ctx)
            hT = [sb(f"hT_{k}", [P, G], ctx=ctx) for k in range(2)]
            we1 = sb("we1", [P, 2, D], ctx=ctx)
            be1_b = sb("be1_b", [P, D], ctx=ctx)
            nought = sb("nought", [P, G], ctx=ctx)
            den = sb("den", [P, G], ctx=ctx)
            rden = sb("rden", [P, G], ctx=ctx)
            mean_v = sb("mean_v", [P, G], ctx=ctx)
            pre = sb("pre", [P, G], ctx=ctx)
            upd = sb("upd", [P, G], ctx=ctx)
            h2 = sb("h2", [P, G], ctx=ctx)
            outT = sb("outT", [P, G], ctx=ctx)
            xn = sb("xn", [P, GB, D], ctx=ctx)
            x1T_g = sb("x1T_g", [P, G], ctx=ctx)
            y = sb("y", [P, GB, D], ctx=ctx)
            stats = sb("stats", [P, GB, 6], ctx=ctx)
            mv = sb("mv", [P, GB, 2], ctx=ctx)
            std = sb("std", [P, GB], ctx=ctx)
            rstd = sb("rstd", [P, GB], ctx=ctx)
            p_rows = sb("p_rows", [P, GB, D], ctx=ctx)
            r_f = sb("r_f", [P, GB, D], ctx=ctx)
            r_g = sb("r_g", [P, GB, D], ctx=ctx)
            r_rows = sb("r_rows", [P, GB, 3, D], BF16, ctx=ctx)

            ps = [ctx.enter_context(nc.psum_tensor(f"psC{k}", [P, 512], F32)) for k in range(8)]
            p_den, p_val, p_anti, p_out, p_x1, p_pr0, p_pr1, _ = ps

            names = ("den_full val_full anti_full den_done rden_done mean_done pre_done upd_done h2_done outT_done out_full "
                     "y_done stats_done mv_done std_done rstd_done x1_done x1_full x1T_done pr_full p_done r_done hi_done "
                     "g_done mid_done lo_done kept").split()
            s = {n: sem(n) for n in names}
            loads = sem("loads_c")
            x_zero = sem("x_zero_c")
            x_in = sem("x_in_c")
            hT_in = [sem(f"hT_in{k}") for k in range(2)]
            p_out_d = sem("p_out_d")
            r_out_d = sem("r_out_d")

            block = ctx.enter_context(nc.Block())
            LOADS2 = 16 * 9

            @block.sync
            def _(e):
                e.dma_start(we1[:, :, :], We1.rearrange("(k p) d -> p k d", p=P)).then_inc(loads, 16)
                e.dma_start(wn1[:, :, :], Wn1.rearrange("(k p) d -> p k d", p=P)).then_inc(loads, 16)
                e.dma_start(we2[:, :], We2).then_inc(loads, 16)
                e.dma_start(wn2[:, :], Wn2).then_inc(loads, 16)
                e.dma_start(be1_b[:, :], be1.partition_broadcast(P)).then_inc(loads, 16)
                e.dma_start(bn2_b[:, :], bn2.partition_broadcast(P)).then_inc(loads, 16)
                e.dma_start(be2_r[:, :], row(be2)).then_inc(loads, 16)
                with nc.allow_non_contiguous_dma(reason="a bias column of 128 numbers"):
                    e.dma_start(bn1_c[:, :], col(bn1)).then_inc(loads, 16)
                e.wait_ge(x_zero, 3)
                e.dma_start(X[:, 0:FULL, :], x[0:FULL * P, :].rearrange("(b p) d -> p b d", p=P)).then_inc(loads, 16)
                e.dma_start(X[0:REST, FULL, :], x[FULL * P:N, :]).then_inc(x_in, 16)

                def load(g, k):
                    at = val(e, g * G)
                    again(e, s["h2_done"], val(e, g - 1))
                    e.sem_inc(passed, 1)
                    e.dma_start(hT[k][:, :], hT_dram[:, bass.ds(at, G)]).then_inc(hT_in[k], 16)

                def store(g):
                    at = val(e, g * G)
                    seen = val(e, g + 1)
                    e.wait_ge(s["p_done"], seen)
                    e.sem_inc(passed, 1)
                    e.dma_start(p_table[bass.ds(at, G), :].rearrange("(b p) d -> p b d", p=P), p_rows[:, :, :]).then_inc(p_out_d, 16)
                    e.wait_ge(s["lo_done"], seen)
                    e.sem_inc(passed, 1)
                    e.dma_start(r_table[bass.ds(at, G), :].rearrange("(b p) (k d) -> p b k d", p=P, k=3), r_rows[:, :, :, :]).then_inc(r_out_d, 16)

                load(0, 0)
                load(1, 1)
                store(0)
                with e.Fori(0, NG // 2 - 1) as m:
                    load(m * 2 + 2, 0)
                    store(m * 2 + 1)
                    load(m * 2 + 3, 1)
                    store(m * 2 + 2)
                load(NG - 1, 0)
                store(NG - 2)
                store(NG - 1)
                e.wait_ge(p_out_d, 16 * NG)
                e.wait_ge(r_out_d, 16 * NG)

            @block.gpsimd
            def _(e):
                e.memset(X[:, FULL:BLOCKS, :], 0.0).then_inc(x_zero, 1)
                e.memset(nought[:, :], 0.0).then_inc(x_zero, 1)

                def clear(g):
                    at = g * G if isinstance(g, int) else e.snap(g * G, min_val=0, max_val=NP - G)
                    e.wait_ge(s["val_full"], val(e, g + 1))
                    e.wait_ge(s["den_full"], val(e, g + 1))
                    e.sem_inc(passed, 1)
                    for k in range(2):
                        e.tensor_copy(acc[:, k, bass.ds(at, G)], nought[:, :])
                    blk = e.snap(g * GB, min_val=0, max_val=BLOCKS - GB)
                    e.wait_ge(s["x1_done"], val(e, g * GB + GB))
                    e.wait_ge(s["x1T_done"], val(e, g + 1))
                    e.sem_inc(passed, 1)
                    e.tensor_copy(x1_rows[:, bass.ds(blk, GB), :], xn[:, :, :])
                    e.tensor_copy(x1T[:, bass.ds(at, G)], x1T_g[:, :]).then_inc(s["kept"], 1)

                e.wait_ge(x_zero, 3)
                with e.Fori(0, NG) as g:
                    clear(g)

            def groups(e, group):
                group(0, 0, 0)
                with e.Fori(0, NG // 2) as m:
                    group(m * 2 + 1, 1, m)
                    group(m * 2 + 2, 0, m + 1)

            assert NG % 2 == 1

            @block.tensor
            def _(e):
                def first(g, k, t):
                    at = g * G if isinstance(g, int) else e.snap(g * G, min_val=0, max_val=NP - G)
                    n0, n1 = val(e, g), val(e, g + 1)
                    again(e, s["den_done"], n0)
                    e.matmul(p_den[:, :], one_row[:, :], acc[0:A2, 1, bass.ds(at, G)], start=True, stop=True).then_inc(s["den_full"], 1)
                    again(e, s["mean_done"], n0)
                    e.matmul(p_val[:, :], wvT[:, :], acc[:, 0, bass.ds(at, G)], start=True, stop=False)
                    e.matmul(p_val[:, :], we_bvT[:, :], acc[0:A2, 1, bass.ds(at, G)], start=False, stop=True).then_inc(s["val_full"], 1)
                    e.wait_ge(hT_in[k], val(e, t * 16 + 16))
                    again(e, s["pre_done"], n0)
                    e.matmul(p_anti[:, :], aT[:, :], hT[k][:, :], start=True, stop=True).then_inc(s["anti_full"], 1)

                def second(g, k):
                    n0, n1 = val(e, g), val(e, g + 1)
                    e.wait_ge(s["outT_done"], n1)
                    again(e, s["y_done"], n0)
                    for b in range(GB):
                        mm = e.transpose(p_out[:, b * P:(b + 1) * P], outT[:, b * P:(b + 1) * P], ident[:, :])
                    mm.then_inc(s["out_full"], 1)

                def third(g, k):
                    n0, n1 = val(e, g), val(e, g + 1)
                    e.wait_ge(s["x1_done"], val(e, g * GB + GB))
                    again(e, s["x1T_done"], n0)
                    for b in range(GB):
                        mm = e.transpose(p_x1[:, b * P:(b + 1) * P], xn[:, b, :], ident[:, :])
                    mm.then_inc(s["x1_full"], 1)
                    e.wait_ge(s["x1T_done"], n1)
                    again(e, s["p_done"], n0)
                    again(e, s["r_done"], n0)
                    for b in range(GB):
                        mm = e.matmul((p_pr0, p_pr1)[b // 2][:, (b % 2) * 256:(b % 2) * 256 + 256], x1T_g[:, b * P:(b + 1) * P],
                                      we1[:, :, :].rearrange("p k d -> p (k d)"), start=True, stop=True)
                    mm.then_inc(s["pr_full"], 1)

                def group(g, k, t):
                    first(g, k, t)
                    second(g, k)
                    third(g, k)

                e.wait_ge(loads, LOADS2)
                groups(e, group)

            @block.scalar
            def _(e):
                def group(g, k, t):
                    n0, n1 = val(e, g), val(e, g + 1)
                    e.wait_ge(s["pre_done"], n1)
                    again(e, s["h2_done"], n0)
                    e.sem_inc(passed, 1)
                    e.activation(upd[:, :], pre[:, :], ACT.Tanh, bias=bac_c[:, 0:1]).then_inc(s["upd_done"], 1)
                    e.wait_ge(s["h2_done"], n1)
                    again(e, s["out_full"], n0)
                    e.sem_inc(passed, 1)
                    e.activation(outT[:, :], h2[:, :], ACT.Tanh).then_inc(s["outT_done"], 1)
                    e.wait_ge(s["mv_done"], val(e, g * GB + GB))
                    again(e, s["rstd_done"], n0)
                    e.sem_inc(passed, 1)
                    e.activation(std[:, :], mv[:, :, 1:2].rearrange("p b o -> p (b o)"), ACT.Sqrt, bias=eps_c[:, 0:1]).then_inc(s["std_done"], 1)
                    e.wait_ge(s["x1_full"], n1)
                    again(e, s["kept"], n0)
                    again(e, s["pr_full"], n0)
                    e.sem_inc(passed, 1)
                    e.activation(x1T_g[:, :], p_x1[:, :], ACT.Copy).then_inc(s["x1T_done"], 1)
                    e.wait_ge(s["pr_full"], n1)
                    again(e, p_out_d, val(e, g * 16))
                    e.sem_inc(passed, 1)
                    e.activation(p_rows[:, 0:2, :], p_pr0[:, :].rearrange("p (b k d) -> p b k d", k=2, d=D)[:, :, 0, :], ACT.Copy)
                    e.activation(p_rows[:, 2:4, :], p_pr1[:, :].rearrange("p (b k d) -> p b k d", k=2, d=D)[:, :, 0, :], ACT.Copy).then_inc(s["p_done"], 1)

                e.wait_ge(x_zero, 3)
                groups(e, group)

            @block.vector
            def _(e):
                e.memset(eps_c[:, :], EPS).then_inc(x_zero, 1)

                def group(g, k, t):
                    n0, n1 = val(e, g), val(e, g + 1)
                    at = g * G if isinstance(g, int) else e.snap(g * G, min_val=0, max_val=NP - G)
                    blk = g * GB if isinstance(g, int) else e.snap(g * GB, min_val=0, max_val=BLOCKS - GB)
                    e.wait_ge(s["den_full"], n1)
                    e.tensor_scalar(den[:, :], p_den[:, :], 1.0e-16, None, ALU.add).then_inc(s["den_done"], 1)
                    e.wait_ge(s["den_done"], n1)
                    e.reciprocal(rden[:, :], den[:, :]).then_inc(s["rden_done"], 1)
                    e.wait_ge(s["rden_done"], n1)
                    e.wait_ge(s["val_full"], n1)
                    e.tensor_tensor(mean_v[:, :], p_val[:, :], rden[:, :], ALU.mult).then_inc(s["mean_done"], 1)
                    e.wait_ge(s["mean_done"], n1)
                    e.wait_ge(s["anti_full"], n1)
                    e.tensor_tensor(pre[:, :], p_anti[:, :], mean_v[:, :], ALU.add).then_inc(s["pre_done"], 1)
                    e.wait_ge(s["upd_done"], n1)
                    again(e, s["outT_done"], n0)
                    e.tensor_tensor(h2[:, :], hT[k][:, :], upd[:, :], ALU.add).then_inc(s["h2_done"], 1)
                    e.wait_ge(s["out_full"], n1)
                    e.tensor_tensor(y[:, :, :], X[:, bass.ds(blk, GB), :], p_out[:, :].rearrange("p (b d) -> p b d", d=D), ALU.add).then_inc(s["y_done"], 1)
                    e.wait_ge(s["y_done"], n1)
                    for b in range(GB):
                        e.bn_stats(stats[:, b, :], y[:, b, :]).then_inc(s["stats_done"], 1)
                    again(e, s["std_done"], n0)
                    e.wait_ge(s["stats_done"], val(e, g * GB + GB))
                    e.sem_inc(passed, 1)
                    for b in range(GB):
                        e.bn_aggr(mv[:, b, :], stats[:, b, :]).then_inc(s["mv_done"], 1)
                    e.wait_ge(s["std_done"], n1)
                    e.reciprocal(rstd[:, :], std[:, :]).then_inc(s["rstd_done"], 1)
                    e.wait_ge(s["rstd_done"], n1)
                    again(e, s["kept"], n0)
                    again(e, s["x1_full"], n0)
                    for b in range(GB):
                        e.tensor_scalar(xn[:, b, :], y[:, b, :], mv[:, b, 0:1],
                                        rstd[:, b:b + 1], ALU.subtract, ALU.mult).then_inc(s["x1_done"], 1)
                    e.wait_ge(s["p_done"], n1)
                    for h, p in enumerate((p_pr0, p_pr1)):
                        op = e.tensor_tensor(r_f[:, 2 * h:2 * h + 2, :], p[:, :].rearrange("p (b k d) -> p b k d", k=2, d=D)[:, :, 1, :],
                                             be1_b[:, :].unsqueeze(1).broadcast_to([P, 2, D]), ALU.add)
                    op.then_inc(s["r_done"], 1)
                    e.wait_ge(s["r_done"], n1)
                    again(e, r_out_d, val(e, g * 16))
                    e.tensor_copy(r_rows[:, :, 0, :], r_f[:, :, :]).then_inc(s["hi_done"], 1)
                    e.wait_ge(s["hi_done"], n1)
                    e.tensor_tensor(r_g[:, :, :], r_f[:, :, :], r_rows[:, :, 0, :], ALU.subtract).then_inc(s["g_done"], 1)
                    e.wait_ge(s["g_done"], n1)
                    e.tensor_copy(r_rows[:, :, 1, :], r_g[:, :, :]).then_inc(s["mid_done"], 1)
                    e.wait_ge(s["mid_done"], n1)
                    e.tensor_tensor(r_rows[:, :, 2, :], r_g[:, :, :], r_rows[:, :, 1, :], ALU.subtract).then_inc(s["lo_done"], 1)

                e.wait_ge(loads, LOADS2)
                e.wait_ge(x_in, 16)
                groups(e, group)

        with ExitStack() as ctx:
            msg = [sb(f"msg{k}", [P, J, D], ctx=ctx) for k in range(SLOTS)]
            src_i = [sb(f"src1_{k}", [P, J], I32, ctx=ctx) for k in range(SLOTS)]
            dst_c = [sb(f"dst_c{k}", [P, J], I32, ctx=ctx) for k in range(2)]
            dst_b = [sb(f"dst1_b{k}", [P, CH], I32, ctx=ctx) for k in range(2)]
            r_win = [sb(f"r_win{k}", [P, 3, D], BF16, ctx=ctx) for k in range(2)]
            in_win = sb("in_win", [P, J], ctx=ctx)
            hotT = sb("hotT", [P, CH], BF16, ctx=ctx)
            hot = [sb(f"hot{k}", [P, J, W], ctx=ctx) for k in range(2)]
            p_edge = [ctx.enter_context(nc.psum_tensor(f"p_edge{k}", [P, 4, D], F32)) for k in range(2)]
            p_sum = ctx.enter_context(nc.psum_tensor("p_sum1", [P, 2, W], F32))

            src_in = [sem(f"src1_in{k}") for k in range(SLOTS)]
            win_in = [sem(f"win_in{k}") for k in range(2)]
            rows_in = [sem(f"rows1_in{k}") for k in range(SLOTS)]
            in_win_done = sem("in_win_done")
            hotT_done = sem("hotT_done")
            hot_done = sem("hot_done")
            edge_full = [sem(f"edge_full{h}") for h in range(2)]
            both_done = [sem(f"both_done{h}") for h in range(2)]
            relu_done = sem("relu_done")
            sum_full = sem("sum1_full")
            added = sem("added1")
            added2 = sem("added2")
            cut_done = sem("cut1_done")

            def layer1_round(r):
                base = r * TURNS
                with ExitStack() as c2:
                    block = c2.enter_context(nc.Block())

                    def shift(c, k):
                        return c[0] + (c[1] + k) // SLOTS, (c[1] + k) % SLOTS

                    def number(c):
                        return c[0] * SLOTS + c[1]

                    def count(c):
                        return (c[0] + base) * SLOTS + c[1]

                    def turns_of(e, run):
                        for u in range(SLOTS):
                            run((0, u))
                        with e.Fori(1, TURNS - 1) as i:
                            for u in range(SLOTS):
                                run((i, u))
                        for u in range(SLOTS):
                            run((TURNS - 1, u))

                    @block.sync
                    def _(e):
                        def load(c):
                            i, u = c
                            v = u % 2
                            last = isinstance(i, int) and number(c) == NCH - 1
                            at = LAST if last else val(e, number(c) * CH)
                            start = pick(e, start_i, number(c))
                            n = count(c)
                            free, free2 = val(e, n - SLOTS + 1), val(e, n - 1)
                            again(e, sum_full, free)
                            e.sem_inc(passed, 1)
                            e.dma_start(src_i[u][:, :], src[bass.ds(at, CH)].rearrange("(p j) -> p j", j=J)).then_inc(src_in[u], 16)
                            again(e, hot_done, free2)
                            again(e, edge_full[1], free2)
                            e.sem_inc(passed, 1)
                            e.dma_start(dst_c[v][:, :], dst[bass.ds(at, CH)].rearrange("(p j) -> p j", j=J)).then_inc(win_in[v], 16)
                            e.dma_start(dst_b[v][:, :], dst[bass.ds(at, CH)].partition_broadcast(P)).then_inc(win_in[v], 16)
                            e.dma_start(r_win[v][:, :, :], r_table[bass.ds(start, W), :].rearrange("p (k d) -> p k d", k=3)).then_inc(win_in[v], 16)

                        turns_of(e, load)

                    @block.gpsimd
                    def _(e):
                        def gather(c):
                            u = c[1]
                            e.wait_ge(src_in[u], val(e, (c[0] + base) * 16 + 16))
                            e.sem_inc(passed, 1)
                            for j in range(J):
                                e.indirect_dma_start(
                                    out=msg[u][:, j, :], out_offset=None, in_=p_table[:, :],
                                    in_offset=bass.IndirectOffsetOnAxis(ap=src_i[u][:, j:j + 1], axis=0)).then_inc(rows_in[u], 16)

                        with e.Fori(0, TURNS) as i:
                            for u in range(SLOTS):
                                gather((i, u))

                    @block.tensor
                    def _(e):
                        def edges(c):
                            v = c[1] % 2
                            n = count(c)
                            n0, n1 = val(e, n), val(e, n + 1)
                            e.wait_ge(hotT_done, n1)
                            for h in range(2):
                                again(e, both_done[h], n0)
                                for j in range(4 * h, 4 * h + 4):
                                    for k in range(3):
                                        mm = e.matmul(p_edge[h][:, j % 4, :], hotT[:, j:CH:J], r_win[v][:, k, :], start=(k == 0), stop=(k == 2))
                                mm.then_inc(edge_full[h], 1)

                        def sums(c):
                            u, v = c[1], c[1] % 2
                            n = count(c)
                            n0, n1 = val(e, n), val(e, n + 1)
                            e.wait_ge(relu_done, n1)
                            e.wait_ge(hot_done, n1)
                            again(e, added, n0)
                            again(e, added2, n0)
                            for j in range(J):
                                e.matmul(p_sum[:, 0, :], msg[u][:, j, :], hot[v][:, j, :], start=(j == 0), stop=(j == J - 1))
                            for j in range(J):
                                mm = e.matmul(p_sum[0:1, 1, :], ones[:, 0:1], hot[v][:, j, :], start=(j == 0), stop=(j == J - 1))
                            mm.then_inc(sum_full, 1)

                        def step(c):
                            if not (isinstance(c[0], int) and number(c) == NCH - 1):
                                edges(shift(c, 1))
                            sums(c)

                        edges((0, 0))
                        turns_of(e, step)

                    @block.scalar
                    def _(e):
                        def relus(c):
                            u = c[1]
                            e.wait_ge(both_done[1], val(e, count(c) + 1))
                            e.sem_inc(passed, 1)
                            e.activation(msg[u][:, :, :], msg[u][:, :, :], ACT.Relu).then_inc(relu_done, 1)

                        turns_of(e, relus)

                    @block.vector
                    def _(e):
                        def front(c):
                            i, u = c
                            v = u % 2
                            n = count(c)
                            n0, n1, nm = val(e, n), val(e, n + 1), val(e, n - 1)
                            idx = number(c)
                            uses = (i + base) * 2 + u // 2 + 1
                            e.wait_ge(win_in[v], val(e, uses * 48))
                            if isinstance(i, int) and idx == NCH - 1:
                                e.memset(dst_b[v][:, 0:DUP], -1).then_inc(cut_done, 1)
                                e.memset(dst_c[v][0:DUP // J, :], -1).then_inc(cut_done, 1)
                                e.wait_ge(cut_done, val(e, r * 2 + 2))
                            again(e, hot_done, n0)
                            e.tensor_scalar(in_win[:, :], dst_c[v][:, :], start_b[:, bass.ds(idx, 1)], None, ALU.subtract).then_inc(in_win_done, 1)
                            again(e, edge_full[1], n0)
                            e.tensor_scalar(hotT[:, :], dst_b[v][:, :], node_of[:, bass.ds(idx, 1)], None, ALU.is_equal).then_inc(hotT_done, 1)
                            e.wait_ge(in_win_done, n1)
                            again(e, sum_full, nm)
                            e.tensor_tensor(hot[v][:, :, :], in_win[:, :].unsqueeze(2).broadcast_to([P, J, W]),
                                            iota_row[:, :].unsqueeze(1).broadcast_to([P, J, W]), ALU.is_equal).then_inc(hot_done, 1)
                            e.wait_ge(rows_in[u], val(e, (i + base) * (16 * J) + 16 * J))
                            for h in range(2):
                                e.wait_ge(edge_full[h], n1)
                                part = msg[u][:, 4 * h:4 * h + 4, :]
                                e.tensor_tensor(part, part, p_edge[h][:, :, :], ALU.add).then_inc(both_done[h], 1)

                        def add(c):
                            n = count(c)
                            n0, n1 = val(e, n), val(e, n + 1)
                            start = pick(e, start_i, number(c))
                            again(e, added, n0)
                            again(e, added2, n0)
                            e.wait_ge(sum_full, n1)
                            here = acc[:, 0, bass.ds(start, W)]
                            e.tensor_tensor(here, here, p_sum[:, 0, :], ALU.add).then_inc(added, 1)
                            here = acc[0:1, 1, bass.ds(start, W)]
                            e.tensor_tensor(here, here, p_sum[0:1, 1, :], ALU.add).then_inc(added2, 1)

                        def step(c):
                            if not (isinstance(c[0], int) and number(c) == NCH - 1):
                                front(shift(c, 1))
                            add(c)

                        front((0, 0))
                        turns_of(e, step)

            with ExitStack() as c2:
                back_in = sem("back_in")
                back_done = sem("back_done")
                block = c2.enter_context(nc.Block())

                @block.sync
                def _(e):
                    e.dma_start(start_b[:, :], start_dram[0, :].partition_broadcast(P)).then_inc(back_in, 16)

                @block.vector
                def _(e):
                    e.wait_ge(back_in, 16)
                    e.tensor_copy(start_i[:, :], start_b[0:1, :])
                    e.tensor_scalar(node_of[:, :], start_b[:, :], iota_col[:, 0:1], None, ALU.add)

            layer1_round(0)
            spread_out = nc.values_load(span_i[0:1, 0:1], min_val=0, max_val=N)
            with nc.If(spread_out >= W):
                with nc.Fori(1, ROUNDS) as w:
                    move_windows()
                    layer1_round(w)

        with ExitStack() as ctx:
            agg = sb("agg", [P, G], ctx=ctx)
            hid = sb("hid", [P, G], ctx=ctx)
            twice = sb("twice", [P, GB, D], ctx=ctx)
            y = sb("y1", [P, GB, D], ctx=ctx)
            stats = sb("stats1", [P, GB, 6], ctx=ctx)
            mv = sb("mv1", [P, GB, 2], ctx=ctx)
            std = sb("std1", [P, GB], ctx=ctx)
            rstd = sb("rstd1", [P, GB], ctx=ctx)
            o_rows = [sb(f"o_rows{k}", [P, GB, D], ctx=ctx) for k in range(2)]
            p_agg, p_hid, p_mesh = (ctx.enter_context(nc.psum_tensor(f"psE{k}", [P, 512], F32)) for k in range(3))

            names = "agg_full agg_done hid_full hid_done mesh_full twice_done y_done stats_done mv_done std_done rstd_done o_done".split()
            s = {n: sem(n + "1") for n in names}
            o_out = [sem(f"o_out{k}") for k in range(2)]
            block = ctx.enter_context(nc.Block())

            @block.sync
            def _(e):
                def store(g, k, t):
                    at = val(e, g * G)
                    e.wait_ge(s["o_done"], val(e, g * GB + GB))
                    e.sem_inc(passed, 1)
                    e.dma_start(out[bass.ds(at, G), :].rearrange("(b p) d -> p b d", p=P), o_rows[k][:, :, :]).then_inc(o_out[k], 16)

                with e.Fori(0, NG // 2) as m:
                    store(m * 2, 0, m)
                    store(m * 2 + 1, 1, m)
                e.wait_ge(s["o_done"], NG * GB)
                e.dma_start(out[FULL * P:N, :], o_rows[0][0:REST, 0, :]).then_inc(o_out[0], 16)
                e.wait_ge(o_out[0], 16 * (NG // 2 + 1))
                e.wait_ge(o_out[1], 16 * (NG // 2))

            @block.tensor
            def _(e):
                def group(g, k, t):
                    at = g * G if isinstance(g, int) else e.snap(g * G, min_val=0, max_val=NP - G)
                    n0, n1 = val(e, g), val(e, g + 1)
                    again(e, s["agg_done"], n0)
                    e.matmul(p_agg[:, :], we2[:, :], acc[:, 0, bass.ds(at, G)], start=True, stop=False)
                    e.matmul(p_agg[:, :], be2_r[:, :], acc[0:1, 1, bass.ds(at, G)], start=False, stop=True).then_inc(s["agg_full"], 1)
                    e.wait_ge(s["agg_done"], n1)
                    again(e, s["hid_done"], n0)
                    e.matmul(p_hid[:, :], wn1[:, 0, :], x1T[:, bass.ds(at, G)], start=True, stop=False)
                    e.matmul(p_hid[:, :], wn1[:, 1, :], agg[:, :], start=False, stop=True).then_inc(s["hid_full"], 1)
                    e.wait_ge(s["hid_done"], n1)
                    again(e, s["y_done"], n0)
                    for b in range(GB):
                        mm = e.matmul(p_mesh[:, b * D:(b + 1) * D], hid[:, b * P:(b + 1) * P], wn2[:, :], start=True, stop=True)
                    mm.then_inc(s["mesh_full"], 1)

                groups(e, group)

            @block.scalar
            def _(e):
                def group(g, k, t):
                    n0, n1 = val(e, g), val(e, g + 1)
                    e.wait_ge(s["agg_full"], n1)
                    again(e, s["hid_full"], n0)
                    e.sem_inc(passed, 1)
                    e.activation(agg[:, :], p_agg[:, :], ACT.Copy).then_inc(s["agg_done"], 1)
                    e.wait_ge(s["hid_full"], n1)
                    again(e, s["mesh_full"], n0)
                    e.sem_inc(passed, 1)
                    e.activation(hid[:, :], p_hid[:, :], ACT.Relu, bias=bn1_c[:, 0:1]).then_inc(s["hid_done"], 1)
                    e.wait_ge(s["mv_done"], val(e, g * GB + GB))
                    again(e, s["rstd_done"], n0)
                    e.sem_inc(passed, 1)
                    e.activation(std[:, :], mv[:, :, 1:2].rearrange("p b o -> p (b o)"), ACT.Sqrt, bias=eps_c[:, 0:1]).then_inc(s["std_done"], 1)

                groups(e, group)

            @block.vector
            def _(e):
                def group(g, k, t):
                    n0, n1 = val(e, g), val(e, g + 1)
                    blk = g * GB if isinstance(g, int) else e.snap(g * GB, min_val=0, max_val=BLOCKS - GB)
                    e.scalar_tensor_tensor(out=twice[:, :, :], in0=x1_rows[:, bass.ds(blk, GB), :], scalar=2.0,
                                           in1=bn2_b[:, :].unsqueeze(1).broadcast_to([P, GB, D]), op0=ALU.mult,
                                           op1=ALU.add).then_inc(s["twice_done"], 1)
                    e.wait_ge(s["twice_done"], n1)
                    e.wait_ge(s["mesh_full"], n1)
                    e.tensor_tensor(y[:, :, :], twice[:, :, :], p_mesh[:, :].rearrange("p (b d) -> p b d", d=D), ALU.add).then_inc(s["y_done"], 1)
                    e.wait_ge(s["y_done"], n1)
                    for b in range(GB):
                        e.bn_stats(stats[:, b, :], y[:, b, :]).then_inc(s["stats_done"], 1)
                    again(e, s["std_done"], n0)
                    e.wait_ge(s["stats_done"], val(e, g * GB + GB))
                    e.sem_inc(passed, 1)
                    for b in range(GB):
                        e.bn_aggr(mv[:, b, :], stats[:, b, :]).then_inc(s["mv_done"], 1)
                    e.wait_ge(s["std_done"], n1)
                    e.reciprocal(rstd[:, :], std[:, :]).then_inc(s["rstd_done"], 1)
                    e.wait_ge(s["rstd_done"], n1)
                    again(e, o_out[k], val(e, t * 16))
                    for b in range(GB):
                        e.tensor_scalar(o_rows[k][:, b, :], y[:, b, :], mv[:, b, 0:1], rstd[:, b:b + 1], ALU.subtract,
                                        ALU.mult).then_inc(s["o_done"], 1)

                groups(e, group)


_INS = ["x", "src", "dst", "edge_attr_32", "edge_weight", "node_vec", "L0_gnn_time_w", "L0_gnn_time_b", "L0_gnn_Wx",
        "L0_gnn_bx", "L0_gnn_Wq", "L0_gnn_bq", "L0_gnn_Wk", "L0_gnn_bk", "L0_gnn_Wv", "L0_gnn_bv", "L0_gnn_We",
        "L0_gnn_W_ac", "L0_gnn_b_ac", "L1_gnn_We1", "L1_gnn_be1", "L1_gnn_We2", "L1_gnn_be2", "L1_gnn_Wn1",
        "L1_gnn_bn1", "L1_gnn_Wn2", "L1_gnn_bn2"]
_OUTS = [((6250, 128), "float32")]


def kernel(**inputs):
    import numpy as _np
    import concourse.bacc as _bacc
    from concourse import mybir as _mybir
    from concourse.bass_utils import run_bass_kernel_spmd as _run

    nc = _bacc.Bacc("TRN2", target_bir_lowering=False, num_devices=1)
    arrays, args = {}, []
    for name in _INS:
        a = _np.ascontiguousarray(inputs[name])
        arrays[f"in_{name}_dram"] = a
        args.append(nc.dram_tensor(f"in_{name}_dram", a.shape, _mybir.dt.from_np(a.dtype), kind="ExternalInput").ap())
    for i, (shape, dtype) in enumerate(_OUTS):
        dt = _mybir.dt.from_np(_np.dtype(dtype))
        args.append(nc.dram_tensor(f"out_{i}_dram", shape, dt, kind="ExternalOutput").ap())
    gnn_kernel(nc, *args)
    r = _run(nc, [arrays], core_ids=[0])
    return r.results[0]["out_0_dram"]
```

```python
from contextlib import ExitStack
from math import pi

import concourse.bass as bass
from concourse import mybir

F32 = mybir.dt.float32
BF16 = mybir.dt.bfloat16
I32 = mybir.dt.int32
ALU = mybir.AluOpType
ACT = mybir.ActivationFunctionType
AX_X = mybir.AxisListType.X

P = 128
D = 128
FE = 32
J = 8
CH = P * J
HALF = CH // 2
W = 80
SLOTS = 7
G = 512
GB = G // P
ROW = 1 + D
A2 = 2 * FE + 1
HEW = ROW + A2
NEVER = -1.0e30
LOW = -1.0e20
ROUND = 1.5 * 2.0**23
EPS = 1.0e-5
GAMMA = 0.1


def gnn_kernel(nc, x, src, dst, edge_attr, edge_weight, node_vec, time_w, time_b, Wx, bx, Wq, bq, Wk, bk,
               Wv, bv, We, W_ac, b_ac, We1, be1, We2, be2, Wn1, bn1, Wn2, bn2, out):
    N = x.shape[0]
    E = src.shape[0]
    NCH = -(-E // CH)
    LAST = E - CH
    DUP = NCH * CH - E
    TURNS = NCH // SLOTS
    NG = -(-(N + W) // G)
    NP = NG * G
    BLOCKS = NP // P
    FULL, REST = N // P, N % P
    ROUNDS = -(-N // W)
    SCALE = float(D) ** -0.5
    assert NCH % SLOTS == 0 and DUP % J == 0 and TURNS > 1 and REST and FULL // GB == NG - 1

    h_table = nc.dram_tensor("h_table", [NP, ROW], F32)
    qk_table = nc.dram_tensor("qk_table", [P, 2, NP], F32)
    hT_dram = nc.dram_tensor("hT_dram", [P, NP], F32)
    p_table = nc.dram_tensor("p_table", [NP, D], F32)
    r_table = nc.dram_tensor("r_table", [NP, 3 * D], BF16)
    start_dram = nc.dram_tensor("start_dram", [2, NCH], F32)

    with ExitStack() as whole:
        def sb(name, shape, dt=F32, ctx=whole):
            return ctx.enter_context(nc.sbuf_tensor(name, shape, dt))

        def sem(name, ctx=whole):
            return ctx.enter_context(nc.semaphore(name))

        def val(eng, v):
            return v if isinstance(v, int) else eng.snap(v)

        def again(eng, s, v):
            if not isinstance(v, int) or v > 0:
                eng.wait_ge(s, v)

        ident = sb("ident", [P, P])
        ones = sb("ones", [P, P])
        iota_row = sb("iota_row", [P, W])
        start_i = sb("start_i", [1, NCH], I32)
        start_b = sb("start_b", [P, NCH])
        span_i = sb("span_i", [1, 1], I32)
        wvT = sb("wvT", [P, D])
        we_bvT = sb("we_bvT", [A2, D])
        one_row = sb("one_row", [A2, P])
        aT = sb("aT", [P, D])
        bac_c = sb("bac_c", [P, 1])
        tw_b = sb("tw_b", [P, FE])
        tb_b = sb("tb_b", [P, FE])
        acc = sb("acc", [P, 2, NP])

        passed = sem("passed")

        layer0 = whole.enter_context(ExitStack())
        tops_so_far = sb("tops_so_far", [P, NP], ctx=layer0)

        with ExitStack() as ctx:
            xg = [sb(f"xg{k}", [P, GB, D], ctx=ctx) for k in range(2)]
            x_tail = sb("x_tail", [P, GB, D], ctx=ctx)
            wx = sb("wx", [P, D], ctx=ctx)
            wq = sb("wq", [P, D], ctx=ctx)
            wk = sb("wk", [P, D], ctx=ctx)
            wv = sb("wv", [P, D], ctx=ctx)
            wac = sb("wac", [P, D], ctx=ctx)
            we_bk = sb("we_bk", [P, A2], ctx=ctx)
            wxT = sb("wxT", [P, D], ctx=ctx)
            wqT = sb("wqT", [P, D], ctx=ctx)
            bx_c = sb("bx_c", [P, 1], ctx=ctx)
            bq_c = sb("bq_c", [P, 1], ctx=ctx)
            bx_b = sb("bx_b", [P, D], ctx=ctx)
            tw_raw = sb("tw_raw", [P, FE], ctx=ctx)
            tb_raw = sb("tb_raw", [P, FE], ctx=ctx)
            nv_rows = sb("nv_rows", [BLOCKS, P], ctx=ctx)
            nv_cols = sb("nv_cols", [P, BLOCKS], ctx=ctx)
            dT = sb("dT", [P, D], ctx=ctx)
            xT = sb("xT", [P, G], ctx=ctx)
            hT = sb("hT", [P, G], ctx=ctx)
            qT = sb("qT", [P, G], ctx=ctx)
            qk = sb("qk", [P, 2, G], ctx=ctx)
            h_rows = sb("h_rows", [P, GB, ROW], ctx=ctx)
            CP = (NCH - 1) // 3
            dst_a = sb("dst_a", [CP, 3, CH], I32, ctx=ctx)
            dst_z = sb("dst_z", [1, CH], I32, ctx=ctx)
            ends_a = sb("ends_a", [CP, 2, 3], ctx=ctx)
            ends_z = sb("ends_z", [1, 2], ctx=ctx)
            ends_r = sb("ends_r", [1, 2, NCH], ctx=ctx)
            span_r = sb("span_r", [1, NCH], ctx=ctx)
            span_m = sb("span_m", [1, 1], ctx=ctx)

            ps = [ctx.enter_context(nc.psum_tensor(f"psA{k}", [P, 512], F32)) for k in range(7)]
            p_xT, p_hT, p_rows, p_qT, p_k1, p_k2, p_w = ps

            early = whole.enter_context(ExitStack())
            loads = sem("loads", early)
            x_zero = sem("x_zero", early)
            x_in = [sem(f"x_in{k}", early) for k in range(2)]
            tail_in = sem("tail_in", early)
            qk_out = sem("qk_out", early)
            dst_in = sem("dst_in", early)
            ends_done = sem("ends_done", early)
            ends_out = sem("ends_out", early)
            ends_in = sem("ends_in", early)
            consts = sem("consts", early)
            w_turned = sem("w_turned", early)
            w_copied = sem("w_copied", early)
            step = sem("step", early)
            one_done = sem("one_done", early)
            xT_full = sem("xT_full", early)
            xT_done = sem("xT_done", early)
            hT_full = sem("hT_full", early)
            hT_done = sem("hT_done", early)
            rows_full = sem("rows_full", early)
            rows_done = sem("rows_done", early)
            q_full = sem("q_full", early)
            q_done = sem("q_done", early)
            k1_full = sem("k1_full", early)
            k1_done = sem("k1_done", early)
            k2_full = sem("k2_full", early)
            k2_done = sem("k2_done", early)
            h_out = sem("h_out", early)
            hT_out = sem("hT_out", early)

            def col(v):
                return v.rearrange("(p o) -> p o", o=1)

            def row(v):
                return v.rearrange("(o d) -> o d", o=1)

            steps = ctx.enter_context(ExitStack())
            block = steps.enter_context(nc.Block())

            LOADS = 16 * 14

            @block.sync
            def _(e):
                for tile, m in ((wx, Wx), (wq, Wq), (wk, Wk), (wv, Wv), (wac, W_ac)):
                    e.dma_start(tile[:, :], m).then_inc(loads, 16)
                e.dma_start(we_bk[:, 0:2 * FE], We).then_inc(loads, 16)
                with nc.allow_non_contiguous_dma(reason="bias columns, 128 numbers each"):
                    e.dma_start(we_bk[:, 2 * FE:A2], col(bk)).then_inc(loads, 16)
                    e.dma_start(bx_c[:, :], col(bx)).then_inc(loads, 16)
                    e.dma_start(bq_c[:, :], col(bq)).then_inc(loads, 16)
                    e.dma_start(bac_c[:, :], col(b_ac)).then_inc(loads, 16)
                e.dma_start(bx_b[:, :], bx.partition_broadcast(P)).then_inc(loads, 16)
                e.dma_start(tw_raw[:, :], time_w.partition_broadcast(P)).then_inc(loads, 16)
                e.dma_start(tb_raw[:, :], time_b.partition_broadcast(P)).then_inc(loads, 16)
                e.dma_start(we_bvT[2 * FE:A2, :], row(bv)).then_inc(loads, 16)
                e.wait_ge(x_zero, 2)
                e.dma_start(x_tail[0:REST, 0, :], x[FULL * P:N, :]).then_inc(tail_in, 16)
                e.dma_start(nv_rows[0:FULL, :], node_vec[0:FULL * P].rearrange("(b p) -> b p", p=P)).then_inc(tail_in, 16)
                e.dma_start(nv_rows[FULL:FULL + 1, 0:REST], row(node_vec[FULL * P:N])).then_inc(tail_in, 16)
                e.dma_start(dst_a[:, :, :], dst[0:3 * CP * CH].rearrange("(p k c) -> p k c", k=3, c=CH)).then_inc(dst_in, 16)
                e.dma_start(dst_z[:, :], row(dst[LAST:E])).then_inc(dst_in, 16)
                e.wait_ge(ends_done, 4)
                for k in range(2):
                    e.dma_start(start_dram[k, 0:NCH - 1].rearrange("(p k) -> p k", k=3), ends_a[:, k, :]).then_inc(ends_out, 16)
                    e.dma_start(start_dram[k:k + 1, NCH - 1:NCH], ends_z[:, k:k + 1]).then_inc(ends_out, 16)
                e.wait_ge(ends_out, 64)
                e.dma_start(ends_r[:, :, :], start_dram[:, :].rearrange("(o k) c -> o k c", o=1)).then_inc(ends_in, 16)
                e.dma_start(start_b[:, :], start_dram[0, :].partition_broadcast(P)).then_inc(ends_in, 16)

                def load(g, k):
                    at = val(e, g * G)
                    again(e, xT_full, val(e, g - 1))
                    e.sem_inc(passed, 1)
                    e.dma_start(xg[k][:, :, :], x[bass.ds(at, G), :].rearrange("(b p) d -> p b d", p=P)).then_inc(x_in[k], 16)

                def store(g):
                    at = val(e, g * G)
                    seen = val(e, g + 1)
                    e.wait_ge(hT_done, seen)
                    e.sem_inc(passed, 1)
                    e.dma_start(hT_dram[:, bass.ds(at, G)], hT[:, :]).then_inc(hT_out, 16)
                    e.wait_ge(rows_done, seen)
                    e.sem_inc(passed, 1)
                    e.dma_start(h_table[bass.ds(at, G), :].rearrange("(b p) d -> p b d", p=P), h_rows[:, :, :]).then_inc(h_out, 16)
                    e.wait_ge(k1_done, seen)
                    e.wait_ge(k2_done, seen)
                    e.sem_inc(passed, 1)
                    e.dma_start(qk_table[:, :, bass.ds(at, G)], qk[:, :, :]).then_inc(qk_out, 16)

                load(0, 0)
                load(1, 1)
                store(0)
                with e.Fori(0, NG // 2 - 1) as m:
                    load(m * 2 + 2, 0)
                    store(m * 2 + 1)
                    load(m * 2 + 3, 1)
                    store(m * 2 + 2)
                store(NG - 2)
                store(NG - 1)
                e.wait_ge(hT_out, 16 * NG)
                e.wait_ge(h_out, 16 * NG)
                e.wait_ge(qk_out, 16 * NG)

            @block.gpsimd
            def _(e):
                e.memset(x_tail[:, :, :], 0.0).then_inc(x_zero, 1)
                e.memset(nv_rows[:, :], 0.0).then_inc(x_zero, 1)
                e.memset(ident[:, :], 0.0).then_inc(step, 1)
                e.memset(ones[:, :], 1.0).then_inc(consts, 1)
                e.wait_ge(step, 1)
                e.affine_select(out=ident[:, :], in_=ident[:, :], compare_op=ALU.not_equal, fill=1.0, base=0,
                                pattern=[[-1, P]], channel_multiplier=1).then_inc(consts, 1)
                e.iota(iota_row[:, :], pattern=[[1, W]], base=0, channel_multiplier=0,
                       allow_small_or_imprecise_dtypes=True).then_inc(consts, 1)
                e.memset(acc[:, :, :], 0.0).then_inc(consts, 1)
                e.memset(tops_so_far[:, :], LOW).then_inc(consts, 1)
                e.memset(qk[:, 1, :], 0.0).then_inc(consts, 1)

            @block.tensor
            def _(e):
                e.wait_ge(consts, 3)
                e.wait_ge(loads, LOADS)
                e.wait_ge(tail_in, 48)
                turned = 0
                for tile in (wx, wq, wv, wac):
                    e.transpose(p_w[:, turned * P:(turned + 1) * P], tile[:, :], ident[:, :])
                    turned += 1
                e.transpose(p_k2[0:2 * FE, 0:P], we_bk[:, 0:2 * FE], ident[:, :])
                e.transpose(p_k2[:, P:P + BLOCKS], nv_rows[:, :], ident[0:BLOCKS, 0:BLOCKS]).then_inc(w_turned, 1)
                e.wait_ge(w_copied, 6)

                def group(g, k, t):
                    before, seen = val(e, g), val(e, g + 1)
                    rows = x_tail if k is None else xg[k]
                    if k is not None:
                        e.wait_ge(x_in[k], val(e, t * 16 + 16))
                    again(e, xT_done, before)
                    for b in range(GB):
                        mm = e.transpose(p_xT[:, b * P:(b + 1) * P], rows[:, b, :], ident[:, :])
                    mm.then_inc(xT_full, 1)
                    e.wait_ge(xT_done, seen)
                    again(e, hT_done, before)
                    e.matmul(p_hT[:, :], wxT[:, :], xT[:, :], start=True, stop=True).then_inc(hT_full, 1)
                    again(e, rows_done, before)
                    for k in range(GB):
                        mm = e.matmul(p_rows[:, k * D:(k + 1) * D], xT[:, k * P:(k + 1) * P], wxT[:, :], start=True, stop=True)
                    mm.then_inc(rows_full, 1)
                    e.wait_ge(hT_done, seen)
                    again(e, q_done, before)
                    e.matmul(p_qT[:, :], wqT[:, :], hT[:, :], start=True, stop=True).then_inc(q_full, 1)
                    e.wait_ge(q_done, seen)
                    again(e, k1_done, before)
                    e.matmul(p_k1[:, :], wk[:, :], qT[:, :], start=True, stop=True).then_inc(k1_full, 1)
                    again(e, k2_done, before)
                    e.matmul(p_k2[0:A2, :], we_bk[:, :], qT[:, :], start=True, stop=True).then_inc(k2_full, 1)

                group(0, 0, 0)
                with e.Fori(0, NG // 2 - 1) as m:
                    group(m * 2 + 1, 1, m)
                    group(m * 2 + 2, 0, m + 1)
                group(NG - 2, 1, NG // 2 - 1)
                group(NG - 1, None, 0)

            @block.scalar
            def _(e):
                e.wait_ge(loads, LOADS)
                e.wait_ge(consts, 6)

                def group(g):
                    before, seen = val(e, g), val(e, g + 1)
                    again(e, rows_full, before)
                    e.wait_ge(xT_full, seen)
                    e.sem_inc(passed, 1)
                    e.activation(xT[:, :], p_xT[:, :], ACT.Copy).then_inc(xT_done, 1)
                    again(e, q_full, before)
                    again(e, hT_out, g * 16)
                    e.wait_ge(hT_full, seen)
                    e.sem_inc(passed, 1)
                    e.activation(hT[:, :], p_hT[:, :], ACT.Identity, bias=bx_c[:, 0:1]).then_inc(hT_done, 1)
                    again(e, k2_full, before)
                    e.wait_ge(q_full, seen)
                    e.sem_inc(passed, 1)
                    e.activation(qT[:, :], p_qT[:, :], ACT.Identity, bias=bq_c[:, 0:1]).then_inc(q_done, 1)
                    e.wait_ge(k2_full, seen)
                    again(e, qk_out, g * 16)
                    e.sem_inc(passed, 1)
                    e.activation(qk[0:A2, 1, :], p_k2[0:A2, :], ACT.Copy, scale=SCALE).then_inc(k2_done, 1)

                group(0)
                with e.Fori(1, NG) as g:
                    group(g)

            @block.vector
            def _(e):
                e.memset(one_row[:, :], 0.0).then_inc(one_done, 1)
                e.wait_ge(one_done, 1)
                e.memset(one_row[2 * FE:A2, :], 1.0).then_inc(one_done, 1)
                e.wait_ge(w_turned, 1)
                e.tensor_copy(wxT[:, :], p_w[:, 0:P]).then_inc(w_copied, 1)
                e.tensor_copy(wqT[:, :], p_w[:, P:2 * P]).then_inc(w_copied, 1)
                e.tensor_copy(wvT[:, :], p_w[:, 2 * P:3 * P]).then_inc(w_copied, 1)
                e.tensor_copy(we_bvT[0:2 * FE, :], p_k2[0:2 * FE, 0:P]).then_inc(w_copied, 1)
                e.tensor_copy(nv_cols[:, :], p_k2[:, P:P + BLOCKS]).then_inc(w_copied, 1)
                e.tensor_tensor(dT[:, :], p_w[:, 3 * P:4 * P], wac[:, :], ALU.subtract).then_inc(w_copied, 1)
                e.wait_ge(w_copied, 6)
                e.scalar_tensor_tensor(out=aT[:, :], in0=ident[:, :], scalar=-GAMMA, in1=dT[:, :], op0=ALU.mult,
                                       op1=ALU.add).then_inc(w_copied, 1)
                e.wait_ge(loads, LOADS)
                e.tensor_scalar(tw_b[:, :], tw_raw[:, :], 1.0 / (2.0 * pi), None, ALU.mult)
                e.tensor_scalar(tb_b[:, :], tb_raw[:, :], 1.0 / (2.0 * pi), 0.25, ALU.mult, ALU.add)
                e.wait_ge(dst_in, 32)
                for k, op in enumerate((ALU.min, ALU.max)):
                    e.tensor_reduce(ends_a[:, k, :], dst_a[:, :, :], AX_X, op).then_inc(ends_done, 1)
                    e.tensor_reduce(ends_z[:, k:k + 1], dst_z[:, :], AX_X, op).then_inc(ends_done, 1)
                e.wait_ge(ends_in, 32)
                e.wait_ge(consts, 6)
                e.tensor_copy(start_i[:, :], ends_r[:, 0, :])
                e.tensor_tensor(span_r[:, :], ends_r[:, 1, :], ends_r[:, 0, :], ALU.subtract).then_inc(ends_done, 1)
                e.wait_ge(ends_done, 5)
                e.tensor_reduce(span_m[:, :], span_r[:, :], AX_X, ALU.max).then_inc(ends_done, 1)
                e.wait_ge(ends_done, 6)
                e.tensor_copy(span_i[:, :], span_m[:, :]).then_inc(ends_done, 1)

                def group(g):
                    blk = g * GB if isinstance(g, int) else e.snap(g * GB, min_val=0, max_val=BLOCKS - GB)
                    seen = val(e, g + 1)
                    again(e, h_out, g * 16)
                    e.tensor_copy(h_rows[:, :, 0:1], nv_cols[:, bass.ds(blk, GB)].rearrange("p (b o) -> p b o", o=1))
                    e.wait_ge(rows_full, seen)
                    e.tensor_tensor(h_rows[:, :, 1:ROW], p_rows[:, :].rearrange("p (b d) -> p b d", d=D),
                                    bx_b[:, :].unsqueeze(1).broadcast_to([P, GB, D]), ALU.add).then_inc(rows_done, 1)
                    e.wait_ge(k1_full, seen)
                    again(e, qk_out, g * 16)
                    e.tensor_scalar(qk[:, 0, :], p_k1[:, :], SCALE, None, ALU.mult).then_inc(k1_done, 1)

                group(0)
                with e.Fori(1, NG) as g:
                    group(g)

            steps.close()
            with ExitStack() as c2:
                block = c2.enter_context(nc.Block())

                @block.sync
                def _(e):
                    for used in (x_in[0], x_in[1], loads, x_zero, tail_in, qk_out, dst_in, ends_done, ends_out, ends_in, consts, w_turned, w_copied, step, one_done, xT_full, xT_done, hT_full, hT_done, rows_full, rows_done, q_full, q_done, k1_full, k1_done, k2_full, k2_done, h_out, hT_out):
                        e.sem_clear(used)

            early.close()

        moved = sem("moved")

        def move_windows():
            with ExitStack() as ctx:
                block = ctx.enter_context(nc.Block())

                @block.vector
                def _(e):
                    e.tensor_scalar(start_b[:, :], start_b[:, :], float(W), float(N), ALU.add, ALU.min).then_inc(moved, 1)
                    e.wait_ge(moved, 1)
                    e.tensor_copy(start_i[:, :], start_b[0:1, :]).then_inc(moved, 1)
                    e.wait_ge(moved, 2)
                    e.sem_clear(moved)

        def pick(e, index):
            return e.value_load(start_i[0:1, bass.ds(index, 1)], min_val=0, max_val=N)

        def shift(c, k):
            return c[0] + (c[1] + k) // SLOTS, (c[1] + k) % SLOTS

        def number(c):
            return c[0] * SLOTS + c[1]

        def is_last(c):
            return isinstance(c[0], int) and number(c) == NCH - 1

        def is_first(c):
            return isinstance(c[0], int) and number(c) == 0

        def chunks(e, run):
            for u in range(SLOTS):
                run((0, u))
            with e.Fori(1, TURNS - 1) as i:
                for u in range(SLOTS):
                    run((i, u))
            for u in range(SLOTS):
                run((TURNS - 1, u))

        with ExitStack() as ctx:
            he = [sb(f"he{k}", [P, J, HEW], ctx=ctx) for k in range(SLOTS)]
            src_i = [sb(f"src_i{k}", [P, J], I32, ctx=ctx) for k in range(SLOTS)]
            dst_c = [sb(f"dst_c{k}", [P, J], I32, ctx=ctx) for k in range(SLOTS)]
            when = [sb(f"when{k}", [P, J], ctx=ctx) for k in range(SLOTS)]
            feat = [sb(f"feat{k}", [P, J, FE], ctx=ctx) for k in range(SLOTS)]
            qk_win = [sb(f"qk_win{k}", [P, 2, W], ctx=ctx) for k in range(SLOTS)]
            gap = sb("gap", [P, J], ctx=ctx)
            dist = sb("dist", [P, J], ctx=ctx)
            turns_w = sb("turns_w", [P, J, FE], ctx=ctx)
            turns = sb("turns", [P, J, FE], ctx=ctx)
            turns_r = sb("turns_r", [P, J, FE], ctx=ctx)
            in_win = sb("in_win", [P, J], ctx=ctx)
            other = sb("other", [P, J, W], BF16, ctx=ctx)
            heT1 = sb("heT1", [P, CH], ctx=ctx)
            heT2 = sb("heT2", [A2, CH], ctx=ctx)
            score = sb("score", [P, J, W], ctx=ctx)
            top_j = sb("top_j", [P, W], ctx=ctx)
            top_n = sb("top_n", [W, 1], ctx=ctx)
            top_d = sb("top_d", [W, W], ctx=ctx)
            top = sb("top", [P, W], ctx=ctx)
            rise = sb("rise", [P, W], ctx=ctx)
            fade = sb("fade", [P, W], ctx=ctx)
            prob = sb("prob", [P, J, W], ctx=ctx)

            p_turn = [ctx.enter_context(nc.psum_tensor(f"p_turn{k}", [P, 512], F32)) for k in range(4)]
            p_score = [ctx.enter_context(nc.psum_tensor(f"p_score{k}", [P, J // 2, W], F32)) for k in range(2)]
            p_sum = ctx.enter_context(nc.psum_tensor("p_sum", [P, 2, W], F32))
            p_small = ctx.enter_context(nc.psum_tensor("p_small", [P, P + W], F32))
            p_topT, p_top = p_small[0:W, 0:P], p_small[:, P:P + W]

            loaded = [sem(f"loaded{k}") for k in range(SLOTS)]
            rows_in = [sem(f"rows_in{k}") for k in range(SLOTS)]
            gap_done = sem("gap_done")
            dist_done = sem("dist_done")
            turns_w_done = sem("turns_w_done")
            turns_done = sem("turns_done")
            turns_r_done = sem("turns_r_done")
            phase_done = sem("phase_done")
            he_done = sem("he_done")
            in_win_done = sem("in_win0_done")
            other_done = sem("other_done")
            turn_full = [sem(f"turn_full{q}") for q in range(4)]
            turn_done = [sem(f"turn_done{q}") for q in range(4)]
            score_full = [sem(f"score_full{h}") for h in range(2)]
            masked = [sem(f"masked{h}") for h in range(2)]
            top_j_done = sem("top_j_done")
            topT_full = sem("topT_full")
            top_n_done = sem("top_n_done")
            top_d_done = sem("top_d_done")
            top_full = sem("top_full")
            top_done = sem("top_done")
            rise_done = sem("rise_done")
            below_done = sem("below_done")
            fade_done = sem("fade_done")
            prob_done = sem("prob_done")
            kept_top = sem("kept_top")
            faded = sem("faded")
            sum_full = sem("sum_full")
            added = sem("added")
            cut_done = sem("cut_done")
            ready = sem("ready")

            with ExitStack() as c2:
                block = c2.enter_context(nc.Block())

                @block.gpsimd
                def _(e):
                    for k in range(SLOTS):
                        e.memset(he[k][:, :, HEW - 1:HEW], 1.0).then_inc(ready, 1)

                @block.vector
                def _(e):
                    e.memset(p_sum[:, :, :], 0.0).then_inc(ready, 1)

            def layer0_round(r):
                base = r * TURNS
                with ExitStack() as c2:
                    block = c2.enter_context(nc.Block())

                    def count(c):
                        return (c[0] + base) * SLOTS + c[1]

                    @block.sync
                    def _(e):
                        def load(c):
                            i, u = c
                            at = LAST if is_last(c) else val(e, number(c) * CH)
                            start = pick(e, number(c))
                            again(e, sum_full, val(e, count(c) - SLOTS + 1))
                            e.sem_inc(passed, 1)
                            e.dma_start(src_i[u][:, :], src[bass.ds(at, CH)].rearrange("(p j) -> p j", j=J)).then_inc(loaded[u], 16)
                            e.dma_start(when[u][:, :], edge_weight[bass.ds(at, CH)].rearrange("(p j) -> p j", j=J)).then_inc(loaded[u], 16)
                            e.dma_start(feat[u][:, :, :], edge_attr[bass.ds(at, CH), :].rearrange("(p j) f -> p j f", j=J)).then_inc(loaded[u], 16)
                            e.dma_start(dst_c[u][:, :], dst[bass.ds(at, CH)].rearrange("(p j) -> p j", j=J)).then_inc(loaded[u], 16)
                            e.dma_start(qk_win[u][:, :, :], qk_table[:, :, bass.ds(start, W)]).then_inc(loaded[u], 16)

                        chunks(e, load)

                    @block.gpsimd
                    def _(e):
                        def gather(c):
                            u = c[1]
                            e.wait_ge(loaded[u], val(e, (c[0] + base) * 80 + 80))
                            e.sem_inc(passed, 1)
                            for j in range(J):
                                e.indirect_dma_start(
                                    out=he[u][:, j, 0:ROW], out_offset=None, in_=h_table[:, :],
                                    in_offset=bass.IndirectOffsetOnAxis(ap=src_i[u][:, j:j + 1], axis=0)).then_inc(rows_in[u], 16)

                        with e.Fori(0, TURNS) as i:
                            for u in range(SLOTS):
                                gather((i, u))

                    @block.tensor
                    def _(e):
                        def turn(c):
                            u = c[1]
                            n = count(c)
                            n0, n1 = val(e, n), val(e, n + 1)
                            e.wait_ge(he_done, n1)
                            for q in range(4):
                                again(e, turn_done[q], n0)
                                for k in range(4):
                                    j = 4 * (q % 2) + k
                                    if q < 2:
                                        mm = e.transpose(p_turn[q][:, k * P:(k + 1) * P], he[u][:, j, 1:ROW], ident[:, :])
                                    else:
                                        mm = e.transpose(p_turn[q][0:A2, k * P:(k + 1) * P], he[u][:, j, ROW:HEW], ident[:, :])
                                mm.then_inc(turn_full[q], 1)

                        def scores(c):
                            u = c[1]
                            n = count(c)
                            n0, n1 = val(e, n), val(e, n + 1)
                            e.wait_ge(loaded[u], val(e, (c[0] + base) * 80 + 80))
                            for h in range(2):
                                e.wait_ge(turn_done[h], n1)
                                e.wait_ge(turn_done[2 + h], n1)
                                again(e, masked[h], n0)
                                for k in range(4):
                                    j = 4 * h + k
                                    e.matmul(p_score[h][:, k, :], heT1[:, j * P:(j + 1) * P], qk_win[u][:, 0, :], start=True, stop=False)
                                    mm = e.matmul(p_score[h][:, k, :], heT2[:, j * P:(j + 1) * P], qk_win[u][0:A2, 1, :], start=False, stop=True)
                                mm.then_inc(score_full[h], 1)

                        def turn_top(c):
                            n = count(c)
                            e.wait_ge(top_j_done, val(e, n + 1))
                            again(e, top_done, val(e, n))
                            e.transpose(p_topT, top_j[:, :], ident[:, :]).then_inc(topT_full, 1)

                        def spread_top(c):
                            e.wait_ge(top_d_done, val(e, count(c) + 1))
                            e.matmul(p_top, ones[0:W, :], top_d[:, :], start=True, stop=True).then_inc(top_full, 1)

                        def sums(c):
                            u = c[1]
                            n = count(c)
                            e.wait_ge(prob_done, val(e, n + 1))
                            again(e, added, val(e, n))
                            for k, (a, b) in enumerate(((1, ROW), (ROW, HEW))):
                                for j in range(J):
                                    mm = e.matmul(p_sum[0:b - a, k, :], he[u][:, j, a:b], prob[:, j, :], start=(j == 0), stop=(j == J - 1))
                            mm.then_inc(sum_full, 1)

                        def step(c):
                            if not is_last(c):
                                turn(shift(c, 1))
                            turn_top(c)
                            if not is_first(c):
                                sums(shift(c, -1))
                            spread_top(c)
                            if not is_last(c):
                                scores(shift(c, 1))

                        e.wait_ge(ready, SLOTS + 1)
                        turn((0, 0))
                        scores((0, 0))
                        chunks(e, step)
                        sums((TURNS - 1, SLOTS - 1))

                    @block.scalar
                    def _(e):
                        def times(c):
                            u = c[1]
                            e.wait_ge(phase_done, val(e, count(c) + 1))
                            e.sem_inc(passed, 1)
                            e.activation(he[u][:, :, ROW:ROW + FE], feat[u][:, :, :], ACT.Copy)
                            part = he[u][:, :, ROW + FE:ROW + 2 * FE]
                            e.activation(part, part, ACT.Sin, scale=-2.0 * pi).then_inc(he_done, 1)

                        def copy_turns(c):
                            n = count(c)
                            n0, n1 = val(e, n), val(e, n + 1)
                            for h in range(2):
                                again(e, score_full[h], n0)
                                for q in (h, 2 + h):
                                    e.wait_ge(turn_full[q], n1)
                                    e.sem_inc(passed, 1)
                                    rows, to = (P, heT1) if q < 2 else (A2, heT2)
                                    e.activation(to[:, h * HALF:(h + 1) * HALF], p_turn[q][0:rows, :], ACT.Copy).then_inc(turn_done[q], 1)

                        def exps(c):
                            n = count(c)
                            n0, n1 = val(e, n), val(e, n + 1)
                            start = pick(e, number(c))
                            e.wait_ge(below_done, n1)
                            e.sem_inc(passed, 1)
                            e.activation(prob[:, :, :], prob[:, :, :], ACT.Exp).then_inc(prob_done, 1)
                            again(e, faded, n0)
                            e.sem_inc(passed, 1)
                            e.activation(fade[:, :], rise[:, :], ACT.Exp).then_inc(fade_done, 1)
                            e.activation(tops_so_far[:, bass.ds(start, W)], top[:, :], ACT.Copy).then_inc(kept_top, 1)

                        def step(c):
                            if not is_last(c):
                                copy_turns(shift(c, 1))
                                if not is_last(shift(c, 1)):
                                    times(shift(c, 2))
                            exps(c)

                        e.wait_ge(ready, SLOTS + 1)
                        times((0, 0))
                        times((0, 1))
                        copy_turns((0, 0))
                        chunks(e, step)

                    @block.vector
                    def _(e):
                        def phases(c):
                            i, u = c
                            n1 = val(e, count(c) + 1)
                            e.wait_ge(rows_in[u], val(e, (i + base) * (16 * J) + 16 * J))
                            e.tensor_tensor(gap[:, :], he[u][:, :, 0:1].rearrange("p j o -> p (j o)"), when[u][:, :], ALU.subtract).then_inc(gap_done, 1)
                            e.wait_ge(gap_done, n1)
                            e.scalar_tensor_tensor(out=dist[:, :], in0=gap[:, :], scalar=-1.0, in1=gap[:, :], op0=ALU.mult,
                                                   op1=ALU.max).then_inc(dist_done, 1)
                            e.wait_ge(dist_done, n1)
                            e.tensor_tensor(turns_w[:, :, :], dist[:, :].unsqueeze(2).broadcast_to([P, J, FE]),
                                            tw_b[:, :].unsqueeze(1).broadcast_to([P, J, FE]), ALU.mult).then_inc(turns_w_done, 1)
                            e.wait_ge(turns_w_done, n1)
                            e.tensor_tensor(turns[:, :, :], turns_w[:, :, :], tb_b[:, :].unsqueeze(1).broadcast_to([P, J, FE]),
                                            ALU.add).then_inc(turns_done, 1)
                            e.wait_ge(turns_done, n1)
                            e.tensor_scalar(turns_r[:, :, :], turns[:, :, :], ROUND, None, ALU.add).then_inc(turns_r_done, 1)
                            e.wait_ge(turns_r_done, n1)
                            e.scalar_tensor_tensor(out=he[u][:, :, ROW + FE:ROW + 2 * FE], in0=turns_r[:, :, :], scalar=-ROUND,
                                                   in1=turns[:, :, :], op0=ALU.add, op1=ALU.subtract).then_inc(phase_done, 1)

                        def others(c):
                            i, u = c
                            n = count(c)
                            n0, n1 = val(e, n), val(e, n + 1)
                            e.wait_ge(loaded[u], val(e, (i + base) * 80 + 80))
                            if is_last(c):
                                e.memset(dst_c[u][0:DUP // J, :], -1).then_inc(cut_done, 1)
                                e.wait_ge(cut_done, val(e, r + 1))
                            again(e, other_done, n0)
                            e.tensor_scalar(in_win[:, :], dst_c[u][:, :], start_b[:, bass.ds(number(c), 1)], None, ALU.subtract).then_inc(in_win_done, 1)
                            e.wait_ge(in_win_done, n1)
                            for h in range(2):
                                again(e, masked[h], n0)
                            e.tensor_tensor(other[:, :, :], in_win[:, :].unsqueeze(2).broadcast_to([P, J, W]),
                                            iota_row[:, :].unsqueeze(1).broadcast_to([P, J, W]), ALU.not_equal).then_inc(other_done, 1)

                        def masks(c):
                            n = count(c)
                            n1 = val(e, n + 1)
                            e.wait_ge(other_done, n1)
                            again(e, below_done, val(e, n))
                            for h in range(2):
                                e.wait_ge(score_full[h], n1)
                                e.scalar_tensor_tensor(out=score[:, 4 * h:4 * h + 4, :], in0=other[:, 4 * h:4 * h + 4, :], scalar=NEVER,
                                                       in1=p_score[h][:, :, :], op0=ALU.mult, op1=ALU.add).then_inc(masked[h], 1)
                            for h in range(2):
                                e.wait_ge(masked[h], n1)
                            e.tensor_reduce(top_j[:, :], score[:, :, :].rearrange("p j w -> p w j"), AX_X, ALU.max).then_inc(top_j_done, 1)

                        def tops_of_nodes(c):
                            n1 = val(e, count(c) + 1)
                            e.wait_ge(topT_full, n1)
                            e.tensor_reduce(top_n[:, :], p_topT, AX_X, ALU.max).then_inc(top_n_done, 1)
                            e.wait_ge(top_n_done, n1)
                            e.tensor_scalar(top_d[:, :], ident[0:W, 0:W], top_n[:, 0:1], None, ALU.mult).then_inc(top_d_done, 1)

                        def belows(c):
                            n = count(c)
                            n0, n1 = val(e, n), val(e, n + 1)
                            start = pick(e, number(c))
                            again(e, kept_top, n0)
                            e.wait_ge(top_full, n1)
                            before = tops_so_far[:, bass.ds(start, W)]
                            e.tensor_tensor(top[:, :], before, p_top, ALU.max).then_inc(top_done, 1)
                            e.wait_ge(top_done, n1)
                            e.tensor_tensor(rise[:, :], before, top[:, :], ALU.subtract).then_inc(rise_done, 1)
                            again(e, sum_full, n0)
                            e.tensor_tensor(prob[:, :, :], score[:, :, :], top[:, :].unsqueeze(1).broadcast_to([P, J, W]),
                                            ALU.subtract).then_inc(below_done, 1)

                        def add(c):
                            n = count(c)
                            n0, n1 = val(e, n), val(e, n + 1)
                            start = pick(e, number(c))
                            here = acc[:, :, bass.ds(start, W)]
                            again(e, added, n0)
                            e.wait_ge(fade_done, n1)
                            e.tensor_tensor(here, here, fade[:, :].unsqueeze(1).broadcast_to([P, 2, W]), ALU.mult).then_inc(faded, 1)
                            e.wait_ge(faded, n1)
                            e.wait_ge(sum_full, n1)
                            e.tensor_tensor(here, here, p_sum[:, :, :], ALU.add).then_inc(added, 1)

                        def step(c):
                            if not is_last(c):
                                others(shift(c, 1))
                            tops_of_nodes(c)
                            if not is_last(c) and not is_last(shift(c, 1)):
                                phases(shift(c, 2))
                            if not is_first(c):
                                add(shift(c, -1))
                            belows(c)
                            if not is_last(c):
                                masks(shift(c, 1))

                        e.wait_ge(ready, SLOTS + 1)
                        phases((0, 0))
                        phases((0, 1))
                        others((0, 0))
                        masks((0, 0))
                        chunks(e, step)
                        add((TURNS - 1, SLOTS - 1))

            layer0_round(0)
            spread_out = nc.values_load(span_i[0:1, 0:1], min_val=0, max_val=N)
            with nc.If(spread_out >= W):
                with nc.Fori(1, ROUNDS) as w:
                    move_windows()
                    layer0_round(w)

        layer0.close()
        x1_rows = sb("x1_rows", [P, BLOCKS, D])
        x1T = sb("x1T", [P, NP])
        bn2_b = sb("bn2_b", [P, D])
        be2_r = sb("be2_r", [1, D])
        bn1_c = sb("bn1_c", [P, 1])
        we2 = sb("we2", [P, D])
        wn1 = sb("wn1", [P, 2, D])
        wn2 = sb("wn2", [P, D])
        eps_c = sb("eps_c", [P, 1])

        with ExitStack() as ctx:
            X = sb("X2", [P, BLOCKS, D], ctx=ctx)
            hT = [sb(f"hT_{k}", [P, G], ctx=ctx) for k in range(2)]
            we1 = sb("we1", [P, 2, D], ctx=ctx)
            be1_b = sb("be1_b", [P, D], ctx=ctx)
            nought = sb("nought", [P, G], ctx=ctx)
            den = sb("den", [P, G], ctx=ctx)
            rden = sb("rden", [P, G], ctx=ctx)
            mean_v = sb("mean_v", [P, G], ctx=ctx)
            pre = sb("pre", [P, G], ctx=ctx)
            upd = sb("upd", [P, G], ctx=ctx)
            h2 = sb("h2", [P, G], ctx=ctx)
            outT = sb("outT", [P, G], ctx=ctx)
            xn = sb("xn", [P, GB, D], ctx=ctx)
            x1T_g = sb("x1T_g", [P, G], ctx=ctx)
            y = sb("y", [P, GB, D], ctx=ctx)
            stats = sb("stats", [P, GB, 6], ctx=ctx)
            mv = sb("mv", [P, GB, 2], ctx=ctx)
            std = sb("std", [P, GB], ctx=ctx)
            rstd = sb("rstd", [P, GB], ctx=ctx)
            p_rows = sb("p_rows", [P, GB, D], ctx=ctx)
            r_f = sb("r_f", [P, GB, D], ctx=ctx)
            r_g = sb("r_g", [P, GB, D], ctx=ctx)
            r_rows = sb("r_rows", [P, GB, 3, D], BF16, ctx=ctx)

            ps = [ctx.enter_context(nc.psum_tensor(f"psC{k}", [P, 512], F32)) for k in range(8)]
            p_den, p_val, p_anti, p_out, p_x1, p_pr0, p_pr1, _ = ps

            names = ("den_full val_full anti_full den_done rden_done mean_done pre_done upd_done h2_done outT_done out_full "
                     "y_done stats_done mv_done std_done rstd_done x1_done x1_full x1T_done pr_full p_done r_done hi_done "
                     "g_done mid_done lo_done kept").split()
            s = {n: sem(n) for n in names}
            loads = sem("loads_c")
            x_zero = sem("x_zero_c")
            x_in = sem("x_in_c")
            hT_in = [sem(f"hT_in{k}") for k in range(2)]
            p_out_d = sem("p_out_d")
            r_out_d = sem("r_out_d")

            block = ctx.enter_context(nc.Block())
            LOADS2 = 16 * 9

            @block.sync
            def _(e):
                e.dma_start(we1[:, :, :], We1.rearrange("(k p) d -> p k d", p=P)).then_inc(loads, 16)
                e.dma_start(wn1[:, :, :], Wn1.rearrange("(k p) d -> p k d", p=P)).then_inc(loads, 16)
                e.dma_start(we2[:, :], We2).then_inc(loads, 16)
                e.dma_start(wn2[:, :], Wn2).then_inc(loads, 16)
                e.dma_start(be1_b[:, :], be1.partition_broadcast(P)).then_inc(loads, 16)
                e.dma_start(bn2_b[:, :], bn2.partition_broadcast(P)).then_inc(loads, 16)
                e.dma_start(be2_r[:, :], row(be2)).then_inc(loads, 16)
                with nc.allow_non_contiguous_dma(reason="a bias column of 128 numbers"):
                    e.dma_start(bn1_c[:, :], col(bn1)).then_inc(loads, 16)
                e.wait_ge(x_zero, 3)
                e.dma_start(X[:, 0:FULL, :], x[0:FULL * P, :].rearrange("(b p) d -> p b d", p=P)).then_inc(loads, 16)
                e.dma_start(X[0:REST, FULL, :], x[FULL * P:N, :]).then_inc(x_in, 16)

                def load(g, k):
                    at = val(e, g * G)
                    again(e, s["h2_done"], val(e, g - 1))
                    e.sem_inc(passed, 1)
                    e.dma_start(hT[k][:, :], hT_dram[:, bass.ds(at, G)]).then_inc(hT_in[k], 16)

                def store(g):
                    at = val(e, g * G)
                    seen = val(e, g + 1)
                    e.wait_ge(s["p_done"], seen)
                    e.sem_inc(passed, 1)
                    e.dma_start(p_table[bass.ds(at, G), :].rearrange("(b p) d -> p b d", p=P), p_rows[:, :, :]).then_inc(p_out_d, 16)
                    e.wait_ge(s["lo_done"], seen)
                    e.sem_inc(passed, 1)
                    e.dma_start(r_table[bass.ds(at, G), :].rearrange("(b p) (k d) -> p b k d", p=P, k=3), r_rows[:, :, :, :]).then_inc(r_out_d, 16)

                load(0, 0)
                load(1, 1)
                store(0)
                with e.Fori(0, NG // 2 - 1) as m:
                    load(m * 2 + 2, 0)
                    store(m * 2 + 1)
                    load(m * 2 + 3, 1)
                    store(m * 2 + 2)
                load(NG - 1, 0)
                store(NG - 2)
                store(NG - 1)
                e.wait_ge(p_out_d, 16 * NG)
                e.wait_ge(r_out_d, 16 * NG)

            @block.gpsimd
            def _(e):
                e.memset(X[:, FULL:BLOCKS, :], 0.0).then_inc(x_zero, 1)
                e.memset(nought[:, :], 0.0).then_inc(x_zero, 1)

                def clear(g):
                    at = g * G if isinstance(g, int) else e.snap(g * G, min_val=0, max_val=NP - G)
                    e.wait_ge(s["val_full"], val(e, g + 1))
                    e.wait_ge(s["den_full"], val(e, g + 1))
                    e.sem_inc(passed, 1)
                    for k in range(2):
                        e.tensor_copy(acc[:, k, bass.ds(at, G)], nought[:, :])
                    blk = e.snap(g * GB, min_val=0, max_val=BLOCKS - GB)
                    e.wait_ge(s["x1_done"], val(e, g * GB + GB))
                    e.wait_ge(s["x1T_done"], val(e, g + 1))
                    e.sem_inc(passed, 1)
                    e.tensor_copy(x1_rows[:, bass.ds(blk, GB), :], xn[:, :, :])
                    e.tensor_copy(x1T[:, bass.ds(at, G)], x1T_g[:, :]).then_inc(s["kept"], 1)

                e.wait_ge(x_zero, 3)
                with e.Fori(0, NG) as g:
                    clear(g)

            def groups(e, group):
                group(0, 0, 0)
                with e.Fori(0, NG // 2) as m:
                    group(m * 2 + 1, 1, m)
                    group(m * 2 + 2, 0, m + 1)

            assert NG % 2 == 1

            @block.tensor
            def _(e):
                def first(g, k, t):
                    at = g * G if isinstance(g, int) else e.snap(g * G, min_val=0, max_val=NP - G)
                    n0, n1 = val(e, g), val(e, g + 1)
                    again(e, s["den_done"], n0)
                    e.matmul(p_den[:, :], one_row[:, :], acc[0:A2, 1, bass.ds(at, G)], start=True, stop=True).then_inc(s["den_full"], 1)
                    again(e, s["mean_done"], n0)
                    e.matmul(p_val[:, :], wvT[:, :], acc[:, 0, bass.ds(at, G)], start=True, stop=False)
                    e.matmul(p_val[:, :], we_bvT[:, :], acc[0:A2, 1, bass.ds(at, G)], start=False, stop=True).then_inc(s["val_full"], 1)
                    e.wait_ge(hT_in[k], val(e, t * 16 + 16))
                    again(e, s["pre_done"], n0)
                    e.matmul(p_anti[:, :], aT[:, :], hT[k][:, :], start=True, stop=True).then_inc(s["anti_full"], 1)

                def second(g, k):
                    n0, n1 = val(e, g), val(e, g + 1)
                    e.wait_ge(s["outT_done"], n1)
                    again(e, s["y_done"], n0)
                    for b in range(GB):
                        mm = e.transpose(p_out[:, b * P:(b + 1) * P], outT[:, b * P:(b + 1) * P], ident[:, :])
                    mm.then_inc(s["out_full"], 1)

                def third(g, k):
                    n0, n1 = val(e, g), val(e, g + 1)
                    e.wait_ge(s["x1_done"], val(e, g * GB + GB))
                    again(e, s["x1T_done"], n0)
                    for b in range(GB):
                        mm = e.transpose(p_x1[:, b * P:(b + 1) * P], xn[:, b, :], ident[:, :])
                    mm.then_inc(s["x1_full"], 1)
                    e.wait_ge(s["x1T_done"], n1)
                    again(e, s["p_done"], n0)
                    again(e, s["r_done"], n0)
                    for b in range(GB):
                        mm = e.matmul((p_pr0, p_pr1)[b // 2][:, (b % 2) * 256:(b % 2) * 256 + 256], x1T_g[:, b * P:(b + 1) * P],
                                      we1[:, :, :].rearrange("p k d -> p (k d)"), start=True, stop=True)
                    mm.then_inc(s["pr_full"], 1)

                def group(g, k, t):
                    first(g, k, t)
                    second(g, k)
                    third(g, k)

                e.wait_ge(loads, LOADS2)
                groups(e, group)

            @block.scalar
            def _(e):
                def group(g, k, t):
                    n0, n1 = val(e, g), val(e, g + 1)
                    e.wait_ge(s["pre_done"], n1)
                    again(e, s["h2_done"], n0)
                    e.sem_inc(passed, 1)
                    e.activation(upd[:, :], pre[:, :], ACT.Tanh, bias=bac_c[:, 0:1]).then_inc(s["upd_done"], 1)
                    e.wait_ge(s["h2_done"], n1)
                    again(e, s["out_full"], n0)
                    e.sem_inc(passed, 1)
                    e.activation(outT[:, :], h2[:, :], ACT.Tanh).then_inc(s["outT_done"], 1)
                    e.wait_ge(s["mv_done"], val(e, g * GB + GB))
                    again(e, s["rstd_done"], n0)
                    e.sem_inc(passed, 1)
                    e.activation(std[:, :], mv[:, :, 1:2].rearrange("p b o -> p (b o)"), ACT.Sqrt, bias=eps_c[:, 0:1]).then_inc(s["std_done"], 1)
                    e.wait_ge(s["x1_full"], n1)
                    again(e, s["kept"], n0)
                    again(e, s["pr_full"], n0)
                    e.sem_inc(passed, 1)
                    e.activation(x1T_g[:, :], p_x1[:, :], ACT.Copy).then_inc(s["x1T_done"], 1)
                    e.wait_ge(s["pr_full"], n1)
                    again(e, p_out_d, val(e, g * 16))
                    e.sem_inc(passed, 1)
                    e.activation(p_rows[:, 0:2, :], p_pr0[:, :].rearrange("p (b k d) -> p b k d", k=2, d=D)[:, :, 0, :], ACT.Copy)
                    e.activation(p_rows[:, 2:4, :], p_pr1[:, :].rearrange("p (b k d) -> p b k d", k=2, d=D)[:, :, 0, :], ACT.Copy).then_inc(s["p_done"], 1)

                e.wait_ge(x_zero, 3)
                groups(e, group)

            @block.vector
            def _(e):
                e.memset(eps_c[:, :], EPS).then_inc(x_zero, 1)

                def group(g, k, t):
                    n0, n1 = val(e, g), val(e, g + 1)
                    at = g * G if isinstance(g, int) else e.snap(g * G, min_val=0, max_val=NP - G)
                    blk = g * GB if isinstance(g, int) else e.snap(g * GB, min_val=0, max_val=BLOCKS - GB)
                    e.wait_ge(s["den_full"], n1)
                    e.tensor_scalar(den[:, :], p_den[:, :], 1.0e-16, None, ALU.add).then_inc(s["den_done"], 1)
                    e.wait_ge(s["den_done"], n1)
                    e.reciprocal(rden[:, :], den[:, :]).then_inc(s["rden_done"], 1)
                    e.wait_ge(s["rden_done"], n1)
                    e.wait_ge(s["val_full"], n1)
                    e.tensor_tensor(mean_v[:, :], p_val[:, :], rden[:, :], ALU.mult).then_inc(s["mean_done"], 1)
                    e.wait_ge(s["mean_done"], n1)
                    e.wait_ge(s["anti_full"], n1)
                    e.tensor_tensor(pre[:, :], p_anti[:, :], mean_v[:, :], ALU.add).then_inc(s["pre_done"], 1)
                    e.wait_ge(s["upd_done"], n1)
                    again(e, s["outT_done"], n0)
                    e.tensor_tensor(h2[:, :], hT[k][:, :], upd[:, :], ALU.add).then_inc(s["h2_done"], 1)
                    e.wait_ge(s["out_full"], n1)
                    e.tensor_tensor(y[:, :, :], X[:, bass.ds(blk, GB), :], p_out[:, :].rearrange("p (b d) -> p b d", d=D), ALU.add).then_inc(s["y_done"], 1)
                    e.wait_ge(s["y_done"], n1)
                    for b in range(GB):
                        e.bn_stats(stats[:, b, :], y[:, b, :]).then_inc(s["stats_done"], 1)
                    again(e, s["std_done"], n0)
                    e.wait_ge(s["stats_done"], val(e, g * GB + GB))
                    e.sem_inc(passed, 1)
                    for b in range(GB):
                        e.bn_aggr(mv[:, b, :], stats[:, b, :]).then_inc(s["mv_done"], 1)
                    e.wait_ge(s["std_done"], n1)
                    e.reciprocal(rstd[:, :], std[:, :]).then_inc(s["rstd_done"], 1)
                    e.wait_ge(s["rstd_done"], n1)
                    again(e, s["kept"], n0)
                    again(e, s["x1_full"], n0)
                    for b in range(GB):
                        e.tensor_scalar(xn[:, b, :], y[:, b, :], mv[:, b, 0:1],
                                        rstd[:, b:b + 1], ALU.subtract, ALU.mult).then_inc(s["x1_done"], 1)
                    e.wait_ge(s["p_done"], n1)
                    for h, p in enumerate((p_pr0, p_pr1)):
                        op = e.tensor_tensor(r_f[:, 2 * h:2 * h + 2, :], p[:, :].rearrange("p (b k d) -> p b k d", k=2, d=D)[:, :, 1, :],
                                             be1_b[:, :].unsqueeze(1).broadcast_to([P, 2, D]), ALU.add)
                    op.then_inc(s["r_done"], 1)
                    e.wait_ge(s["r_done"], n1)
                    again(e, r_out_d, val(e, g * 16))
                    e.tensor_copy(r_rows[:, :, 0, :], r_f[:, :, :]).then_inc(s["hi_done"], 1)
                    e.wait_ge(s["hi_done"], n1)
                    e.tensor_tensor(r_g[:, :, :], r_f[:, :, :], r_rows[:, :, 0, :], ALU.subtract).then_inc(s["g_done"], 1)
                    e.wait_ge(s["g_done"], n1)
                    e.tensor_copy(r_rows[:, :, 1, :], r_g[:, :, :]).then_inc(s["mid_done"], 1)
                    e.wait_ge(s["mid_done"], n1)
                    e.tensor_tensor(r_rows[:, :, 2, :], r_g[:, :, :], r_rows[:, :, 1, :], ALU.subtract).then_inc(s["lo_done"], 1)

                e.wait_ge(loads, LOADS2)
                e.wait_ge(x_in, 16)
                groups(e, group)

        with ExitStack() as ctx:
            msg = [sb(f"msg{k}", [P, J, D], ctx=ctx) for k in range(SLOTS)]
            src_i = [sb(f"src1_{k}", [P, J], I32, ctx=ctx) for k in range(SLOTS)]
            dst_c = [sb(f"dst1_{k}", [P, J], I32, ctx=ctx) for k in range(SLOTS)]
            r_win = [sb(f"r_win{k}", [W, 3, D], BF16, ctx=ctx) for k in range(SLOTS)]
            hot = [sb(f"hot{k}", [P, J, W], ctx=ctx) for k in range(SLOTS)]
            in_win = sb("in_win1", [P, J], ctx=ctx)
            hotT = sb("hotT", [W, CH], BF16, ctx=ctx)
            p_hot = [ctx.enter_context(nc.psum_tensor(f"p_hot{k}", [P, 512], F32)) for k in range(2)]
            p_edge = [ctx.enter_context(nc.psum_tensor(f"p_edge{k}", [P, 4, D], F32)) for k in range(2)]
            p_sum = ctx.enter_context(nc.psum_tensor("p_sum1", [P, 2, W], F32))

            loaded = [sem(f"loaded1_{k}") for k in range(SLOTS)]
            rows_in = [sem(f"rows1_in{k}") for k in range(SLOTS)]
            in_win_done = sem("in_win_done")
            hot_done = sem("hot_done")
            hot_full = [sem(f"hot_full{h}") for h in range(2)]
            hotT_done = [sem(f"hotT_done{h}") for h in range(2)]
            edge_full = [sem(f"edge_full{h}") for h in range(2)]
            both_done = [sem(f"both_done{h}") for h in range(2)]
            relu_done = sem("relu_done")
            sum_full = sem("sum1_full")
            added = sem("added1")
            added2 = sem("added2")
            cut_done = sem("cut1_done")

            def layer1_round(r):
                base = r * TURNS
                with ExitStack() as c2:
                    block = c2.enter_context(nc.Block())

                    def count(c):
                        return (c[0] + base) * SLOTS + c[1]

                    @block.sync
                    def _(e):
                        def load(c):
                            u = c[1]
                            at = LAST if is_last(c) else val(e, number(c) * CH)
                            start = pick(e, number(c))
                            again(e, sum_full, val(e, count(c) - SLOTS + 1))
                            e.sem_inc(passed, 1)
                            e.dma_start(src_i[u][:, :], src[bass.ds(at, CH)].rearrange("(p j) -> p j", j=J)).then_inc(loaded[u], 16)
                            e.dma_start(dst_c[u][:, :], dst[bass.ds(at, CH)].rearrange("(p j) -> p j", j=J)).then_inc(loaded[u], 16)
                            e.dma_start(r_win[u][:, :, :], r_table[bass.ds(start, W), :].rearrange("p (k d) -> p k d", k=3)).then_inc(loaded[u], 16)

                        chunks(e, load)

                    @block.gpsimd
                    def _(e):
                        def gather(c):
                            u = c[1]
                            e.wait_ge(loaded[u], val(e, (c[0] + base) * 48 + 48))
                            e.sem_inc(passed, 1)
                            for j in range(J):
                                e.indirect_dma_start(
                                    out=msg[u][:, j, :], out_offset=None, in_=p_table[:, :],
                                    in_offset=bass.IndirectOffsetOnAxis(ap=src_i[u][:, j:j + 1], axis=0)).then_inc(rows_in[u], 16)

                        with e.Fori(0, TURNS) as i:
                            for u in range(SLOTS):
                                gather((i, u))

                    @block.tensor
                    def _(e):
                        def turn_hot(c):
                            u = c[1]
                            n = count(c)
                            n0, n1 = val(e, n), val(e, n + 1)
                            e.wait_ge(hot_done, n1)
                            for h in range(2):
                                again(e, hotT_done[h], n0)
                                for k in range(4):
                                    mm = e.transpose(p_hot[h][0:W, k * P:(k + 1) * P], hot[u][:, 4 * h + k, :], ident[:, :])
                                mm.then_inc(hot_full[h], 1)

                        def edges(c):
                            u = c[1]
                            n = count(c)
                            n0, n1 = val(e, n), val(e, n + 1)
                            for h in range(2):
                                e.wait_ge(hotT_done[h], n1)
                                again(e, both_done[h], n0)
                                for j in range(4 * h, 4 * h + 4):
                                    for k in range(3):
                                        mm = e.matmul(p_edge[h][:, j % 4, :], hotT[:, j * P:(j + 1) * P], r_win[u][:, k, :], start=(k == 0), stop=(k == 2))
                                mm.then_inc(edge_full[h], 1)

                        def sums(c):
                            u = c[1]
                            n = count(c)
                            n0, n1 = val(e, n), val(e, n + 1)
                            e.wait_ge(relu_done, n1)
                            again(e, added, n0)
                            again(e, added2, n0)
                            for j in range(J):
                                e.matmul(p_sum[:, 0, :], msg[u][:, j, :], hot[u][:, j, :], start=(j == 0), stop=(j == J - 1))
                            for j in range(J):
                                mm = e.matmul(p_sum[0:1, 1, :], ones[:, 0:1], hot[u][:, j, :], start=(j == 0), stop=(j == J - 1))
                            mm.then_inc(sum_full, 1)

                        def step(c):
                            if not is_last(c):
                                turn_hot(shift(c, 1))
                            if not is_first(c):
                                sums(shift(c, -1))
                            if not is_last(c):
                                edges(shift(c, 1))

                        turn_hot((0, 0))
                        edges((0, 0))
                        chunks(e, step)
                        sums((TURNS - 1, SLOTS - 1))

                    @block.scalar
                    def _(e):
                        def copy_hot(c):
                            n = count(c)
                            n0, n1 = val(e, n), val(e, n + 1)
                            for h in range(2):
                                again(e, edge_full[h], n0)
                                e.wait_ge(hot_full[h], n1)
                                e.sem_inc(passed, 1)
                                e.activation(hotT[:, h * HALF:(h + 1) * HALF], p_hot[h][0:W, :], ACT.Copy).then_inc(hotT_done[h], 1)

                        def relus(c):
                            u = c[1]
                            e.wait_ge(both_done[1], val(e, count(c) + 1))
                            e.sem_inc(passed, 1)
                            e.activation(msg[u][:, :, :], msg[u][:, :, :], ACT.Relu).then_inc(relu_done, 1)

                        def step(c):
                            if not is_last(c):
                                copy_hot(shift(c, 1))
                            relus(c)

                        copy_hot((0, 0))
                        chunks(e, step)

                    @block.vector
                    def _(e):
                        def hots(c):
                            i, u = c
                            n = count(c)
                            n0, n1 = val(e, n), val(e, n + 1)
                            e.wait_ge(loaded[u], val(e, (i + base) * 48 + 48))
                            again(e, hot_done, n0)
                            if is_last(c):
                                e.memset(dst_c[u][0:DUP // J, :], -1).then_inc(cut_done, 1)
                                e.wait_ge(cut_done, val(e, r + 1))
                            e.tensor_scalar(in_win[:, :], dst_c[u][:, :], start_b[:, bass.ds(number(c), 1)], None, ALU.subtract).then_inc(in_win_done, 1)
                            e.wait_ge(in_win_done, n1)
                            e.tensor_tensor(hot[u][:, :, :], in_win[:, :].unsqueeze(2).broadcast_to([P, J, W]),
                                            iota_row[:, :].unsqueeze(1).broadcast_to([P, J, W]), ALU.is_equal).then_inc(hot_done, 1)

                        def boths(c):
                            i, u = c
                            n1 = val(e, count(c) + 1)
                            e.wait_ge(rows_in[u], val(e, (i + base) * (16 * J) + 16 * J))
                            for h in range(2):
                                e.wait_ge(edge_full[h], n1)
                                part = msg[u][:, 4 * h:4 * h + 4, :]
                                e.tensor_tensor(part, part, p_edge[h][:, :, :], ALU.add).then_inc(both_done[h], 1)

                        def add(c):
                            n = count(c)
                            n0, n1 = val(e, n), val(e, n + 1)
                            start = pick(e, number(c))
                            again(e, added, n0)
                            again(e, added2, n0)
                            e.wait_ge(sum_full, n1)
                            here = acc[:, 0, bass.ds(start, W)]
                            e.tensor_tensor(here, here, p_sum[:, 0, :], ALU.add).then_inc(added, 1)
                            here = acc[0:1, 1, bass.ds(start, W)]
                            e.tensor_tensor(here, here, p_sum[0:1, 1, :], ALU.add).then_inc(added2, 1)

                        def step(c):
                            if not is_last(c):
                                hots(shift(c, 1))
                            boths(c)
                            if not is_first(c):
                                add(shift(c, -1))

                        hots((0, 0))
                        chunks(e, step)
                        add((TURNS - 1, SLOTS - 1))

            with ExitStack() as c2:
                back_in = sem("back_in")
                block = c2.enter_context(nc.Block())

                @block.sync
                def _(e):
                    e.dma_start(start_b[:, :], start_dram[0, :].partition_broadcast(P)).then_inc(back_in, 16)

                @block.vector
                def _(e):
                    e.wait_ge(back_in, 16)
                    e.tensor_copy(start_i[:, :], start_b[0:1, :])

            layer1_round(0)
            spread_out = nc.values_load(span_i[0:1, 0:1], min_val=0, max_val=N)
            with nc.If(spread_out >= W):
                with nc.Fori(1, ROUNDS) as w:
                    move_windows()
                    layer1_round(w)

        with ExitStack() as ctx:
            agg = sb("agg", [P, G], ctx=ctx)
            hid = sb("hid", [P, G], ctx=ctx)
            twice = sb("twice", [P, GB, D], ctx=ctx)
            y = sb("y1", [P, GB, D], ctx=ctx)
            stats = sb("stats1", [P, GB, 6], ctx=ctx)
            mv = sb("mv1", [P, GB, 2], ctx=ctx)
            std = sb("std1", [P, GB], ctx=ctx)
            rstd = sb("rstd1", [P, GB], ctx=ctx)
            o_rows = [sb(f"o_rows{k}", [P, GB, D], ctx=ctx) for k in range(2)]
            p_agg, p_hid, p_mesh = (ctx.enter_context(nc.psum_tensor(f"psE{k}", [P, 512], F32)) for k in range(3))

            names = "agg_full agg_done hid_full hid_done mesh_full twice_done y_done stats_done mv_done std_done rstd_done o_done".split()
            s = {n: sem(n + "1") for n in names}
            o_out = [sem(f"o_out{k}") for k in range(2)]
            block = ctx.enter_context(nc.Block())

            @block.sync
            def _(e):
                def store(g, k, t):
                    at = val(e, g * G)
                    e.wait_ge(s["o_done"], val(e, g * GB + GB))
                    e.sem_inc(passed, 1)
                    e.dma_start(out[bass.ds(at, G), :].rearrange("(b p) d -> p b d", p=P), o_rows[k][:, :, :]).then_inc(o_out[k], 16)

                with e.Fori(0, NG // 2) as m:
                    store(m * 2, 0, m)
                    store(m * 2 + 1, 1, m)
                e.wait_ge(s["o_done"], NG * GB)
                e.dma_start(out[FULL * P:N, :], o_rows[0][0:REST, 0, :]).then_inc(o_out[0], 16)
                e.wait_ge(o_out[0], 16 * (NG // 2 + 1))
                e.wait_ge(o_out[1], 16 * (NG // 2))

            @block.tensor
            def _(e):
                def group(g, k, t):
                    at = g * G if isinstance(g, int) else e.snap(g * G, min_val=0, max_val=NP - G)
                    n0, n1 = val(e, g), val(e, g + 1)
                    again(e, s["agg_done"], n0)
                    e.matmul(p_agg[:, :], we2[:, :], acc[:, 0, bass.ds(at, G)], start=True, stop=False)
                    e.matmul(p_agg[:, :], be2_r[:, :], acc[0:1, 1, bass.ds(at, G)], start=False, stop=True).then_inc(s["agg_full"], 1)
                    e.wait_ge(s["agg_done"], n1)
                    again(e, s["hid_done"], n0)
                    e.matmul(p_hid[:, :], wn1[:, 0, :], x1T[:, bass.ds(at, G)], start=True, stop=False)
                    e.matmul(p_hid[:, :], wn1[:, 1, :], agg[:, :], start=False, stop=True).then_inc(s["hid_full"], 1)
                    e.wait_ge(s["hid_done"], n1)
                    again(e, s["y_done"], n0)
                    for b in range(GB):
                        mm = e.matmul(p_mesh[:, b * D:(b + 1) * D], hid[:, b * P:(b + 1) * P], wn2[:, :], start=True, stop=True)
                    mm.then_inc(s["mesh_full"], 1)

                groups(e, group)

            @block.scalar
            def _(e):
                def group(g, k, t):
                    n0, n1 = val(e, g), val(e, g + 1)
                    e.wait_ge(s["agg_full"], n1)
                    again(e, s["hid_full"], n0)
                    e.sem_inc(passed, 1)
                    e.activation(agg[:, :], p_agg[:, :], ACT.Copy).then_inc(s["agg_done"], 1)
                    e.wait_ge(s["hid_full"], n1)
                    again(e, s["mesh_full"], n0)
                    e.sem_inc(passed, 1)
                    e.activation(hid[:, :], p_hid[:, :], ACT.Relu, bias=bn1_c[:, 0:1]).then_inc(s["hid_done"], 1)
                    e.wait_ge(s["mv_done"], val(e, g * GB + GB))
                    again(e, s["rstd_done"], n0)
                    e.sem_inc(passed, 1)
                    e.activation(std[:, :], mv[:, :, 1:2].rearrange("p b o -> p (b o)"), ACT.Sqrt, bias=eps_c[:, 0:1]).then_inc(s["std_done"], 1)

                groups(e, group)

            @block.vector
            def _(e):
                def group(g, k, t):
                    n0, n1 = val(e, g), val(e, g + 1)
                    blk = g * GB if isinstance(g, int) else e.snap(g * GB, min_val=0, max_val=BLOCKS - GB)
                    e.scalar_tensor_tensor(out=twice[:, :, :], in0=x1_rows[:, bass.ds(blk, GB), :], scalar=2.0,
                                           in1=bn2_b[:, :].unsqueeze(1).broadcast_to([P, GB, D]), op0=ALU.mult,
                                           op1=ALU.add).then_inc(s["twice_done"], 1)
                    e.wait_ge(s["twice_done"], n1)
                    e.wait_ge(s["mesh_full"], n1)
                    e.tensor_tensor(y[:, :, :], twice[:, :, :], p_mesh[:, :].rearrange("p (b d) -> p b d", d=D), ALU.add).then_inc(s["y_done"], 1)
                    e.wait_ge(s["y_done"], n1)
                    for b in range(GB):
                        e.bn_stats(stats[:, b, :], y[:, b, :]).then_inc(s["stats_done"], 1)
                    again(e, s["std_done"], n0)
                    e.wait_ge(s["stats_done"], val(e, g * GB + GB))
                    e.sem_inc(passed, 1)
                    for b in range(GB):
                        e.bn_aggr(mv[:, b, :], stats[:, b, :]).then_inc(s["mv_done"], 1)
                    e.wait_ge(s["std_done"], n1)
                    e.reciprocal(rstd[:, :], std[:, :]).then_inc(s["rstd_done"], 1)
                    e.wait_ge(s["rstd_done"], n1)
                    again(e, o_out[k], val(e, t * 16))
                    for b in range(GB):
                        e.tensor_scalar(o_rows[k][:, b, :], y[:, b, :], mv[:, b, 0:1], rstd[:, b:b + 1], ALU.subtract,
                                        ALU.mult).then_inc(s["o_done"], 1)

                groups(e, group)


_INS = ["x", "src", "dst", "edge_attr_32", "edge_weight", "node_vec", "L0_gnn_time_w", "L0_gnn_time_b", "L0_gnn_Wx",
        "L0_gnn_bx", "L0_gnn_Wq", "L0_gnn_bq", "L0_gnn_Wk", "L0_gnn_bk", "L0_gnn_Wv", "L0_gnn_bv", "L0_gnn_We",
        "L0_gnn_W_ac", "L0_gnn_b_ac", "L1_gnn_We1", "L1_gnn_be1", "L1_gnn_We2", "L1_gnn_be2", "L1_gnn_Wn1",
        "L1_gnn_bn1", "L1_gnn_Wn2", "L1_gnn_bn2"]
_OUTS = [((6250, 128), "float32")]


def kernel(**inputs):
    import numpy as _np
    import concourse.bacc as _bacc
    from concourse import mybir as _mybir
    from concourse.bass_utils import run_bass_kernel_spmd as _run

    nc = _bacc.Bacc("TRN2", target_bir_lowering=False, num_devices=1)
    arrays, args = {}, []
    for name in _INS:
        a = _np.ascontiguousarray(inputs[name])
        arrays[f"in_{name}_dram"] = a
        args.append(nc.dram_tensor(f"in_{name}_dram", a.shape, _mybir.dt.from_np(a.dtype), kind="ExternalInput").ap())
    for i, (shape, dtype) in enumerate(_OUTS):
        dt = _mybir.dt.from_np(_np.dtype(dtype))
        args.append(nc.dram_tensor(f"out_{i}_dram", shape, dt, kind="ExternalOutput").ap())
    gnn_kernel(nc, *args)
    r = _run(nc, [arrays], core_ids=[0])
    return r.results[0]["out_0_dram"]
```

```python
from contextlib import ExitStack
from math import pi

import concourse.bass as bass
from concourse import mybir

F32 = mybir.dt.float32
BF16 = mybir.dt.bfloat16
I32 = mybir.dt.int32
ALU = mybir.AluOpType
ACT = mybir.ActivationFunctionType
AX_X = mybir.AxisListType.X

P = 128
D = 128
FE = 32
J = 8
CH = P * J
HALF = CH // 2
W = 80
SLOTS = 7
G = 512
GB = G // P
ROW = 1 + D
A2 = 2 * FE + 1
NEVER = -1.0e30
LOW = -1.0e20
ROUND = 1.5 * 2.0**23
EPS = 1.0e-5
GAMMA = 0.1


def gnn_kernel(nc, x, src, dst, edge_attr, edge_weight, node_vec, time_w, time_b, Wx, bx, Wq, bq, Wk, bk,
               Wv, bv, We, W_ac, b_ac, We1, be1, We2, be2, Wn1, bn1, Wn2, bn2, out):
    N = x.shape[0]
    E = src.shape[0]
    NCH = -(-E // CH)
    LAST = E - CH
    DUP = NCH * CH - E
    SKIP = DUP // P
    TURNS = NCH // SLOTS
    NG = -(-(N + W) // G)
    NP = NG * G
    BLOCKS = NP // P
    FULL, REST = N // P, N % P
    ROUNDS = -(-N // W)
    SCALE = float(D) ** -0.5
    assert NCH % SLOTS == 0 and TURNS > 1 and REST and FULL // GB == NG - 1

    h_table = nc.dram_tensor("h_table", [NP, ROW], F32)
    qk_table = nc.dram_tensor("qk_table", [P, 2, NP], F32)
    hT_dram = nc.dram_tensor("hT_dram", [P, NP], F32)
    p_table = nc.dram_tensor("p_table", [NP, D], F32)
    r_table = nc.dram_tensor("r_table", [NP, D], F32)
    den_dram = nc.dram_tensor("den_dram", [2, NP], F32)
    start_dram = nc.dram_tensor("start_dram", [2, NCH], F32)

    with ExitStack() as whole:
        def sb(name, shape, dt=F32, ctx=whole):
            return ctx.enter_context(nc.sbuf_tensor(name, shape, dt))

        def sem(name, ctx=whole):
            return ctx.enter_context(nc.semaphore(name))

        def val(eng, v):
            return v if isinstance(v, int) else eng.snap(v)

        def again(eng, s, v):
            if not isinstance(v, int) or v > 0:
                eng.wait_ge(s, v)

        ident = sb("ident", [P, P])
        ones = sb("ones", [P, P])
        iota_row = sb("iota_row", [P, W])
        iota_b = sb("iota_b", [P, W], BF16)
        start_i = sb("start_i", [1, NCH], I32)
        start_b = sb("start_b", [P, NCH])
        span_i = sb("span_i", [1, 1], I32)
        wvT = sb("wvT", [P, D])
        we_bvT = sb("we_bvT", [A2, D])
        aT = sb("aT", [P, D])
        bac_c = sb("bac_c", [P, 1])
        tw_b = sb("tw_b", [P, FE])
        tb_b = sb("tb_b", [P, FE])
        acc = sb("acc", [P, 2, NP])
        eps_c = sb("eps_c", [P, 1])

        passed = sem("passed")

        early = whole.enter_context(ExitStack())
        early_sems = []

        def early_sem(name):
            early_sems.append(sem(name, early))
            return early_sems[-1]

        def col(v):
            return v.rearrange("(p o) -> p o", o=1)

        def row(v):
            return v.rearrange("(o d) -> o d", o=1)

        def place(e, g, unit):
            return g * unit if isinstance(g, int) else e.snap(g * unit, min_val=0, max_val=(NG - 1) * unit)

        PEEL = 5
        assert (NG - PEEL) % 2 == 0 and NG > PEEL + 2

        def pipelined(e, *stages):
            most = max(lag for lag, _ in stages)
            assert most + 2 <= PEEL

            def apart(t):
                for lag, stage in stages:
                    if 0 <= t - lag < NG:
                        stage(t - lag, (t - lag) % 2)

            for t in range(PEEL):
                apart(t)
            with e.Fori(0, (NG - PEEL) // 2 - 1) as m:
                for t in (PEEL, PEEL + 1):
                    for lag, stage in stages:
                        stage(m * 2 + (t - lag), (t - lag) % 2)
            for t in range(NG - 2, NG + most):
                apart(t)

        hT = sb("hT", [P, NP])
        layer0 = whole.enter_context(ExitStack())
        tops_so_far = sb("tops_so_far", [P, NP], ctx=layer0)
        wqT = sb("wqT", [P, D], ctx=layer0)
        wk = sb("wk", [P, D], ctx=layer0)
        we_bk = sb("we_bk", [P, A2], ctx=layer0)
        bq_c = sb("bq_c", [P, 1], ctx=layer0)

        with ExitStack() as ctx:
            xg = [sb(f"xg{k}", [P, GB, D], ctx=ctx) for k in range(2)]
            x_tail = sb("x_tail", [P, GB, D], ctx=ctx)
            wx = sb("wx", [P, D], ctx=ctx)
            wq = sb("wq", [P, D], ctx=ctx)
            wv = sb("wv", [P, D], ctx=ctx)
            wac = sb("wac", [P, D], ctx=ctx)
            wxT = sb("wxT", [P, D], ctx=ctx)
            bx_c = sb("bx_c", [P, 1], ctx=ctx)
            bx_b = sb("bx_b", [P, D], ctx=ctx)
            tw_raw = sb("tw_raw", [P, FE], ctx=ctx)
            tb_raw = sb("tb_raw", [P, FE], ctx=ctx)
            nv_rows = sb("nv_rows", [BLOCKS, P], ctx=ctx)
            nv_cols = sb("nv_cols", [P, BLOCKS], ctx=ctx)
            dT = sb("dT", [P, D], ctx=ctx)
            xT = [sb(f"xT{k}", [P, G], ctx=ctx) for k in range(2)]
            h_rows = [sb(f"h_rows{k}", [P, GB, ROW], ctx=ctx) for k in range(2)]
            CP = (NCH - 1) // 3
            dst_a = sb("dst_a", [CP, 3, CH], I32, ctx=ctx)
            dst_z = sb("dst_z", [1, CH], I32, ctx=ctx)
            ends_a = sb("ends_a", [CP, 2, 3], ctx=ctx)
            ends_z = sb("ends_z", [1, 2], ctx=ctx)
            ends_r = sb("ends_r", [1, 2, NCH], ctx=ctx)
            span_r = sb("span_r", [1, NCH], ctx=ctx)
            span_m = sb("span_m", [1, 1], ctx=ctx)

            ps = [ctx.enter_context(nc.psum_tensor(f"psA{k}", [P, 512], F32)) for k in range(8)]
            p_xT, p_hT, p_rows, p_w, p_w2 = ps[0:2], ps[2:4], ps[4:6], ps[6], ps[7]

            first_in = early_sem("first_in")
            x_in = [early_sem(f"x_in{k}") for k in range(2)]
            tail_in = early_sem("tail_in")
            loads = early_sem("loads")
            x_zero = early_sem("x_zero")
            dst_in = early_sem("dst_in")
            ends_done = early_sem("ends_done")
            ends_out = early_sem("ends_out")
            ends_in = early_sem("ends_in")
            consts = early_sem("consts")
            w_turned = early_sem("w_turned")
            w_copied = early_sem("w_copied")
            step = early_sem("step")
            xT_full = early_sem("xT_full")
            xT_done = early_sem("xT_done")
            hT_full = early_sem("hT_full")
            hT_done = early_sem("hT_done")
            rows_full = early_sem("rows_full")
            rows_done = early_sem("rows_done")
            h_out = [early_sem(f"h_out{k}") for k in range(2)]

            steps = ctx.enter_context(ExitStack())
            block = steps.enter_context(nc.Block())

            FIRST = 16 * 5
            LOADS = 16 * 11

            @block.sync
            def _(e):
                e.dma_start(wx[:, :], Wx).then_inc(first_in, 16)

                def load(g, k):
                    if isinstance(g, int) and g == NG - 1:
                        return
                    at = val(e, g * G)
                    again(e, xT_full, val(e, g - 1))
                    e.sem_inc(passed, 1)
                    e.dma_start(xg[k][:, :, :], x[bass.ds(at, G), :].rearrange("(b p) d -> p b d", p=P)).then_inc(x_in[k], 16)

                load(0, 0)
                load(1, 1)
                e.wait_ge(x_zero, 2)
                e.dma_start(nv_rows[0:FULL, :], node_vec[0:FULL * P].rearrange("(b p) -> b p", p=P)).then_inc(first_in, 16)
                e.dma_start(nv_rows[FULL:FULL + 1, 0:REST], row(node_vec[FULL * P:N])).then_inc(first_in, 16)
                with nc.allow_non_contiguous_dma(reason="a bias column of 128 numbers"):
                    e.dma_start(bx_c[:, :], col(bx)).then_inc(first_in, 16)
                e.dma_start(bx_b[:, :], bx.partition_broadcast(P)).then_inc(first_in, 16)
                e.dma_start(x_tail[0:REST, 0, :], x[FULL * P:N, :]).then_inc(tail_in, 16)
                pipelined(e, (0, lambda g, k: None if isinstance(g, int) and g < 2 else load(g, k)))
                e.wait_ge(ends_done, 4)
                for k in range(2):
                    e.dma_start(start_dram[k, 0:NCH - 1].rearrange("(p k) -> p k", k=3), ends_a[:, k, :]).then_inc(ends_out, 16)
                    e.dma_start(start_dram[k:k + 1, NCH - 1:NCH], ends_z[:, k:k + 1]).then_inc(ends_out, 16)
                e.wait_ge(ends_out, 64)
                e.dma_start(ends_r[:, :, :], start_dram[:, :].rearrange("(o k) c -> o k c", o=1)).then_inc(ends_in, 16)
                e.dma_start(start_b[:, :], start_dram[0, :].partition_broadcast(P)).then_inc(ends_in, 16)


            @block.gpsimd
            def _(e):
                e.memset(nv_rows[:, :], 0.0).then_inc(x_zero, 1)
                e.memset(x_tail[:, :, :], 0.0).then_inc(x_zero, 1)
                e.memset(ident[:, :], 0.0).then_inc(step, 1)
                e.memset(ones[:, :], 1.0).then_inc(consts, 1)
                e.wait_ge(step, 1)
                e.affine_select(out=ident[:, :], in_=ident[:, :], compare_op=ALU.not_equal, fill=1.0, base=0,
                                pattern=[[-1, P]], channel_multiplier=1).then_inc(consts, 1)
                e.iota(iota_row[:, :], pattern=[[1, W]], base=0, channel_multiplier=0,
                       allow_small_or_imprecise_dtypes=True).then_inc(consts, 1)
                e.memset(acc[:, :, :], 0.0).then_inc(consts, 1)
                e.memset(tops_so_far[:, :], LOW).then_inc(consts, 1)

            @block.tensor
            def _(e):
                e.wait_ge(consts, 3)
                e.wait_ge(first_in, FIRST)
                e.transpose(p_w[:, 0:P], wx[:, :], ident[:, :])
                e.transpose(p_w[:, P:P + BLOCKS], nv_rows[:, :], ident[0:BLOCKS, 0:BLOCKS]).then_inc(w_turned, 1)

                def turn_x(g, k):
                    if isinstance(g, int) and g == NG - 1:
                        rows = x_tail
                        e.wait_ge(tail_in, 16)
                    else:
                        rows = xg[k]
                        e.wait_ge(x_in[k], val(e, (g - k) * 8 + 16))
                    again(e, xT_done, val(e, g - 1))
                    for b in range(GB):
                        mm = e.transpose(p_xT[k][:, b * P:(b + 1) * P], rows[:, b, :], ident[:, :])
                    mm.then_inc(xT_full, 1)

                def make_h(g, k):
                    if isinstance(g, int) and g == 0:
                        e.wait_ge(w_copied, 2)
                    before, seen = val(e, g - 1), val(e, g + 1)
                    e.wait_ge(xT_done, seen)
                    again(e, hT_done, before)
                    e.matmul(p_hT[k][:, :], wxT[:, :], xT[k][:, :], start=True, stop=True).then_inc(hT_full, 1)
                    again(e, rows_done, before)
                    for b in range(GB):
                        mm = e.matmul(p_rows[k][:, b * D:(b + 1) * D], xT[k][:, b * P:(b + 1) * P], wxT[:, :], start=True, stop=True)
                    mm.then_inc(rows_full, 1)

                pipelined(e, (0, turn_x), (1, make_h))
                e.wait_ge(loads, LOADS)
                for k, tile in enumerate((wq, wv, wac)):
                    e.transpose(p_w[:, k * P:(k + 1) * P], tile[:, :], ident[:, :])
                e.transpose(p_w2[0:2 * FE, 0:P], we_bk[:, 0:2 * FE], ident[:, :]).then_inc(w_turned, 1)

            @block.scalar
            def _(e):
                e.dma_start(dst_a[:, :, :], dst[0:3 * CP * CH].rearrange("(p k c) -> p k c", k=3, c=CH)).then_inc(dst_in, 16)
                e.dma_start(dst_z[:, :], row(dst[LAST:E])).then_inc(dst_in, 16)
                for tile, m in ((wq, Wq), (wk, Wk), (wv, Wv), (wac, W_ac)):
                    e.dma_start(tile[:, :], m).then_inc(loads, 16)
                e.dma_start(we_bk[:, 0:2 * FE], We).then_inc(loads, 16)
                with nc.allow_non_contiguous_dma(reason="bias columns, 128 numbers each"):
                    e.dma_start(we_bk[:, 2 * FE:A2], col(bk)).then_inc(loads, 16)
                    e.dma_start(bq_c[:, :], col(bq)).then_inc(loads, 16)
                    e.dma_start(bac_c[:, :], col(b_ac)).then_inc(loads, 16)
                e.dma_start(tw_raw[:, :], time_w.partition_broadcast(P)).then_inc(loads, 16)
                e.dma_start(tb_raw[:, :], time_b.partition_broadcast(P)).then_inc(loads, 16)
                e.dma_start(we_bvT[2 * FE:A2, :], row(bv)).then_inc(loads, 16)
                e.wait_ge(w_turned, 1)
                e.activation(wxT[:, :], p_w[:, 0:P], ACT.Copy).then_inc(w_copied, 1)
                e.activation(nv_cols[:, :], p_w[:, P:P + BLOCKS], ACT.Copy).then_inc(w_copied, 1)
                e.wait_ge(first_in, FIRST)

                def copy_x(g, k):
                    again(e, rows_full, val(e, g - 1))
                    e.wait_ge(xT_full, val(e, g + 1))
                    e.sem_inc(passed, 1)
                    e.activation(xT[k][:, :], p_xT[k][:, :], ACT.Copy).then_inc(xT_done, 1)

                def copy_h(g, k):
                    at = place(e, g, G)
                    e.wait_ge(hT_full, val(e, g + 1))
                    e.sem_inc(passed, 1)
                    e.activation(hT[:, bass.ds(at, G)], p_hT[k][:, :], ACT.Identity, bias=bx_c[:, 0:1]).then_inc(hT_done, 1)

                def store(g, k):
                    at, seen = val(e, g * G), val(e, g + 1)
                    e.wait_ge(rows_done, seen)
                    e.sem_inc(passed, 1)
                    e.dma_start(h_table[bass.ds(at, G), :].rearrange("(b p) d -> p b d", p=P), h_rows[k][:, :, :]).then_inc(h_out[k], 16)

                pipelined(e, (0, copy_x), (1, copy_h), (2, store))
                e.wait_ge(h_out[0], 16 * (NG - NG // 2))
                e.wait_ge(h_out[1], 16 * (NG // 2))

            @block.vector
            def _(e):
                e.memset(eps_c[:, :], EPS)
                e.wait_ge(dst_in, 32)
                for k, op in enumerate((ALU.min, ALU.max)):
                    e.tensor_reduce(ends_a[:, k, :], dst_a[:, :, :], AX_X, op).then_inc(ends_done, 1)
                    e.tensor_reduce(ends_z[:, k:k + 1], dst_z[:, :], AX_X, op).then_inc(ends_done, 1)

                def copy_rows(g, k):
                    blk = place(e, g, GB)
                    again(e, h_out[k], val(e, (g - k) * 8))
                    e.tensor_copy(h_rows[k][:, :, 0:1], nv_cols[:, bass.ds(blk, GB)].rearrange("p (b o) -> p b o", o=1))
                    e.wait_ge(rows_full, val(e, g + 1))
                    e.tensor_tensor(h_rows[k][:, :, 1:ROW], p_rows[k][:, :].rearrange("p (b d) -> p b d", d=D),
                                    bx_b[:, :].unsqueeze(1).broadcast_to([P, GB, D]), ALU.add).then_inc(rows_done, 1)

                e.wait_ge(w_copied, 2)
                pipelined(e, (1, copy_rows))
                e.wait_ge(w_turned, 2)
                e.tensor_copy(wqT[:, :], p_w[:, 0:P])
                e.tensor_copy(wvT[:, :], p_w[:, P:2 * P])
                e.tensor_copy(we_bvT[0:2 * FE, :], p_w2[0:2 * FE, 0:P])
                e.tensor_tensor(dT[:, :], p_w[:, 2 * P:3 * P], wac[:, :], ALU.subtract).then_inc(w_copied, 1)
                e.wait_ge(w_copied, 3)
                e.scalar_tensor_tensor(out=aT[:, :], in0=ident[:, :], scalar=-GAMMA, in1=dT[:, :], op0=ALU.mult, op1=ALU.add)
                e.wait_ge(loads, LOADS)
                e.tensor_scalar(tw_b[:, :], tw_raw[:, :], 1.0 / (2.0 * pi), None, ALU.mult)
                e.tensor_scalar(tb_b[:, :], tb_raw[:, :], 1.0 / (2.0 * pi), 0.25, ALU.mult, ALU.add)
                e.tensor_copy(iota_b[:, :], iota_row[:, :])
                e.wait_ge(ends_in, 32)
                e.tensor_copy(start_i[:, :], ends_r[:, 0, :])
                e.tensor_tensor(span_r[:, :], ends_r[:, 1, :], ends_r[:, 0, :], ALU.subtract).then_inc(ends_done, 1)
                e.wait_ge(ends_done, 5)
                e.tensor_reduce(span_m[:, :], span_r[:, :], AX_X, ALU.max).then_inc(ends_done, 1)
                e.wait_ge(ends_done, 6)
                e.tensor_copy(span_i[:, :], span_m[:, :]).then_inc(ends_done, 1)

            steps.close()

        moved = sem("moved")
        back_in = sem("back_in")

        def move_windows():
            with ExitStack() as ctx:
                block = ctx.enter_context(nc.Block())

                @block.vector
                def _(e):
                    e.tensor_scalar(start_b[:, :], start_b[:, :], float(W), float(N), ALU.add, ALU.min).then_inc(moved, 1)
                    e.wait_ge(moved, 1)
                    e.tensor_copy(start_i[:, :], start_b[0:1, :]).then_inc(moved, 1)
                    e.wait_ge(moved, 2)
                    e.sem_clear(moved)

        def pick(e, index):
            return e.value_load(start_i[0:1, bass.ds(index, 1)], min_val=0, max_val=N)

        def shift(c, k):
            return c[0] + (c[1] + k) // SLOTS, (c[1] + k) % SLOTS

        def number(c):
            return c[0] * SLOTS + c[1]

        def is_last(c):
            return isinstance(c[0], int) and number(c) == NCH - 1

        def is_first(c):
            return isinstance(c[0], int) and number(c) == 0

        def gathered(c, r):
            skipped = 16 * SKIP if c[1] == SLOTS - 1 else 0
            return c[0] * (16 * J) + r * (TURNS * 16 * J - skipped) + (16 * J - (skipped if is_last(c) else 0))

        def chunks(e, run, apart_first=None):
            for u in range(SLOTS):
                (apart_first or run)((0, u))
            with e.Fori(1, TURNS - 1) as i:
                for u in range(SLOTS):
                    run((i, u))
            for u in range(SLOTS):
                run((TURNS - 1, u))

        with ExitStack() as ctx:
            he = [sb(f"he{k}", [P, J, ROW], ctx=ctx) for k in range(SLOTS)]
            rest = [sb(f"rest{k}", [P, J // 2, A2, 2], ctx=ctx) for k in range(SLOTS)]
            src_i = [sb(f"src_i{k}", [P, J], I32, ctx=ctx) for k in range(SLOTS)]
            dst_c = [sb(f"dst_c{k}", [P, J], I32, ctx=ctx) for k in range(SLOTS)]
            when = [sb(f"when{k}", [P, J], ctx=ctx) for k in range(SLOTS)]
            feat = [sb(f"feat{k}", [P, J, FE], ctx=ctx) for k in range(SLOTS)]
            qk_win = [sb(f"qk_win{k}", [P, W], ctx=ctx) for k in range(SLOTS)]
            qk_two = [sb(f"qk_two{k}", [P, 2, W], ctx=ctx) for k in range(SLOTS)]
            top_d = [sb(f"top_d{k}", [W + 1, 2, W], ctx=ctx) for k in range(SLOTS)]
            gap = sb("gap", [P, J], ctx=ctx)
            dist = sb("dist", [P, J], ctx=ctx)
            turns_w = sb("turns_w", [P, J // 2, FE, 2], ctx=ctx)
            turns = sb("turns", [P, J // 2, FE, 2], ctx=ctx)
            turns_r = sb("turns_r", [P, J // 2, FE, 2], ctx=ctx)
            in_win = sb("in_win", [P, J], BF16, ctx=ctx)
            other = sb("other", [P, J, W], BF16, ctx=ctx)
            heT1 = sb("heT1", [P, CH], ctx=ctx)
            heT2 = sb("heT2", [P, HALF], ctx=ctx)
            score = sb("score", [P, J, W], ctx=ctx)
            top_j = sb("top_j", [P, W], ctx=ctx)
            top_n = sb("top_n", [W, 1], ctx=ctx)
            top = sb("top", [P, W], ctx=ctx)
            rise = sb("rise", [P, W], ctx=ctx)
            level = sb("level", [P, W], ctx=ctx)
            fade = sb("fade", [P, W], ctx=ctx)
            prob = sb("prob", [P, J, W], ctx=ctx)
            qT = [sb(f"qT{k}", [P, G], ctx=ctx) for k in range(2)]
            qk = [sb(f"qk{k}", [P, 2, G], ctx=ctx) for k in range(2)]

            p_turn = [ctx.enter_context(nc.psum_tensor(f"p_turn{k}", [P, 512], F32)) for k in range(4)]
            p_score = [ctx.enter_context(nc.psum_tensor(f"p_score{k}", [P, J // 2, W], F32)) for k in range(2)]
            p_sum = ctx.enter_context(nc.psum_tensor("p_sum", [P, 2, W], F32))
            p_small = ctx.enter_context(nc.psum_tensor("p_small", [P, P + 2 * W], F32))
            p_topT, p_tops = p_small[0:W, 0:P], p_small[:, P:P + 2 * W]
            p_top, p_qbk = p_small[:, P:P + W], p_small[:, P + W:P + 2 * W]

            loaded = [sem(f"loaded{k}") for k in range(SLOTS)]
            win_in = [early_sem(f"win_in{k}") for k in range(SLOTS)]
            rows_in = [sem(f"rows_in{k}") for k in range(SLOTS)]
            q_full = early_sem("q_full")
            q_done = early_sem("q_done")
            k1_full = early_sem("k1_full")
            k1_done = early_sem("k1_done")
            k2_full = early_sem("k2_full")
            k2_done = early_sem("k2_done")
            qk_out = [early_sem(f"qk_out{k}") for k in range(2)]
            gap_done = sem("gap_done")
            dist_done = sem("dist_done")
            turns_w_done = sem("turns_w_done")
            turns_done = sem("turns_done")
            turns_r_done = sem("turns_r_done")
            phase_done = sem("phase_done")
            he_done = sem("he_done")
            in_win_done = sem("in_win0_done")
            other_done = sem("other_done")
            turn_full = [sem(f"turn_full{q}") for q in range(3)]
            turn_done = [sem(f"turn_done{q}") for q in range(3)]
            score_full = [sem(f"score_full{h}") for h in range(2)]
            masked = [sem(f"masked{h}") for h in range(2)]
            top_j_done = sem("top_j_done")
            topT_full = sem("topT_full")
            top_n_done = sem("top_n_done")
            top_d_done = sem("top_d_done")
            top_full = sem("top_full")
            top_done = sem("top_done")
            rise_done = sem("rise_done")
            level_done = sem("level_done")
            below_done = sem("below_done")
            fade_done = sem("fade_done")
            prob_done = sem("prob_done")
            kept_top = sem("kept_top")
            faded = sem("faded")
            sum_full = sem("sum_full")
            added = sem("added")
            cut_done = sem("cut_done")
            ready = sem("ready")

            READY = 3 * SLOTS + 3

            with ExitStack() as c2:
                block = c2.enter_context(nc.Block())

                @block.gpsimd
                def _(e):
                    for k in range(SLOTS):
                        e.memset(rest[k][:, :, A2 - 1:A2, :], 1.0).then_inc(ready, 1)
                    for k in range(2):
                        e.memset(qk[k][:, 1, :], 0.0).then_inc(ready, 1)

                @block.vector
                def _(e):
                    e.memset(p_sum[:, :, :], 0.0).then_inc(ready, 1)
                    for k in range(SLOTS):
                        e.memset(qk_two[k][:, :, :], 0.0).then_inc(ready, 1)
                        e.memset(top_d[k][:, :, :], 0.0).then_inc(ready, 1)

            def layer0_round(r):
                at_first = isinstance(r, int)
                base = r * TURNS
                with ExitStack() as c2:
                    block = c2.enter_context(nc.Block())

                    def count(c):
                        return (c[0] + base) * SLOTS + c[1]

                    @block.sync
                    def _(e):
                        def store_qk(g, k):
                            at, seen = val(e, g * G), val(e, g + 1)
                            e.wait_ge(k1_done, seen)
                            e.wait_ge(k2_done, seen)
                            e.sem_inc(passed, 1)
                            e.dma_start(qk_table[:, :, bass.ds(at, G)], qk[k][:, :, :]).then_inc(qk_out[k], 16)

                        def load_window(c):
                            u = c[1]
                            start = pick(e, number(c))
                            e.dma_start(qk_win[u][:, :], qk_table[:, 0, bass.ds(start, W)]).then_inc(win_in[u], 16)
                            for k in range(2):
                                e.dma_start(qk_two[u][k:P:2, k, :], qk_table[0:2 * FE, 1, bass.ds(start, W)]).then_inc(win_in[u], 16)
                            e.dma_start(top_d[u][W:W + 1, :, :], qk_table[2 * FE:A2, 1, bass.ds(start, W)].unsqueeze(1).broadcast_to([1, 2, W])).then_inc(win_in[u], 16)

                        def load_edges(c):
                            i, u = c
                            at = LAST if is_last(c) else val(e, number(c) * CH)
                            by_p = "(j p) -> p j" if is_last(c) else "(p j) -> p j"
                            again(e, sum_full, val(e, count(c) - SLOTS + 1))
                            e.sem_inc(passed, 1)
                            with nc.allow_non_contiguous_dma(reason="order of the last chunk's edges"):
                                e.dma_start(src_i[u][:, :], src[bass.ds(at, CH)].rearrange(by_p, j=J)).then_inc(loaded[u], 16)
                                e.dma_start(when[u][:, :], edge_weight[bass.ds(at, CH)].rearrange(by_p, j=J)).then_inc(loaded[u], 16)
                                e.dma_start(feat[u][:, :, :], edge_attr[bass.ds(at, CH), :].rearrange("(j p) f -> p j f" if is_last(c) else "(p j) f -> p j f", j=J)).then_inc(loaded[u], 16)
                                e.dma_start(dst_c[u][:, :], dst[bass.ds(at, CH)].rearrange(by_p, j=J)).then_inc(loaded[u], 16)

                        def load(c):
                            load_edges(c)
                            load_window(c)

                        if at_first:
                            for u in range(SLOTS):
                                load_edges((0, u))
                            pipelined(e, (1, store_qk))
                            e.wait_ge(qk_out[0], 16 * (NG - NG // 2))
                            e.wait_ge(qk_out[1], 16 * (NG // 2))
                            e.wait_ge(ready, READY)
                            for u in range(SLOTS):
                                load_window((0, u))
                            chunks(e, load, apart_first=lambda c: None)
                        else:
                            chunks(e, load)

                    @block.gpsimd
                    def _(e):
                        def gather(c):
                            u = c[1]
                            e.wait_ge(loaded[u], val(e, (c[0] + base) * 64 + 64))
                            e.sem_inc(passed, 1)
                            for j in range(SKIP if is_last(c) else 0, J):
                                e.indirect_dma_start(
                                    out=he[u][:, j, 0:ROW], out_offset=None, in_=h_table[:, :],
                                    in_offset=bass.IndirectOffsetOnAxis(ap=src_i[u][:, j:j + 1], axis=0)).then_inc(rows_in[u], 16)

                        with e.Fori(0, TURNS - 1) as i:
                            for u in range(SLOTS):
                                gather((i, u))
                        for u in range(SLOTS):
                            gather((TURNS - 1, u))

                    @block.tensor
                    def _(e):
                        def turn(c):
                            u = c[1]
                            n = count(c)
                            n0, n1 = val(e, n), val(e, n + 1)
                            e.wait_ge(he_done, n1)
                            again(e, turn_done[2], n0)
                            for k in range(J // 2):
                                mm = e.transpose(p_turn[2][:, k * P:(k + 1) * P], rest[u][:, k, 0:2 * FE, :].rearrange("p f q -> p (f q)"), ident[:, :])
                            mm.then_inc(turn_full[2], 1)
                            for h in range(2):
                                again(e, turn_done[h], n0)
                                for k in range(4):
                                    mm = e.transpose(p_turn[h][:, k * P:(k + 1) * P], he[u][:, 4 * h + k, 1:ROW], ident[:, :])
                                mm.then_inc(turn_full[h], 1)

                        def scores(c):
                            u = c[1]
                            n = count(c)
                            n0, n1 = val(e, n), val(e, n + 1)
                            e.wait_ge(win_in[u], val(e, (c[0] + base) * 64 + 64))
                            e.wait_ge(turn_done[2], n1)
                            for h in range(2):
                                e.wait_ge(turn_done[h], n1)
                                again(e, masked[h], n0)
                                for k in (0, 2):
                                    pair = (4 * h + k) // 2
                                    e.matmul(p_score[h][:, k:k + 2, :], heT2[:, pair * P:(pair + 1) * P], qk_two[u][:, :, :], start=True, stop=False)
                                    for j in (4 * h + k, 4 * h + k + 1):
                                        mm = e.matmul(p_score[h][:, j % 4, :], heT1[:, j * P:(j + 1) * P], qk_win[u][:, :], start=False, stop=(j % 2 == 1))
                                mm.then_inc(score_full[h], 1)

                        def turn_top(c):
                            n = count(c)
                            e.wait_ge(top_j_done, val(e, n + 1))
                            again(e, level_done, val(e, n))
                            e.transpose(p_topT, top_j[:, :], ident[:, :]).then_inc(topT_full, 1)

                        def spread_top(c):
                            e.wait_ge(top_d_done, val(e, count(c) + 1))
                            e.matmul(p_tops, ones[0:W + 1, :], top_d[c[1]][:, :, :], start=True, stop=True).then_inc(top_full, 1)

                        def sums(c):
                            u = c[1]
                            n = count(c)
                            e.wait_ge(prob_done, val(e, n + 1))
                            again(e, added, val(e, n))
                            for j in range(J):
                                e.matmul(p_sum[:, 0, :], he[u][:, j, 1:ROW], prob[:, j, :], start=(j == 0), stop=(j == J - 1))
                            for j in range(J):
                                mm = e.matmul(p_sum[0:A2, 1, :], rest[u][:, j // 2, :, j % 2], prob[:, j, :], start=(j == 0), stop=(j == J - 1))
                            mm.then_inc(sum_full, 1)

                        def step(c):
                            if not is_last(c):
                                turn(shift(c, 1))
                            turn_top(c)
                            if not is_first(c):
                                sums(shift(c, -1))
                            spread_top(c)
                            if not is_last(c):
                                scores(shift(c, 1))

                        def make_q(g, k):
                            at = place(e, g, G)
                            again(e, q_done, val(e, g - 1))
                            e.matmul(p_turn[k][:, :], wqT[:, :], hT[:, bass.ds(at, G)], start=True, stop=True).then_inc(q_full, 1)

                        def make_qk(g, k):
                            before = val(e, g)
                            e.wait_ge(q_done, val(e, g + 1))
                            again(e, k1_done, before)
                            e.matmul(p_turn[2][:, :], wk[:, :], qT[k][:, :], start=True, stop=True).then_inc(k1_full, 1)
                            again(e, k2_done, before)
                            e.matmul(p_turn[3][0:A2, :], we_bk[:, :], qT[k][:, :], start=True, stop=True).then_inc(k2_full, 1)

                        e.wait_ge(ready, READY)
                        if at_first:
                            pipelined(e, (0, make_q), (1, make_qk))
                            e.wait_ge(k1_done, NG)
                            e.wait_ge(k2_done, NG)
                        turn((0, 0))
                        scores((0, 0))
                        chunks(e, step)
                        sums((TURNS - 1, SLOTS - 1))

                    @block.scalar
                    def _(e):
                        def times(c):
                            u = c[1]
                            e.wait_ge(phase_done, val(e, count(c) + 1))
                            e.sem_inc(passed, 1)
                            e.activation(rest[u][:, :, 0:FE, :], feat[u][:, :, :].rearrange("p (k q) f -> p k f q", q=2), ACT.Copy)
                            part = rest[u][:, :, FE:2 * FE, :]
                            e.activation(part, part, ACT.Sin, scale=-2.0 * pi).then_inc(he_done, 1)

                        def copy_turns(c):
                            n = count(c)
                            n0, n1 = val(e, n), val(e, n + 1)
                            for q in (2, 0, 1):
                                again(e, score_full[1], n0)
                                e.wait_ge(turn_full[q], n1)
                                e.sem_inc(passed, 1)
                                to = heT2[:, :] if q == 2 else heT1[:, q * HALF:(q + 1) * HALF]
                                e.activation(to, p_turn[q][:, :], ACT.Copy).then_inc(turn_done[q], 1)

                        def exps(c):
                            n = count(c)
                            n0, n1 = val(e, n), val(e, n + 1)
                            start = pick(e, number(c))
                            e.wait_ge(below_done, n1)
                            e.sem_inc(passed, 1)
                            e.activation(prob[:, :, :], prob[:, :, :], ACT.Exp).then_inc(prob_done, 1)
                            again(e, faded, n0)
                            e.sem_inc(passed, 1)
                            e.activation(fade[:, :], rise[:, :], ACT.Exp).then_inc(fade_done, 1)
                            e.activation(tops_so_far[:, bass.ds(start, W)], top[:, :], ACT.Copy).then_inc(kept_top, 1)

                        def step(c):
                            if not is_last(c):
                                copy_turns(shift(c, 1))
                                if not is_last(shift(c, 1)):
                                    times(shift(c, 2))
                            exps(c)

                        def copy_q(g, k):
                            again(e, k2_full, val(e, g - 1))
                            e.wait_ge(q_full, val(e, g + 1))
                            e.sem_inc(passed, 1)
                            e.activation(qT[k][:, :], p_turn[k][:, :], ACT.Identity, bias=bq_c[:, 0:1]).then_inc(q_done, 1)

                        def copy_k2(g, k):
                            again(e, qk_out[k], val(e, (g - k) * 8))
                            e.wait_ge(k2_full, val(e, g + 1))
                            e.sem_inc(passed, 1)
                            e.activation(qk[k][0:A2, 1, :], p_turn[3][0:A2, :], ACT.Copy, scale=SCALE).then_inc(k2_done, 1)

                        e.wait_ge(ready, READY)
                        if at_first:
                            pipelined(e, (0, copy_q), (1, copy_k2))
                        times((0, 0))
                        times((0, 1))
                        copy_turns((0, 0))
                        chunks(e, step)

                    @block.vector
                    def _(e):
                        def phases(c):
                            i, u = c
                            n1 = val(e, count(c) + 1)
                            e.wait_ge(rows_in[u], val(e, gathered(c, r)))
                            e.tensor_tensor(gap[:, :], he[u][:, :, 0:1].rearrange("p j o -> p (j o)"), when[u][:, :], ALU.subtract).then_inc(gap_done, 1)
                            e.wait_ge(gap_done, n1)
                            e.scalar_tensor_tensor(out=dist[:, :], in0=gap[:, :], scalar=-1.0, in1=gap[:, :], op0=ALU.mult,
                                                   op1=ALU.max).then_inc(dist_done, 1)
                            e.wait_ge(dist_done, n1)
                            e.tensor_tensor(turns_w[:, :, :, :], dist[:, :].rearrange("p (k q) -> p k q", q=2).unsqueeze(2).broadcast_to([P, J // 2, FE, 2]),
                                            tw_b[:, :].unsqueeze(1).unsqueeze(3).broadcast_to([P, J // 2, FE, 2]), ALU.mult).then_inc(turns_w_done, 1)
                            e.wait_ge(turns_w_done, n1)
                            e.tensor_tensor(turns[:, :, :, :], turns_w[:, :, :, :], tb_b[:, :].unsqueeze(1).unsqueeze(3).broadcast_to([P, J // 2, FE, 2]),
                                            ALU.add).then_inc(turns_done, 1)
                            e.wait_ge(turns_done, n1)
                            e.tensor_scalar(turns_r[:, :, :, :], turns[:, :, :, :], ROUND, None, ALU.add).then_inc(turns_r_done, 1)
                            e.wait_ge(turns_r_done, n1)
                            e.scalar_tensor_tensor(out=rest[u][:, :, FE:2 * FE, :], in0=turns_r[:, :, :, :], scalar=-ROUND,
                                                   in1=turns[:, :, :, :], op0=ALU.add, op1=ALU.subtract).then_inc(phase_done, 1)

                        def places(c):
                            i, u = c
                            n = count(c)
                            n0, n1 = val(e, n), val(e, n + 1)
                            e.wait_ge(loaded[u], val(e, (i + base) * 64 + 64))
                            if is_last(c):
                                e.memset(dst_c[u][:, 0:DUP // P], -1).then_inc(cut_done, 1)
                                e.memset(dst_c[u][0:DUP % P, DUP // P:DUP // P + 1], -1).then_inc(cut_done, 1)
                                e.wait_ge(cut_done, val(e, r * 2 + 2))
                            again(e, other_done, n0)
                            e.tensor_scalar(in_win[:, :], dst_c[u][:, :], start_b[:, bass.ds(number(c), 1)], None, ALU.subtract).then_inc(in_win_done, 1)

                        def others(c):
                            n = count(c)
                            n0, n1 = val(e, n), val(e, n + 1)
                            e.wait_ge(in_win_done, n1)
                            for h in range(2):
                                again(e, masked[h], n0)
                            e.tensor_tensor(other[:, :, :], in_win[:, :].unsqueeze(2).broadcast_to([P, J, W]),
                                            iota_b[:, :].unsqueeze(1).broadcast_to([P, J, W]), ALU.not_equal).then_inc(other_done, 1)

                        def masks(c):
                            n = count(c)
                            n1 = val(e, n + 1)
                            e.wait_ge(other_done, n1)
                            again(e, below_done, val(e, n))
                            for h in range(2):
                                e.wait_ge(score_full[h], n1)
                                e.scalar_tensor_tensor(out=score[:, 4 * h:4 * h + 4, :], in0=other[:, 4 * h:4 * h + 4, :], scalar=NEVER,
                                                       in1=p_score[h][:, :, :], op0=ALU.mult, op1=ALU.add).then_inc(masked[h], 1)
                            for h in range(2):
                                e.wait_ge(masked[h], n1)
                            e.tensor_reduce(top_j[:, :], score[:, :, :].rearrange("p j w -> p w j"), AX_X, ALU.max).then_inc(top_j_done, 1)

                        def tops_of_nodes(c):
                            e.wait_ge(topT_full, val(e, count(c) + 1))
                            e.tensor_reduce(top_n[:, :], p_topT, AX_X, ALU.max).then_inc(top_n_done, 1)

                        def diagonals(c):
                            e.wait_ge(top_n_done, val(e, count(c) + 1))
                            e.tensor_scalar(top_d[c[1]][0:W, 0, :], ident[0:W, 0:W], top_n[:, 0:1], None, ALU.mult).then_inc(top_d_done, 1)

                        starts = {}

                        def pick_start(c):
                            if c[1] == 0 and not is_first(c):
                                starts["before"] = pick(e, number(shift(c, -1)))
                            elif not is_first(c):
                                starts["before"] = starts["now"]
                            starts["now"] = pick(e, number(c))

                        def belows(c):
                            n = count(c)
                            n0, n1 = val(e, n), val(e, n + 1)
                            start = starts["now"]
                            again(e, kept_top, n0)
                            e.wait_ge(top_full, n1)
                            before = tops_so_far[:, bass.ds(start, W)]
                            e.tensor_tensor(top[:, :], before, p_top, ALU.max).then_inc(top_done, 1)
                            e.wait_ge(top_done, n1)
                            e.tensor_tensor(level[:, :], top[:, :], p_qbk, ALU.subtract).then_inc(level_done, 1)
                            e.tensor_tensor(rise[:, :], before, top[:, :], ALU.subtract).then_inc(rise_done, 1)
                            again(e, sum_full, n0)
                            e.wait_ge(level_done, n1)
                            e.tensor_tensor(prob[:, :, :], score[:, :, :], level[:, :].unsqueeze(1).broadcast_to([P, J, W]),
                                            ALU.subtract).then_inc(below_done, 1)

                        def add(c, start):
                            n = count(c)
                            n0, n1 = val(e, n), val(e, n + 1)
                            here = acc[:, :, bass.ds(start, W)]
                            again(e, added, n0)
                            e.wait_ge(fade_done, n1)
                            e.tensor_tensor(here, here, fade[:, :].unsqueeze(1).broadcast_to([P, 2, W]), ALU.mult).then_inc(faded, 1)
                            e.wait_ge(faded, n1)
                            e.wait_ge(sum_full, n1)
                            e.tensor_tensor(here, here, p_sum[:, :, :], ALU.add).then_inc(added, 1)

                        def step(c):
                            if not is_last(c):
                                places(shift(c, 1))
                            tops_of_nodes(c)
                            if not is_last(c):
                                others(shift(c, 1))
                            pick_start(c)
                            diagonals(c)
                            if not is_last(c) and not is_last(shift(c, 1)):
                                phases(shift(c, 2))
                            if not is_first(c):
                                add(shift(c, -1), starts["before"])
                            belows(c)
                            if not is_last(c):
                                masks(shift(c, 1))

                        def copy_k1(g, k):
                            again(e, qk_out[k], val(e, (g - k) * 8))
                            e.wait_ge(k1_full, val(e, g + 1))
                            e.tensor_scalar(qk[k][:, 0, :], p_turn[2][:, :], SCALE, None, ALU.mult).then_inc(k1_done, 1)

                        e.wait_ge(ready, READY)
                        if at_first:
                            pipelined(e, (1, copy_k1))
                        phases((0, 0))
                        phases((0, 1))
                        places((0, 0))
                        others((0, 0))
                        masks((0, 0))
                        chunks(e, step)
                        add((TURNS - 1, SLOTS - 1), starts["now"])

            layer0_round(0)
            spread_out = nc.values_load(span_i[0:1, 0:1], min_val=0, max_val=N)
            with nc.If(spread_out >= W):
                with nc.Fori(1, ROUNDS) as w:
                    move_windows()
                    layer0_round(w)
                with ExitStack() as c2:
                    block = c2.enter_context(nc.Block())

                    @block.sync
                    def _(e):
                        e.dma_start(start_b[:, :], start_dram[0, :].partition_broadcast(P)).then_inc(back_in, 16)

                    @block.vector
                    def _(e):
                        e.wait_ge(back_in, 16)
                        e.tensor_copy(start_i[:, :], start_b[0:1, :])

        with ExitStack() as c2:
            block = c2.enter_context(nc.Block())

            @block.sync
            def _(e):
                for used in early_sems:
                    e.sem_clear(used)

        early.close()

        layer0.close()
        x1_rows = sb("x1_rows", [P, BLOCKS, D])
        x1T = hT
        bn2_b = sb("bn2_b", [P, D])
        bn1_c = sb("bn1_c", [P, 1])
        wn1 = sb("wn1", [P, 2, D])
        wn2 = sb("wn2", [P, D])
        we2n = sb("we2n", [P, D])
        be2n = sb("be2n", [1, D])

        with ExitStack() as ctx:
            X = sb("X", [P, BLOCKS, D], ctx=ctx)
            we1 = sb("we1", [P, 2, D], ctx=ctx)
            we2 = sb("we2", [P, D], ctx=ctx)
            we2T = sb("we2T", [P, D], ctx=ctx)
            be2_c = sb("be2_c", [P, 1], ctx=ctx)
            be1_b = sb("be1_b", [P, D], ctx=ctx)
            nought = sb("nought", [P, G], ctx=ctx)
            den = sb("den", [BLOCKS, P], ctx=ctx)
            den_e = sb("den_e", [BLOCKS, P], ctx=ctx)
            rden = sb("rden", [BLOCKS, P], ctx=ctx)
            rden_b = [sb(f"rden_b{k}", [P, G], ctx=ctx) for k in range(2)]
            mean_v = sb("mean_v", [P, G], ctx=ctx)
            pre = sb("pre", [P, G], ctx=ctx)
            upd = sb("upd", [P, G], ctx=ctx)
            h2 = sb("h2", [P, G], ctx=ctx)
            outT = [sb(f"outT{k}", [P, G], ctx=ctx) for k in range(2)]
            y = [sb(f"y{k}", [P, GB, D], ctx=ctx) for k in range(2)]
            stats = sb("stats", [P, GB, 6], ctx=ctx)
            mv = [sb(f"mv{k}", [P, GB, 2], ctx=ctx) for k in range(2)]
            std = [sb(f"std{k}", [P, GB], ctx=ctx) for k in range(2)]
            rstd = sb("rstd", [P, GB], ctx=ctx)
            xn = [sb(f"xn{k}", [P, GB, D], ctx=ctx) for k in range(2)]
            x1T_g = [sb(f"x1T_g{k}", [P, G], ctx=ctx) for k in range(2)]
            p_rows = [sb(f"p_rows{k}", [P, GB, D], ctx=ctx) for k in range(2)]
            r_rows = [sb(f"r_rows{k}", [P, GB, D], ctx=ctx) for k in range(2)]

            ps = [ctx.enter_context(nc.psum_tensor(f"psC{k}", [P, 512], F32)) for k in range(8)]
            p_val, p_anti, p_out, p_x1, p_p, p_r, p_w, _ = ps

            names = ("val_full anti_full den_done rden_done cleared mean_done pre_done upd_done h2_done outT_done out_full "
                     "y_done stats_done mv_done root_done rstd_done xn_done x1_full x1T_done p_full r_full p_done "
                     "r_done kept").split()
            s = {n: sem(n) for n in names}
            loads = sem("loads_c")
            x_zero = sem("x_zero_c")
            x_in = sem("x_in_c")
            den_io = sem("den_io")
            rden_in = [sem(f"rden_in{k}") for k in range(2)]
            w_full = sem("w_full_c")
            w_done = sem("w_done_c")
            p_out_d = [sem(f"p_out_d{k}") for k in range(2)]
            r_out_d = [sem(f"r_out_d{k}") for k in range(2)]

            block = ctx.enter_context(nc.Block())
            LOADS2 = 16 * 8

            @block.sync
            def _(e):
                e.dma_start(den_dram[0:1, :], acc[2 * FE:A2, 1, :]).then_inc(den_io, 16)
                e.wait_ge(den_io, 16)
                e.dma_start(den[:, :], den_dram[0, :].rearrange("(b p) -> b p", p=P)).then_inc(den_io, 16)
                e.wait_ge(x_zero, 1)
                mid = FULL // 2
                e.dma_start(X[:, 0:mid, :], x[0:mid * P, :].rearrange("(b p) d -> p b d", p=P)).then_inc(x_in, 16)
                e.dma_start(X[:, mid:FULL, :], x[mid * P:FULL * P, :].rearrange("(b p) d -> p b d", p=P)).then_inc(x_in, 16)
                e.dma_start(X[0:REST, FULL, :], x[FULL * P:N, :]).then_inc(x_in, 16)
                e.dma_start(we1[:, :, :], We1.rearrange("(k p) d -> p k d", p=P)).then_inc(loads, 16)
                e.dma_start(be1_b[:, :], be1.partition_broadcast(P)).then_inc(loads, 16)
                e.dma_start(wn1[:, :, :], Wn1.rearrange("(k p) d -> p k d", p=P)).then_inc(loads, 16)
                e.dma_start(we2[:, :], We2).then_inc(loads, 16)
                e.dma_start(wn2[:, :], Wn2).then_inc(loads, 16)
                e.dma_start(bn2_b[:, :], bn2.partition_broadcast(P)).then_inc(loads, 16)
                with nc.allow_non_contiguous_dma(reason="bias columns, 128 numbers each"):
                    e.dma_start(bn1_c[:, :], col(bn1)).then_inc(loads, 16)
                    e.dma_start(be2_c[:, :], col(be2)).then_inc(loads, 16)
                e.wait_ge(s["rden_done"], 1)
                e.dma_start(den_dram[1, :].rearrange("(b p) -> b p", p=P), rden[:, :]).then_inc(den_io, 16)
                e.wait_ge(den_io, 48)

                def load_rden(g, k):
                    at = val(e, g * G)
                    again(e, s["mean_done"], val(e, g - 1))
                    e.sem_inc(passed, 1)
                    e.dma_start(rden_b[k][:, :], den_dram[1, bass.ds(at, G)].partition_broadcast(P)).then_inc(rden_in[k], 16)

                def store(g, k):
                    at, seen = val(e, g * G), val(e, g + 1)
                    e.wait_ge(s["p_done"], seen)
                    e.sem_inc(passed, 1)
                    e.dma_start(p_table[bass.ds(at, G), :].rearrange("(b p) d -> p b d", p=P), p_rows[k][:, :, :]).then_inc(p_out_d[k], 16)
                    e.wait_ge(s["r_done"], seen)
                    e.sem_inc(passed, 1)
                    e.dma_start(r_table[bass.ds(at, G), :].rearrange("(b p) d -> p b d", p=P), r_rows[k][:, :, :]).then_inc(r_out_d[k], 16)

                def load_ahead(g, k):
                    if not (isinstance(g, int) and g + 2 >= NG):
                        load_rden(g + 2, k)

                load_rden(0, 0)
                load_rden(1, 1)
                pipelined(e, (0, load_ahead), (3, store))
                for out_d in (p_out_d, r_out_d):
                    e.wait_ge(out_d[0], 16 * (NG - NG // 2))
                    e.wait_ge(out_d[1], 16 * (NG // 2))

            @block.gpsimd
            def _(e):
                e.memset(X[:, FULL:BLOCKS, :], 0.0).then_inc(x_zero, 1)
                e.memset(nought[:, :], 0.0).then_inc(x_zero, 1)

                def clear(g, k):
                    at = place(e, g, G)
                    e.wait_ge(s["val_full"], val(e, g + 1))
                    e.sem_inc(passed, 1)
                    e.tensor_copy(acc[:, 0, bass.ds(at, G)], nought[:, :]).then_inc(s["cleared"], 1)

                def keep(g, k):
                    at, blk = place(e, g, G), place(e, g, GB)
                    e.wait_ge(s["xn_done"], val(e, g + 1))
                    e.sem_inc(passed, 1)
                    e.tensor_copy(x1_rows[:, bass.ds(blk, GB), :], xn[k][:, :, :])
                    e.wait_ge(s["x1T_done"], val(e, g + 1))
                    e.sem_inc(passed, 1)
                    e.tensor_copy(x1T[:, bass.ds(at, G)], x1T_g[k][:, :]).then_inc(s["kept"], 1)

                e.wait_ge(x_zero, 2)
                pipelined(e, (3, keep), (1, clear))

            @block.tensor
            def _(e):
                def values(g, k):
                    at = place(e, g, G)
                    n0 = val(e, g)
                    again(e, s["mean_done"], n0)
                    e.matmul(p_val[:, :], wvT[:, :], acc[:, 0, bass.ds(at, G)], start=True, stop=False)
                    e.matmul(p_val[:, :], we_bvT[:, :], acc[0:A2, 1, bass.ds(at, G)], start=False, stop=True).then_inc(s["val_full"], 1)
                    again(e, s["pre_done"], n0)
                    e.matmul(p_anti[:, :], aT[:, :], hT[:, bass.ds(at, G)], start=True, stop=True).then_inc(s["anti_full"], 1)

                def turn_out(g, k):
                    e.wait_ge(s["outT_done"], val(e, g + 1))
                    again(e, s["y_done"], val(e, g))
                    for b in range(GB):
                        mm = e.transpose(p_out[:, b * P:(b + 1) * P], outT[k][:, b * P:(b + 1) * P], ident[:, :])
                    mm.then_inc(s["out_full"], 1)

                def turn_x1(g, k):
                    e.wait_ge(s["xn_done"], val(e, g + 1))
                    again(e, s["x1T_done"], val(e, g))
                    for b in range(GB):
                        mm = e.transpose(p_x1[:, b * P:(b + 1) * P], xn[k][:, b, :], ident[:, :])
                    mm.then_inc(s["x1_full"], 1)

                def tables(g, k):
                    n0 = val(e, g)
                    if isinstance(g, int) and g == 0:
                        e.wait_ge(loads, LOADS2)
                    e.wait_ge(s["x1T_done"], val(e, g + 1))
                    for i, (p, full, done) in enumerate(((p_p, "p_full", "p_done"), (p_r, "r_full", "r_done"))):
                        again(e, s[done], n0)
                        for b in range(GB):
                            mm = e.matmul(p[:, b * D:(b + 1) * D], x1T_g[k][:, b * P:(b + 1) * P], we1[:, i, :], start=True, stop=True)
                        mm.then_inc(s[full], 1)

                pipelined(e, (0, values), (3, turn_x1), (1, turn_out), (3, tables))
                e.transpose(p_w[:, 0:P], we2[:, :], ident[:, :]).then_inc(w_full, 1)
                e.wait_ge(w_done, 1)
                e.matmul(p_w[:, P:2 * P], we2T[:, :], wn1[:, 1, :], start=True, stop=True)
                e.matmul(p_w[0:1, 2 * P:3 * P], be2_c[:, :], wn1[:, 1, :], start=True, stop=True).then_inc(w_full, 1)

            @block.scalar
            def _(e):
                def update(g, k):
                    n0, n1 = val(e, g), val(e, g + 1)
                    e.wait_ge(s["pre_done"], n1)
                    again(e, s["h2_done"], n0)
                    e.sem_inc(passed, 1)
                    e.activation(upd[:, :], pre[:, :], ACT.Tanh, bias=bac_c[:, 0:1]).then_inc(s["upd_done"], 1)

                def outs(g, k):
                    e.wait_ge(s["h2_done"], val(e, g + 1))
                    again(e, s["out_full"], val(e, g - 1))
                    e.sem_inc(passed, 1)
                    e.activation(outT[k][:, :], h2[:, :], ACT.Tanh).then_inc(s["outT_done"], 1)

                def roots(g, k):
                    e.wait_ge(s["mv_done"], val(e, g + 1))
                    again(e, s["rstd_done"], val(e, g - 1))
                    e.sem_inc(passed, 1)
                    e.activation(std[k][:, :], mv[k][:, :, 1:2].rearrange("p b o -> p (b o)"), ACT.Sqrt, bias=eps_c[:, 0:1]).then_inc(s["root_done"], 1)

                def copy_x1(g, k):
                    e.wait_ge(s["x1_full"], val(e, g + 1))
                    again(e, s["kept"], val(e, g - 1))
                    again(e, s["r_full"], val(e, g - 1))
                    e.sem_inc(passed, 1)
                    e.activation(x1T_g[k][:, :], p_x1[:, :], ACT.Copy).then_inc(s["x1T_done"], 1)

                def copy_p(g, k):
                    e.wait_ge(s["p_full"], val(e, g + 1))
                    again(e, p_out_d[k], val(e, (g - k) * 8))
                    e.sem_inc(passed, 1)
                    e.activation(p_rows[k][:, :, :], p_p[:, :].rearrange("p (b d) -> p b d", d=D), ACT.Copy).then_inc(s["p_done"], 1)

                pipelined(e, (2, roots), (3, copy_x1), (0, update), (0, outs), (3, copy_p))

            @block.vector
            def _(e):
                def pres(g, k):
                    n0, n1 = val(e, g), val(e, g + 1)
                    e.wait_ge(rden_in[k], val(e, (g - k) * 8 + 16))
                    e.wait_ge(s["val_full"], n1)
                    e.tensor_tensor(mean_v[:, :], p_val[:, :], rden_b[k][:, :], ALU.mult).then_inc(s["mean_done"], 1)
                    e.wait_ge(s["mean_done"], n1)
                    e.wait_ge(s["anti_full"], n1)
                    again(e, s["upd_done"], n0)
                    e.tensor_tensor(pre[:, :], p_anti[:, :], mean_v[:, :], ALU.add).then_inc(s["pre_done"], 1)

                def add_update(g, k):
                    at = place(e, g, G)
                    n0, n1 = val(e, g), val(e, g + 1)
                    e.wait_ge(s["upd_done"], n1)
                    again(e, s["outT_done"], n0)
                    e.tensor_tensor(h2[:, :], hT[:, bass.ds(at, G)], upd[:, :], ALU.add).then_inc(s["h2_done"], 1)

                def moments(g, k):
                    blk = place(e, g, GB)
                    n0, n1 = val(e, g), val(e, g + 1)
                    if isinstance(g, int) and g == 0:
                        e.wait_ge(x_in, 48)
                        e.wait_ge(loads, LOADS2)
                    e.wait_ge(s["out_full"], n1)
                    again(e, s["xn_done"], val(e, g - 1))
                    e.tensor_tensor(y[k][:, :, :], X[:, bass.ds(blk, GB), :], p_out[:, :].rearrange("p (b d) -> p b d", d=D), ALU.add).then_inc(s["y_done"], 1)
                    e.wait_ge(s["y_done"], n1)
                    again(e, s["mv_done"], n0)
                    for b in range(GB):
                        op = e.bn_stats(stats[:, b, :], y[k][:, b, :])
                    op.then_inc(s["stats_done"], 1)
                    e.wait_ge(s["stats_done"], n1)
                    e.sem_inc(passed, 1)
                    for b in range(GB):
                        op = e.bn_aggr(mv[k][:, b, :], stats[:, b, :])
                    op.then_inc(s["mv_done"], 1)

                def normal(g, k):
                    n0, n1 = val(e, g), val(e, g + 1)
                    e.wait_ge(s["root_done"], n1)
                    again(e, s["xn_done"], n0)
                    e.reciprocal(rstd[:, :], std[k][:, :]).then_inc(s["rstd_done"], 1)
                    e.wait_ge(s["rstd_done"], n1)
                    again(e, s["kept"], val(e, g - 1))
                    again(e, s["x1_full"], val(e, g - 1))
                    for b in range(GB):
                        op = e.tensor_scalar(xn[k][:, b, :], y[k][:, b, :], mv[k][:, b, 0:1], rstd[:, b:b + 1], ALU.subtract, ALU.mult)
                    op.then_inc(s["xn_done"], 1)

                def copy_r(g, k):
                    e.wait_ge(s["r_full"], val(e, g + 1))
                    again(e, r_out_d[k], val(e, (g - k) * 8))
                    e.tensor_tensor(r_rows[k][:, :, :], p_r[:, :].rearrange("p (b d) -> p b d", d=D),
                                    be1_b[:, :].unsqueeze(1).broadcast_to([P, GB, D]), ALU.add).then_inc(s["r_done"], 1)

                e.wait_ge(den_io, 32)
                e.tensor_scalar(den_e[:, :], den[:, :], 1.0e-16, None, ALU.add).then_inc(s["den_done"], 1)
                e.wait_ge(s["den_done"], 1)
                e.reciprocal(rden[:, :], den_e[:, :]).then_inc(s["rden_done"], 1)
                pipelined(e, (0, pres), (1, moments), (2, normal), (0, add_update), (3, copy_r))
                e.wait_ge(w_full, 1)
                e.tensor_copy(we2T[:, :], p_w[:, 0:P]).then_inc(w_done, 1)
                e.wait_ge(w_full, 2)
                e.tensor_copy(we2n[:, :], p_w[:, P:2 * P])
                e.tensor_copy(be2n[:, :], p_w[0:1, 2 * P:3 * P])

        with ExitStack() as ctx:
            msg = [sb(f"msg{k}", [P, J, D], ctx=ctx) for k in range(SLOTS)]
            src_i = [sb(f"src1_{k}", [P, J], I32, ctx=ctx) for k in range(SLOTS)]
            dst_c = [sb(f"dst1_{k}", [P, J], I32, ctx=ctx) for k in range(SLOTS)]
            r_win = [sb(f"r_win{k}", [W, D], ctx=ctx) for k in range(SLOTS)]
            hot = [sb(f"hot{k}", [P, J, W], ctx=ctx) for k in range(SLOTS)]
            in_win = sb("in_win1", [P, J], ctx=ctx)
            hotT = sb("hotT", [W, CH], ctx=ctx)
            p_hot = [ctx.enter_context(nc.psum_tensor(f"p_hot{k}", [P, 512], F32)) for k in range(2)]
            p_edge = [ctx.enter_context(nc.psum_tensor(f"p_edge{k}", [P, 4, D], F32)) for k in range(2)]
            p_sum = ctx.enter_context(nc.psum_tensor("p_sum1", [P, 2, W], F32))

            loaded = [sem(f"loaded1_{k}") for k in range(SLOTS)]
            rows_in = [sem(f"rows1_in{k}") for k in range(SLOTS)]
            in_win_done = sem("in_win_done")
            hot_done = sem("hot_done")
            hot_full = [sem(f"hot_full{h}") for h in range(2)]
            hotT_done = [sem(f"hotT_done{h}") for h in range(2)]
            edge_full = [sem(f"edge_full{h}") for h in range(2)]
            both_done = [sem(f"both_done{h}") for h in range(2)]
            relu_done = sem("relu_done")
            sum_full = sem("sum1_full")
            added = sem("added1")
            added2 = sem("added2")
            cut_done = sem("cut1_done")

            def layer1_round(r):
                at_first = isinstance(r, int)
                base = r * TURNS
                with ExitStack() as c2:
                    block = c2.enter_context(nc.Block())

                    def count(c):
                        return (c[0] + base) * SLOTS + c[1]

                    @block.sync
                    def _(e):
                        def load(c):
                            u = c[1]
                            at = LAST if is_last(c) else val(e, number(c) * CH)
                            by_p = "(j p) -> p j" if is_last(c) else "(p j) -> p j"
                            start = pick(e, number(c))
                            again(e, sum_full, val(e, count(c) - SLOTS + 1))
                            e.sem_inc(passed, 1)
                            with nc.allow_non_contiguous_dma(reason="order of the last chunk's edges"):
                                e.dma_start(src_i[u][:, :], src[bass.ds(at, CH)].rearrange(by_p, j=J)).then_inc(loaded[u], 16)
                                e.dma_start(dst_c[u][:, :], dst[bass.ds(at, CH)].rearrange(by_p, j=J)).then_inc(loaded[u], 16)
                            e.dma_start(r_win[u][:, :], r_table[bass.ds(start, W), :]).then_inc(loaded[u], 16)

                        chunks(e, load)

                    @block.gpsimd
                    def _(e):
                        def gather(c):
                            u = c[1]
                            e.wait_ge(loaded[u], val(e, (c[0] + base) * 48 + 48))
                            e.sem_inc(passed, 1)
                            for j in range(SKIP if is_last(c) else 0, J):
                                e.indirect_dma_start(
                                    out=msg[u][:, j, :], out_offset=None, in_=p_table[:, :],
                                    in_offset=bass.IndirectOffsetOnAxis(ap=src_i[u][:, j:j + 1], axis=0)).then_inc(rows_in[u], 16)

                        with e.Fori(0, TURNS - 1) as i:
                            for u in range(SLOTS):
                                gather((i, u))
                        for u in range(SLOTS):
                            gather((TURNS - 1, u))

                    @block.tensor
                    def _(e):
                        def turn_hot(c):
                            u = c[1]
                            n = count(c)
                            n0, n1 = val(e, n), val(e, n + 1)
                            e.wait_ge(hot_done, n1)
                            for h in range(2):
                                again(e, hotT_done[h], n0)
                                for k in range(4):
                                    mm = e.transpose(p_hot[h][0:W, k * P:(k + 1) * P], hot[u][:, 4 * h + k, :], ident[:, :])
                                mm.then_inc(hot_full[h], 1)

                        def edges(c):
                            u = c[1]
                            n = count(c)
                            n0, n1 = val(e, n), val(e, n + 1)
                            for h in range(2):
                                e.wait_ge(hotT_done[h], n1)
                                again(e, both_done[h], n0)
                                for j in range(4 * h, 4 * h + 4):
                                    mm = e.matmul(p_edge[h][:, j % 4, :], hotT[:, j * P:(j + 1) * P], r_win[u][:, :], start=True, stop=True)
                                mm.then_inc(edge_full[h], 1)

                        def sums(c):
                            u = c[1]
                            n = count(c)
                            n0, n1 = val(e, n), val(e, n + 1)
                            e.wait_ge(relu_done, n1)
                            again(e, added, n0)
                            again(e, added2, n1)
                            for j in range(J):
                                e.matmul(p_sum[:, 0, :], msg[u][:, j, :], hot[u][:, j, :], start=(j == 0), stop=(j == J - 1))
                            for j in range(J):
                                mm = e.matmul(p_sum[0:1, 1, :], ones[:, 0:1], hot[u][:, j, :], start=(j == 0), stop=(j == J - 1))
                            mm.then_inc(sum_full, 1)

                        def step(c):
                            if not is_last(c):
                                turn_hot(shift(c, 1))
                            if not is_first(c):
                                sums(shift(c, -1))
                            if not is_last(c):
                                edges(shift(c, 1))

                        turn_hot((0, 0))
                        edges((0, 0))
                        chunks(e, step)
                        sums((TURNS - 1, SLOTS - 1))

                    @block.scalar
                    def _(e):
                        def copy_hot(c):
                            n = count(c)
                            n0, n1 = val(e, n), val(e, n + 1)
                            for h in range(2):
                                again(e, edge_full[h], n0)
                                e.wait_ge(hot_full[h], n1)
                                e.sem_inc(passed, 1)
                                e.activation(hotT[:, h * HALF:(h + 1) * HALF], p_hot[h][0:W, :], ACT.Copy).then_inc(hotT_done[h], 1)

                        def relus(c):
                            u = c[1]
                            e.wait_ge(both_done[1], val(e, count(c) + 1))
                            e.sem_inc(passed, 1)
                            e.activation(msg[u][:, :, :], msg[u][:, :, :], ACT.Relu).then_inc(relu_done, 1)

                        def step(c):
                            if not is_last(c):
                                copy_hot(shift(c, 1))
                            relus(c)

                        copy_hot((0, 0))
                        chunks(e, step)

                    @block.vector
                    def _(e):
                        def hots(c):
                            i, u = c
                            n = count(c)
                            n0, n1 = val(e, n), val(e, n + 1)
                            e.wait_ge(loaded[u], val(e, (i + base) * 48 + 48))
                            again(e, hot_done, n0)
                            if is_last(c):
                                e.memset(dst_c[u][:, 0:DUP // P], -1).then_inc(cut_done, 1)
                                e.memset(dst_c[u][0:DUP % P, DUP // P:DUP // P + 1], -1).then_inc(cut_done, 1)
                                e.wait_ge(cut_done, val(e, r * 2 + 2))
                            e.tensor_scalar(in_win[:, :], dst_c[u][:, :], start_b[:, bass.ds(number(c), 1)], None, ALU.subtract).then_inc(in_win_done, 1)
                            e.wait_ge(in_win_done, n1)
                            e.tensor_tensor(hot[u][:, :, :], in_win[:, :].unsqueeze(2).broadcast_to([P, J, W]),
                                            iota_row[:, :].unsqueeze(1).broadcast_to([P, J, W]), ALU.is_equal).then_inc(hot_done, 1)

                        def boths(c):
                            i, u = c
                            n1 = val(e, count(c) + 1)
                            e.wait_ge(rows_in[u], val(e, gathered(c, r)))
                            for h in range(2):
                                e.wait_ge(edge_full[h], n1)
                                part = msg[u][:, 4 * h:4 * h + 4, :]
                                e.tensor_tensor(part, part, p_edge[h][:, :, :], ALU.add).then_inc(both_done[h], 1)

                        def add(c):
                            n = count(c)
                            n0, n1 = val(e, n), val(e, n + 1)
                            start = pick(e, number(c))
                            again(e, added, n0)
                            again(e, added2, n1)
                            e.wait_ge(sum_full, n1)
                            here = acc[:, 0, bass.ds(start, W)]
                            e.tensor_tensor(here, here, p_sum[:, 0, :], ALU.add).then_inc(added, 1)
                            here = acc[0:1, 1, bass.ds(start, W)]
                            e.tensor_tensor(here, here, p_sum[0:1, 1, :], ALU.add).then_inc(added2, 1)

                        def step(c):
                            if not is_last(c):
                                hots(shift(c, 1))
                            boths(c)
                            if not is_first(c):
                                add(shift(c, -1))

                        hots((0, 0))
                        if at_first:
                            e.memset(acc[0:1, 1, :], 0.0).then_inc(added2, 1)
                            e.scalar_tensor_tensor(out=x1_rows[:, :, :], in0=x1_rows[:, :, :], scalar=2.0,
                                                   in1=bn2_b[:, :].unsqueeze(1).broadcast_to([P, BLOCKS, D]), op0=ALU.mult, op1=ALU.add)
                        chunks(e, step)
                        add((TURNS - 1, SLOTS - 1))

            layer1_round(0)
            spread_out = nc.values_load(span_i[0:1, 0:1], min_val=0, max_val=N)
            with nc.If(spread_out >= W):
                with nc.Fori(1, ROUNDS) as w:
                    move_windows()
                    layer1_round(w)

        with ExitStack() as ctx:
            hid = [sb(f"hid{k}", [P, G], ctx=ctx) for k in range(2)]
            y = [sb(f"y1_{k}", [P, GB, D], ctx=ctx) for k in range(2)]
            stats = sb("stats1", [P, GB, 6], ctx=ctx)
            mv = sb("mv_last", [P, GB, 2], ctx=ctx)
            std = sb("std_last", [P, GB], ctx=ctx)
            rstd = sb("rstd1", [P, GB], ctx=ctx)
            shift_n = sb("shift_n1", [P, GB], ctx=ctx)
            o_rows = [sb(f"o_rows{k}", [P, GB, D], ctx=ctx) for k in range(2)]
            ps = [ctx.enter_context(nc.psum_tensor(f"psE{k}", [P, 512], F32)) for k in range(4)]
            p_hid, p_mesh = ps[0:2], ps[2:4]

            names = "hid_full hid_done mesh_full y_done stats_done mv_done root_done rstd_done shift_done o_done".split()
            s = {n: sem(n + "1") for n in names}
            o_out = [sem(f"o_out{k}") for k in range(2)]
            block = ctx.enter_context(nc.Block())

            @block.sync
            def _(e):
                def store(g, k):
                    at = val(e, g * G)
                    e.wait_ge(s["o_done"], val(e, g + 1))
                    e.sem_inc(passed, 1)
                    if isinstance(g, int) and g == NG - 1:
                        e.dma_start(out[FULL * P:N, :], o_rows[k][0:REST, 0, :]).then_inc(o_out[k], 16)
                    else:
                        e.dma_start(out[bass.ds(at, G), :].rearrange("(b p) d -> p b d", p=P), o_rows[k][:, :, :]).then_inc(o_out[k], 16)

                pipelined(e, (2, store))
                e.wait_ge(o_out[0], 16 * (NG - NG // 2))
                e.wait_ge(o_out[1], 16 * (NG // 2))

            @block.tensor
            def _(e):
                def hidden(g, k):
                    at = place(e, g, G)
                    again(e, s["hid_done"], val(e, g - 1))
                    e.matmul(p_hid[k][:, :], wn1[:, 0, :], x1T[:, bass.ds(at, G)], start=True, stop=False)
                    e.matmul(p_hid[k][:, :], we2n[:, :], acc[:, 0, bass.ds(at, G)], start=False, stop=False)
                    e.matmul(p_hid[k][:, :], be2n[:, :], acc[0:1, 1, bass.ds(at, G)], start=False, stop=True).then_inc(s["hid_full"], 1)

                def mesh(g, k):
                    e.wait_ge(s["hid_done"], val(e, g + 1))
                    again(e, s["y_done"], val(e, g - 1))
                    for b in range(GB):
                        mm = e.matmul(p_mesh[k][:, b * D:(b + 1) * D], hid[k][:, b * P:(b + 1) * P], wn2[:, :], start=True, stop=True)
                    mm.then_inc(s["mesh_full"], 1)

                pipelined(e, (0, hidden), (1, mesh))

            @block.scalar
            def _(e):
                def relus(g, k):
                    again(e, s["mesh_full"], val(e, g - 1))
                    e.wait_ge(s["hid_full"], val(e, g + 1))
                    e.sem_inc(passed, 1)
                    e.activation(hid[k][:, :], p_hid[k][:, :], ACT.Relu, bias=bn1_c[:, 0:1]).then_inc(s["hid_done"], 1)

                def roots(g, k):
                    e.wait_ge(s["mv_done"], val(e, g + 1))
                    again(e, s["rstd_done"], val(e, g))
                    e.sem_inc(passed, 1)
                    e.activation(std[:, :], mv[:, :, 1:2].rearrange("p b o -> p (b o)"), ACT.Sqrt, bias=eps_c[:, 0:1]).then_inc(s["root_done"], 1)

                def normal(g, k):
                    e.wait_ge(s["shift_done"], val(e, g + 1))
                    again(e, o_out[k], val(e, (g - k) * 8))
                    e.sem_inc(passed, 1)
                    for b in range(GB):
                        op = e.activation(o_rows[k][:, b, :], y[k][:, b, :], ACT.Identity, bias=shift_n[:, b:b + 1], scale=rstd[:, b:b + 1])
                    op.then_inc(s["o_done"], 1)

                pipelined(e, (2, normal), (0, relus), (1, roots))

            @block.vector
            def _(e):
                def moments(g, k):
                    blk = place(e, g, GB)
                    n0, n1 = val(e, g), val(e, g + 1)
                    e.wait_ge(s["mesh_full"], n1)
                    again(e, s["o_done"], val(e, g - 1))
                    e.tensor_tensor(y[k][:, :, :], x1_rows[:, bass.ds(blk, GB), :], p_mesh[k][:, :].rearrange("p (b d) -> p b d", d=D), ALU.add).then_inc(s["y_done"], 1)
                    e.wait_ge(s["y_done"], n1)
                    again(e, s["mv_done"], n0)
                    for b in range(GB):
                        op = e.bn_stats(stats[:, b, :], y[k][:, b, :])
                    op.then_inc(s["stats_done"], 1)
                    again(e, s["shift_done"], n0)
                    e.wait_ge(s["stats_done"], n1)
                    e.sem_inc(passed, 1)
                    for b in range(GB):
                        op = e.bn_aggr(mv[:, b, :], stats[:, b, :])
                    op.then_inc(s["mv_done"], 1)

                def scales(g, k):
                    n0, n1 = val(e, g), val(e, g + 1)
                    e.wait_ge(s["root_done"], n1)
                    again(e, s["o_done"], n0)
                    e.reciprocal(rstd[:, :], std[:, :]).then_inc(s["rstd_done"], 1)
                    e.wait_ge(s["rstd_done"], n1)
                    e.scalar_tensor_tensor(out=shift_n[:, :], in0=mv[:, :, 0:1].rearrange("p b o -> p (b o)"), scalar=-1.0,
                                           in1=rstd[:, :], op0=ALU.mult, op1=ALU.mult).then_inc(s["shift_done"], 1)

                pipelined(e, (2, scales), (1, moments))


_INS = ["x", "src", "dst", "edge_attr_32", "edge_weight", "node_vec", "L0_gnn_time_w", "L0_gnn_time_b", "L0_gnn_Wx",
        "L0_gnn_bx", "L0_gnn_Wq", "L0_gnn_bq", "L0_gnn_Wk", "L0_gnn_bk", "L0_gnn_Wv", "L0_gnn_bv", "L0_gnn_We",
        "L0_gnn_W_ac", "L0_gnn_b_ac", "L1_gnn_We1", "L1_gnn_be1", "L1_gnn_We2", "L1_gnn_be2", "L1_gnn_Wn1",
        "L1_gnn_bn1", "L1_gnn_Wn2", "L1_gnn_bn2"]
_OUTS = [((6250, 128), "float32")]


def kernel(**inputs):
    import numpy as _np
    import concourse.bacc as _bacc
    from concourse import mybir as _mybir
    from concourse.bass_utils import run_bass_kernel_spmd as _run

    nc = _bacc.Bacc("TRN2", target_bir_lowering=False, num_devices=1)
    arrays, args = {}, []
    for name in _INS:
        a = _np.ascontiguousarray(inputs[name])
        arrays[f"in_{name}_dram"] = a
        args.append(nc.dram_tensor(f"in_{name}_dram", a.shape, _mybir.dt.from_np(a.dtype), kind="ExternalInput").ap())
    for i, (shape, dtype) in enumerate(_OUTS):
        dt = _mybir.dt.from_np(_np.dtype(dtype))
        args.append(nc.dram_tensor(f"out_{i}_dram", shape, dt, kind="ExternalOutput").ap())
    gnn_kernel(nc, *args)
    r = _run(nc, [arrays], core_ids=[0])
    return r.results[0]["out_0_dram"]
```
